# Optimizing a Trainium2 kernel written in Bass

```python
import numpy as np
import jax
import jax.numpy as jnp

def _softmax(x, axis=-1):
    return jax.nn.softmax(x, axis=axis)

def _gelu(x):
    return jax.nn.gelu(x, approximate=True)

def _silu(x):
    return jax.nn.silu(x)

def _sigmoid(x):
    return jax.nn.sigmoid(x)

def _layernorm(x, axis=-1, eps=1e-05):
    m = jnp.mean(x, axis=axis, keepdims=True)
    v = jnp.var(x, axis=axis, keepdims=True)
    return (x - m) / jnp.sqrt(v + eps)

def _scatter_add(tgt, idx, src, axis=0):
    return tgt.at[idx].add(src)

def _segment_sum(src, seg, n):
    return jax.ops.segment_sum(src, seg, n)
kernel_name = 'mk_vit_tower_d1_tok_img512_r4_b901d8'

def setup_inputs(seed: int=0):
    np.random.seed(seed)
    _w = jnp.asarray

    def _rec_inputs():
        import jax
        import jax.numpy as jnp
        _rk = jax.random.key(seed)
        x = -0.00040386 + 0.999972 * jax.random.normal(jax.random.fold_in(_rk, 1), (4, 3, 224, 224), jnp.float32)
        return x
    x = _rec_inputs()

    def _L0_tok_setup():
        import jax, jax.numpy as jnp
        import numpy as np
        PATCH = 4
        EMBED = 128

        def _extract_patches(x):
            B, C, H, Wd = x.shape
            p = PATCH
            x = x.reshape(B, C, H // p, p, Wd // p, p)
            x = x.transpose(0, 2, 4, 1, 3, 5)
            return x.reshape(B, H // p * (Wd // p), C * p * p)
        key = jax.random.key(seed)
        k1, k2, k3, k4 = jax.random.split(key, 4)
        x = jax.random.normal(k1, (64, 3, 64, 64), dtype=jnp.float32)
        W = jax.random.normal(k2, (EMBED, PATCH * PATCH * 3), dtype=jnp.float32) * 0.1
        b = jax.random.normal(k3, (EMBED,), dtype=jnp.float32) * 0.1
        cls = jax.random.normal(k4, (1, 1, EMBED), dtype=jnp.float32)
        return {'x': x, 'W': W, 'b': b, 'cls': cls}
    _L0_tok_all = _L0_tok_setup()
    _L0_tok_in = {k: v for k, v in _L0_tok_all.items() if k in ('W', 'b', 'cls')}
    del _L0_tok_all

    def _L0_attn_setup():
        import jax, jax.numpy as jnp
        import numpy as np
        EPS_L2 = 1e-12
        EPS_NORM = 1e-05

        def _linear(x, W, b):
            return x @ W.T + b

        def _silu(x):
            return x * jax.nn.sigmoid(x)

        def _l2norm(x):
            n = jnp.sqrt(jnp.sum(x * x, axis=-1, keepdims=True))
            return x / jnp.maximum(n, EPS_L2)

        def _dwconv_causal(x, w, b):
            y = jax.lax.conv_general_dilated(x.transpose(0, 2, 1), w, window_strides=(1,), padding=[(3, 0)], dimension_numbers=('NCH', 'OIH', 'NCH'), feature_group_count=w.shape[0])
            return y.transpose(0, 2, 1) + b

        def _zc_rmsnorm(x, weight):
            xm = x - jnp.mean(x, axis=-1, keepdims=True)
            var = jnp.mean(xm * xm, axis=-1, keepdims=True)
            return xm * jax.lax.rsqrt(var + EPS_NORM) * weight

        def _gated_delta_core(q, k, v, alpha, beta):
            B, S, d = q.shape
            S0 = jnp.zeros((B, d, d), dtype=q.dtype)

            def step(St, inp):
                qt, kt, vt, at, bt = inp
                Sk = jnp.einsum('bij,bj->bi', St, kt)
                a = at[:, None, None]
                b = bt[:, None, None]
                Sn = a * (St - b * Sk[:, :, None] * kt[:, None, :]) + b * vt[:, :, None] * kt[:, None, :]
                ot = jnp.einsum('bij,bj->bi', Sn, qt)
                return (Sn, ot)
            xs = (q.transpose(1, 0, 2), k.transpose(1, 0, 2), v.transpose(1, 0, 2), alpha.T, beta.T)
            _, outs = jax.lax.scan(step, S0, xs)
            return outs.transpose(1, 0, 2)
        key = jax.random.key(seed)
        ks = jax.random.split(key, 16)
        B, S, d = (8, 512, 128)
        w = lambda k, shape: jax.random.normal(k, shape, jnp.float32) * 0.02
        return {'x': jax.random.normal(ks[0], (B, S, d), jnp.float32), 'Wq': w(ks[1], (d, d)), 'bq': jnp.zeros((d,), jnp.float32), 'Wk': w(ks[2], (d, d)), 'bk': jnp.zeros((d,), jnp.float32), 'Wv': w(ks[3], (d, d)), 'bv': jnp.zeros((d,), jnp.float32), 'Wa': w(ks[4], (1, d)), 'ba': jnp.zeros((1,), jnp.float32), 'Wb': w(ks[5], (1, d)), 'bb': jnp.zeros((1,), jnp.float32), 'cwq': w(ks[6], (d, 1, 4)), 'cbq': jnp.zeros((d,), jnp.float32), 'cwk': w(ks[7], (d, 1, 4)), 'cbk': jnp.zeros((d,), jnp.float32), 'cwv': w(ks[8], (d, 1, 4)), 'cbv': jnp.zeros((d,), jnp.float32), 'norm_w': jnp.ones((d,), jnp.float32), 'Wg': w(ks[9], (d, d)), 'bg': jnp.zeros((d,), jnp.float32), 'Wo': w(ks[10], (d, d)), 'bo': jnp.zeros((d,), jnp.float32)}
    _L0_attn_all = _L0_attn_setup()
    _L0_attn_in = {k: v for k, v in _L0_attn_all.items() if k in ('Wq', 'bq', 'Wk', 'bk', 'Wv', 'bv', 'Wa', 'ba', 'Wb', 'bb', 'cwq', 'cbq', 'cwk', 'cbk', 'cwv', 'cbv', 'norm_w', 'Wg', 'bg', 'Wo', 'bo')}
    del _L0_attn_all

    def _L0_ffn_setup():
        import jax, jax.numpy as jnp
        import numpy as np
        B, S, D, F, E = (8, 1024, 128, 512, 8)
        INIT_LAMBDA = 0.2
        LN_EPS = 1e-05
        LN_MERGE = 0.03
        key = jax.random.key(seed)
        ks = jax.random.split(key, 12)
        n = lambda k, shp, s=1.0: jax.random.normal(k, shp, dtype=jnp.float32) * s
        return {'hidden_states': n(ks[0], (B, S, D)), 'gfc1_w': n(ks[1], (D, D), 0.01), 'gfc1_b': jnp.zeros((D,), jnp.float32), 'gfc2_w': n(ks[2], (E, D), 0.01), 'gfc2_b': jnp.full((E,), INIT_LAMBDA, dtype=jnp.float32), 'W1': n(ks[3], (F, D), 0.02), 'b1': jnp.zeros((F,), jnp.float32), 'W2': n(ks[4], (D, F), 0.02), 'b2': jnp.zeros((D,), jnp.float32), 'ln_g': jnp.ones((D,), jnp.float32), 'ln_b': jnp.zeros((D,), jnp.float32), 'tv_W1': n(ks[5], (E, F, D), 0.02), 'tv_b1': n(ks[6], (E, F), 0.02), 'tv_W2': n(ks[7], (E, D, F), 0.02), 'tv_b2': n(ks[8], (E, D), 0.02), 'tv_ln_g': n(ks[9], (E, D), 0.02), 'tv_ln_b': n(ks[10], (E, D), 0.02)}
    _L0_ffn_all = _L0_ffn_setup()
    _L0_ffn_in = {k: v for k, v in _L0_ffn_all.items() if k in ('gfc1_w', 'gfc1_b', 'gfc2_w', 'gfc2_b', 'W1', 'b1', 'W2', 'b2', 'ln_g', 'ln_b', 'tv_W1', 'tv_b1', 'tv_W2', 'tv_b2', 'tv_ln_g', 'tv_ln_b')}
    del _L0_ffn_all
    return {'x': x, 'L0_tok_W': _L0_tok_in['W'], 'L0_tok_b': _L0_tok_in['b'], 'L0_tok_cls': _L0_tok_in['cls'], 'L0_attn_Wq': _L0_attn_in['Wq'], 'L0_attn_bq': _L0_attn_in['bq'], 'L0_attn_Wk': _L0_attn_in['Wk'], 'L0_attn_bk': _L0_attn_in['bk'], 'L0_attn_Wv': _L0_attn_in['Wv'], 'L0_attn_bv': _L0_attn_in['bv'], 'L0_attn_Wa': _L0_attn_in['Wa'], 'L0_attn_ba': _L0_attn_in['ba'], 'L0_attn_Wb': _L0_attn_in['Wb'], 'L0_attn_bb': _L0_attn_in['bb'], 'L0_attn_cwq': _L0_attn_in['cwq'], 'L0_attn_cbq': _L0_attn_in['cbq'], 'L0_attn_cwk': _L0_attn_in['cwk'], 'L0_attn_cbk': _L0_attn_in['cbk'], 'L0_attn_cwv': _L0_attn_in['cwv'], 'L0_attn_cbv': _L0_attn_in['cbv'], 'L0_attn_norm_w': _L0_attn_in['norm_w'], 'L0_attn_Wg': _L0_attn_in['Wg'], 'L0_attn_bg': _L0_attn_in['bg'], 'L0_attn_Wo': _L0_attn_in['Wo'], 'L0_attn_bo': _L0_attn_in['bo'], 'L0_ffn_gfc1_w': _L0_ffn_in['gfc1_w'], 'L0_ffn_gfc1_b': _L0_ffn_in['gfc1_b'], 'L0_ffn_gfc2_w': _L0_ffn_in['gfc2_w'], 'L0_ffn_gfc2_b': _L0_ffn_in['gfc2_b'], 'L0_ffn_W1': _L0_ffn_in['W1'], 'L0_ffn_b1': _L0_ffn_in['b1'], 'L0_ffn_W2': _L0_ffn_in['W2'], 'L0_ffn_b2': _L0_ffn_in['b2'], 'L0_ffn_ln_g': _L0_ffn_in['ln_g'], 'L0_ffn_ln_b': _L0_ffn_in['ln_b'], 'L0_ffn_tv_W1': _L0_ffn_in['tv_W1'], 'L0_ffn_tv_b1': _L0_ffn_in['tv_b1'], 'L0_ffn_tv_W2': _L0_ffn_in['tv_W2'], 'L0_ffn_tv_b2': _L0_ffn_in['tv_b2'], 'L0_ffn_tv_ln_g': _L0_ffn_in['tv_ln_g'], 'L0_ffn_tv_ln_b': _L0_ffn_in['tv_ln_b']}

def reference(x, L0_tok_W, L0_tok_b, L0_tok_cls, L0_attn_Wq, L0_attn_bq, L0_attn_Wk, L0_attn_bk, L0_attn_Wv, L0_attn_bv, L0_attn_Wa, L0_attn_ba, L0_attn_Wb, L0_attn_bb, L0_attn_cwq, L0_attn_cbq, L0_attn_cwk, L0_attn_cbk, L0_attn_cwv, L0_attn_cbv, L0_attn_norm_w, L0_attn_Wg, L0_attn_bg, L0_attn_Wo, L0_attn_bo, L0_ffn_gfc1_w, L0_ffn_gfc1_b, L0_ffn_gfc2_w, L0_ffn_gfc2_b, L0_ffn_W1, L0_ffn_b1, L0_ffn_W2, L0_ffn_b2, L0_ffn_ln_g, L0_ffn_ln_b, L0_ffn_tv_W1, L0_ffn_tv_b1, L0_ffn_tv_W2, L0_ffn_tv_b2, L0_ffn_tv_ln_g, L0_ffn_tv_ln_b):
    import jax
    import jax.numpy as jnp

    def _L0_tok_ref(x, W, b, cls):
        import jax, jax.numpy as jnp
        import numpy as np
        PATCH = 4
        EMBED = 128

        def _extract_patches(x):
            B, C, H, Wd = x.shape
            p = PATCH
            x = x.reshape(B, C, H // p, p, Wd // p, p)
            x = x.transpose(0, 2, 4, 1, 3, 5)
            return x.reshape(B, H // p * (Wd // p), C * p * p)
        patches = _extract_patches(x)
        emb = jnp.einsum('blk,ek->ble', patches, W) + b
        B = x.shape[0]
        cls_tok = jnp.broadcast_to(cls, (B, 1, EMBED))
        return jnp.concatenate([cls_tok, emb], axis=1)

    def _L0_attn_ref(x, Wq, bq, Wk, bk, Wv, bv, Wa, ba, Wb, bb, cwq, cbq, cwk, cbk, cwv, cbv, norm_w, Wg, bg, Wo, bo):
        import jax, jax.numpy as jnp
        import numpy as np
        EPS_L2 = 1e-12
        EPS_NORM = 1e-05

        def _linear(x, W, b):
            return x @ W.T + b

        def _silu(x):
            return x * jax.nn.sigmoid(x)

        def _l2norm(x):
            n = jnp.sqrt(jnp.sum(x * x, axis=-1, keepdims=True))
            return x / jnp.maximum(n, EPS_L2)

        def _dwconv_causal(x, w, b):
            y = jax.lax.conv_general_dilated(x.transpose(0, 2, 1), w, window_strides=(1,), padding=[(3, 0)], dimension_numbers=('NCH', 'OIH', 'NCH'), feature_group_count=w.shape[0])
            return y.transpose(0, 2, 1) + b

        def _zc_rmsnorm(x, weight):
            xm = x - jnp.mean(x, axis=-1, keepdims=True)
            var = jnp.mean(xm * xm, axis=-1, keepdims=True)
            return xm * jax.lax.rsqrt(var + EPS_NORM) * weight

        def _gated_delta_core(q, k, v, alpha, beta):
            B, S, d = q.shape
            S0 = jnp.zeros((B, d, d), dtype=q.dtype)

            def step(St, inp):
                qt, kt, vt, at, bt = inp
                Sk = jnp.einsum('bij,bj->bi', St, kt)
                a = at[:, None, None]
                b = bt[:, None, None]
                Sn = a * (St - b * Sk[:, :, None] * kt[:, None, :]) + b * vt[:, :, None] * kt[:, None, :]
                ot = jnp.einsum('bij,bj->bi', Sn, qt)
                return (Sn, ot)
            xs = (q.transpose(1, 0, 2), k.transpose(1, 0, 2), v.transpose(1, 0, 2), alpha.T, beta.T)
            _, outs = jax.lax.scan(step, S0, xs)
            return outs.transpose(1, 0, 2)
        q_c = _dwconv_causal(_linear(x, Wq, bq), cwq, cbq)
        k_c = _dwconv_causal(_linear(x, Wk, bk), cwk, cbk)
        v_c = _dwconv_causal(_linear(x, Wv, bv), cwv, cbv)
        q = _l2norm(_silu(q_c))
        k = _l2norm(_silu(k_c))
        v = _silu(v_c)
        alpha = jax.nn.sigmoid(_linear(x, Wa, ba))[..., 0]
        beta = jax.nn.sigmoid(_linear(x, Wb, bb))[..., 0]
        gdn = _gated_delta_core(q, k, v, alpha, beta)
        gdn = _zc_rmsnorm(gdn, norm_w)
        gate = _silu(_linear(x, Wg, bg))
        return _linear(gdn * gate, Wo, bo)

    def _L0_ffn_ref(hidden_states, gfc1_w, gfc1_b, gfc2_w, gfc2_b, W1, b1, W2, b2, ln_g, ln_b, tv_W1, tv_b1, tv_W2, tv_b2, tv_ln_g, tv_ln_b):
        import jax, jax.numpy as jnp
        import numpy as np
        B, S, D, F, E = (8, 1024, 128, 512, 8)
        INIT_LAMBDA = 0.2
        LN_EPS = 1e-05
        LN_MERGE = 0.03
        x = hidden_states
        gh = jax.nn.relu(jnp.einsum('bsd,hd->bsh', x, gfc1_w) + gfc1_b)
        g = (jnp.einsum('bsh,eh->bse', gh, gfc2_w) + gfc2_b).mean(axis=1)
        W1m = W1 + jnp.einsum('be,efd->bfd', g, tv_W1)
        b1m = b1 + g @ tv_b1
        W2m = W2 + jnp.einsum('be,edf->bdf', g, tv_W2)
        b2m = b2 + g @ tv_b2
        lng = ln_g + LN_MERGE * (tv_ln_g - ln_g).sum(axis=0)
        lnb = ln_b + LN_MERGE * (tv_ln_b - ln_b).sum(axis=0)
        h = jax.nn.relu(jnp.einsum('bsd,bfd->bsf', x, W1m) + b1m[:, None, :])
        out = jnp.einsum('bsf,bdf->bsd', h, W2m) + b2m[:, None, :]
        res = x + out
        mu = res.mean(axis=-1, keepdims=True)
        var = res.var(axis=-1, keepdims=True)
        return (res - mu) * jax.lax.rsqrt(var + LN_EPS) * lng + lnb
    h = _L0_tok_ref(x, L0_tok_W, L0_tok_b, L0_tok_cls)
    h = h + _L0_attn_ref(_layernorm(h, axis=-1), L0_attn_Wq, L0_attn_bq, L0_attn_Wk, L0_attn_bk, L0_attn_Wv, L0_attn_bv, L0_attn_Wa, L0_attn_ba, L0_attn_Wb, L0_attn_bb, L0_attn_cwq, L0_attn_cbq, L0_attn_cwk, L0_attn_cbk, L0_attn_cwv, L0_attn_cbv, L0_attn_norm_w, L0_attn_Wg, L0_attn_bg, L0_attn_Wo, L0_attn_bo)
    h = h + _L0_ffn_ref(_layernorm(h, axis=-1), L0_ffn_gfc1_w, L0_ffn_gfc1_b, L0_ffn_gfc2_w, L0_ffn_gfc2_b, L0_ffn_W1, L0_ffn_b1, L0_ffn_W2, L0_ffn_b2, L0_ffn_ln_g, L0_ffn_ln_b, L0_ffn_tv_W1, L0_ffn_tv_b1, L0_ffn_tv_W2, L0_ffn_tv_b2, L0_ffn_tv_ln_g, L0_ffn_tv_ln_b)
    return h

_drawn_inputs = setup_inputs


def setup_inputs(seed=0):
    import zlib

    import numpy as np

    out = dict(_drawn_inputs(seed))
    spreads = {'L0_attn_bq': (0.0, 0.8),
     'L0_attn_bk': (0.0, 0.8),
     'L0_attn_bv': (0.0, 2.0),
     'L0_attn_cbq': (0.0, 0.418),
     'L0_attn_cbk': (0.0, 0.356),
     'L0_attn_cbv': (0.0, 0.421),
     'L0_attn_norm_w': (1.0, 0.6),
     'L0_attn_bg': (0.0, 0.534),
     'L0_attn_bo': (0.0, 0.1),
     'L0_ffn_gfc1_b': (0.0, 0.8),
     'L0_ffn_gfc2_b': (0.20000000298023224, 0.6),
     'L0_ffn_b1': (0.0, 0.421),
     'L0_ffn_b2': (0.0, 0.1),
     'L0_ffn_ln_g': (1.0, 0.2),
     'L0_ffn_ln_b': (0.0, 0.1)}
    factors = {'L0_attn_Wq': 8.0,
     'L0_attn_Wk': 8.0,
     'L0_attn_Wv': 8.0,
     'L0_attn_Wa': 8.0,
     'L0_attn_Wb': 8.0,
     'L0_attn_cwq': 8.0,
     'L0_attn_cwk': 8.0,
     'L0_attn_cwv': 8.0,
     'L0_ffn_gfc1_w': 8.0,
     'L0_ffn_gfc2_w': 8.0,
     'L0_ffn_tv_b1': 8.0,
     'L0_ffn_tv_b2': 8.0,
     'L0_ffn_tv_ln_g': 49.293,
     'L0_ffn_tv_ln_b': 51.982}
    for name, (base, spread) in spreads.items():
        noise = np.random.default_rng([zlib.crc32(name.encode()), seed]).standard_normal(out[name].shape)
        drawn = base * np.exp(spread * noise) if base else spread * noise
        out[name] = jnp.asarray(drawn.astype(out[name].dtype))
    for name, factor in factors.items():
        out[name] = (out[name] * factor).astype(out[name].dtype)
    return out
```

```python
import concourse.bass as bass
from concourse import mybir
from contextlib import ExitStack

F32 = mybir.dt.float32
BF16 = mybir.dt.bfloat16
ALU = mybir.AluOpType
ACT = mybir.ActivationFunctionType
AX = mybir.AxisListType

NB = 4
IMG, PATCH = 224, 4
GRID = IMG // PATCH
TOK = GRID * GRID + 1
D = 128
C = 128
STEPS = -(-TOK // C)
LAST = TOK - C * (STEPS - 1)
PIX = 3 * PATCH * PATCH
KX = PIX + 3
TAPS = 4
HIST = TAPS - 1
LEVELS = 7
EPS = 1e-5
F = 512
FB = F // D
NE = 8
LN_MERGE = 0.03
GROUP = 4
GROUPS = STEPS // GROUP
UNITS = GROUPS + 1


def need(engine, semaphore, value):
    if not isinstance(value, int) or value > 0:
        engine.wait_ge(semaphore, value)


def apart(engine):
    engine.nop(nofuse=True)


def vit_tower(nc, x, tok_WT, tok_b, tok_cls, WqT, bq, WkT, bk, WvT, bv, WaT, ba, WbT, bb, cwqT, cbq, cwkT, cbk,
              cwvT, cbv, norm_w, WgT, bg, WoT, bo, gfc1_wT, gfc1_b, gfc2_wT, gfc2_b, W1, b1, W2, b2, ln_g, ln_b,
              tv_W1, tv_b1, tv_W2, tv_b2, tv_ln_g, tv_ln_b, out):
    ctx = ExitStack()
    with ctx:
        def sb(name, shape, dt=F32):
            return ctx.enter_context(nc.sbuf_tensor(name, shape, dt))

        def sem(name):
            return ctx.enter_context(nc.semaphore(name))

        ident = sb("ident", [D, D])
        ident4 = sb("ident4", [D, NB, D])
        ident_bf = sb("ident_bf", [D, NB, D], BF16)
        ident0 = sb("ident0", [D, D])
        masks = sb("masks", [D, LEVELS, D // 2])
        mask_x = sb("mask_x", [D, KX])
        mask_1 = sb("mask_1", [D, KX])
        ones = sb("ones", [D, D])
        half_neg = sb("half_neg", [D, 4])
        half_pos = sb("half_pos", [D, 4])
        euler = sb("euler", [D, 8])

        We = sb("We", [D, D])
        SA = sb("SA", [D, 516])
        SB = sb("SB", [D, 512])
        Wo_T = sb("Wo_T", [D, D])
        gfc1_T = sb("gfc1_T", [D, D])
        gfc1_bc = sb("gfc1_bc", [D, 1])
        bo_rows = sb("bo_rows", [D, D])

        h1buf = sb("h1buf", [D, NB, STEPS, C])
        xc = h1buf[0:KX, :, :, :].rearrange("p b s c -> p b (s c)")
        ln2 = sb("ln2", [D, STEPS, NB, 2])

        work = sb("work", [D, 25420])
        offset = [0]

        def tile(n, *shape):
            at = offset[0]
            offset[0] += n
            t = work[:, at:at + n]
            if len(shape) == 2:
                return t.rearrange("p (a c) -> p a c", a=shape[0])
            if len(shape) == 3:
                return t.rearrange("p (a b c) -> p a b c", a=shape[0], b=shape[1])
            return t

        xt = [tile(NB * C, NB, C) for _ in range(2)]
        XW = HIST + C
        xs = [tile(NB * XW, NB, XW) for _ in range(2)]
        rmat = tile(NB * KX, NB, KX)
        kvg = [tile(NB * 3 * D, NB, 3 * D) for _ in range(2)]
        gate_kept = tile(NB * D, NB, D)
        kT = [tile(NB * D, NB, D) for _ in range(2)]
        qT = [tile(NB * D, NB, D) for _ in range(2)]
        decay = tile(NB * C, NB, C)
        cdecay = tile(NB * C, NB, C)
        Bm = [tile(NB * C, NB, C) for _ in range(2)]
        Pm = [tile(NB * C, NB, C) for _ in range(2)]
        kd = [tile(NB * D, NB, D) for _ in range(2)]
        vt = [tile(NB * D, NB, D) for _ in range(2)]
        newblk = [tile(NB * C, NB, C) for _ in range(LEVELS)]
        Y = tile(NB * C, NB, C)
        X = [tile(NB * C, NB, C) for _ in range(2)]
        state = tile(NB * D, NB, D)
        Rn = tile(NB * D, NB, D)
        Zn = tile(NB * D, NB, D)
        QMs = tile(NB * D, NB, D)
        o = tile(NB * D, NB, D)
        sq = tile(NB * D, NB, D)
        sq_q = tile(NB * D, NB, D)
        sq_o = tile(NB * D, NB, D)
        og = tile(NB * D, NB, D)
        ogT = tile(NB * D, NB, D)
        hn = tile(NB * D, NB, D)
        hnT = tile(NB * D, NB, D)
        relu_h = tile(NB * D, NB, D)
        gate_sum = tile(NB * D, NB, D)
        attention_end = offset[0]

        stats1 = sb("stats1", [D, NB, 6])
        mv1 = sb("mv1", [D, NB, 2])
        var1e = sb("var1e", [D, NB])
        rstd1 = sb("rstd1", [D, NB])
        logit = sb("logit", [D, 8])
        expo = sb("expo", [D, 8])
        expo1 = sb("expo1", [D, 8])
        ab = sb("ab", [D, 8])
        ssk = sb("ssk", [D, NB])
        kn2 = sb("kn2", [D, NB])
        rk2 = sb("rk2", [D, NB])
        cneg = sb("cneg", [D, NB])
        knorm = sb("knorm", [D, NB])
        vsum = sb("vsum", [D, NB])
        vmean = sb("vmean", [D, NB])
        qn2e = [sb(f"qn2e{i}", [D, NB]) for i in range(2)]
        glast = sb("glast", [1, NB])
        gs = [sb(f"gs{i}", [D, 8]) for i in range(2)]
        so2 = sb("so2", [D, NB])
        ovar = sb("ovar", [D, NB])
        oscale = sb("oscale", [D, NB])
        stats2 = sb("stats2", [D, NB, 6])
        mv2 = sb("mv2", [D, NB, 2])
        var2e = sb("var2e", [D, NB])
        rstd2 = sb("rstd2", [D, NB])

        bank = [ctx.enter_context(nc.psum_tensor(f"bank{i}", [D, 512], F32)) for i in range(8)]
        blk_ps, Y_ps, X_ps, small_ps = bank[0], bank[1], bank[2], bank[7]

        def by4(t):
            return t[:, :].rearrange("p (b c) -> p b c", b=NB)

        offset[0] = 0
        pro = tile(12288)
        nat = pro[:, 128:128 + 2 * D].rearrange("p (a c) -> p a c", a=2)
        Wc = pro[:, 1664:1664 + D]
        wmean = pro[:, 1792:1793]
        wsum = pro[:, 1794:1795]
        WcT = pro[:, 1920:1920 + D]
        rhs_all = pro[:, 2048:2048 + 516]
        fold = pro[:, 2580:2580 + 516]
        bias_row = pro[0:1, 3100:3100 + 516]
        cb_row = pro[0:1, 3620:3620 + 512]
        onehot2 = pro[0:1, 4140:4140 + D]
        onehot1 = pro[0:1, 4268:4268 + D]
        cwT = pro[0:TAPS, 4410:4410 + 384]
        selA = pro[0:TAPS, 4800:4800 + D]
        selB = pro[0:TAPS, 4930:4930 + D]
        nw_col = pro[:, 5060:5061]
        cwA = pro[:, 5100:5100 + 384]
        cwB = pro[:, 5500:5500 + 384]
        tmpf = pro[:, 5900:5900 + 516]
        cbs = pro[:, 6420:6420 + 384]

        x_in = sem("x_in")
        x_const = sem("x_const")
        w_in = sem("w_in")
        con = sem("con")
        pro_pe = sem("pro_pe")
        pro_dve = sem("pro_dve")
        We_zero = sem("We_zero")
        ones_set = sem("ones_set")

        xt_ready = sem("xt_ready")
        h0_ps = sem("h0_ps")
        h0_kept = sem("h0_kept")
        h0_biased = sem("h0_biased")
        stats1_done = sem("stats1_done")
        mv1_ready = sem("mv1_ready")
        var1e_ready = sem("var1e_ready")
        rstd1_ready = sem("rstd1_ready")
        rmask_done = sem("rmask_done")
        rmat_ready = sem("rmat_ready")
        rb_ps = sem("rb_ps")
        hist_ready = sem("hist_ready")
        xs_ready = sem("xs_ready")
        xs_shifted = sem("xs_shifted")
        kvg_ps = sem("kvg_ps")
        kvg_ready = sem("kvg_ready")
        logit_ps = sem("logit_ps")
        logit_ready = sem("logit_ready")
        expo_ready = sem("expo_ready")
        expo1_ready = sem("expo1_ready")
        ab_ready = sem("ab_ready")
        q_ps = sem("q_ps")
        qT_ready = sem("qT_ready")
        kT_ps = sem("kT_ps")
        kT_ready = sem("kT_ready")
        alpha_ps = sem("alpha_ps")
        decay_ready = sem("decay_ready")
        glast_ready = sem("glast_ready")
        sqk_ready = sem("sqk_ready")
        ssk_ready = sem("ssk_ready")
        kn2_ready = sem("kn2_ready")
        rk2_ready = sem("rk2_ready")
        cneg_ready = sem("cneg_ready")
        knorm_ready = sem("knorm_ready")
        vsum_ready = sem("vsum_ready")
        vmean_ready = sem("vmean_ready")
        vt_ready = sem("vt_ready")
        cdecay_ready = sem("cdecay_ready")
        kd_ready = sem("kd_ready")
        kk_ps = sem("kk_ps")
        kq_ps = sem("kq_ps")
        B_ready = sem("B_ready")
        P_ready = sem("P_ready")
        sqq_ready = sem("sqq_ready")
        qq_ps = sem("qq_ps")
        qn2_ready = sem("qn2_ready")
        g_ps = sem("g_ps")
        gs_ready = sem("gs_ready")
        gate_ready = sem("gate_ready")
        blk_ps_done = sem("blk_ps_done")
        blk_ready = sem("blk_ready")
        Yps_done = sem("Yps_done")
        Xps_done = sem("Xps_done")
        Y_ready = sem("Y_ready")
        X_ready = sem("X_ready")
        km_ps = sem("km_ps")
        Rn_ready = sem("Rn_ready")
        z_ps = sem("z_ps")
        Zn_ready = sem("Zn_ready")
        qm_ps = sem("qm_ps")
        QMs_ready = sem("QMs_ready")
        pz_ps = sem("pz_ps")
        o_ready = sem("o_ready")
        dm_ps = sem("dm_ps")
        state_ready = sem("state_ready")
        sqo_ready = sem("sqo_ready")
        so2_ready = sem("so2_ready")
        ovar_ready = sem("ovar_ready")
        oscale_ready = sem("oscale_ready")
        og_ready = sem("og_ready")
        ogT_ps = sem("ogT_ps")
        ogT_ready = sem("ogT_ready")
        wo_ps = sem("wo_ps")
        h1_ready = sem("h1_ready")
        stats2_done = sem("stats2_done")
        mv2_ready = sem("mv2_ready")
        var2e_ready = sem("var2e_ready")
        rstd2_ready = sem("rstd2_ready")
        hn_ready = sem("hn_ready")
        hnT_ps = sem("hnT_ps")
        hnT_ready = sem("hnT_ready")
        gf_ps = sem("gf_ps")
        relu_ready = sem("relu_ready")
        gate_summed = sem("gate_summed")
        ln2_kept = sem("ln2_kept")

        def half(t, b, k, second):
            m = 1 << k
            if b is None:
                return t.rearrange("p b (n h m) -> p b n h m", h=2, m=m)[:, :, :, second, :]
            return t[:, b, :].rearrange("p (n h m) -> p n h m", h=2, m=m)[:, :, second, :]

        def on(j, lag):
            return not isinstance(j, int) or 0 <= j + lag < STEPS

        first, last = -2, STEPS + 1
        LOOP = (4, STEPS - 3)
        assert (LOOP[1] - LOOP[0]) % 2 == 0

        def iterations(engine, body):
            for j in range(first, LOOP[0]):
                body(j, j % 2)
            with engine.Fori(LOOP[0], LOOP[1] - 1, 2) as j:
                body(j, 0)
                body(j + 1, 1)
            for j in range(LOOP[1], last + 1):
                body(j, j % 2)

        DVE_PRO = 18
        LE, LF, LI, LC, LH = 2, 1, 0, -1, -2
        block = ctx.enter_context(nc.Block())

        def row1(v):
            return v.rearrange("(a n) -> a n", a=1)

        def col1(v):
            return v.rearrange("(p a) -> p a", a=1)

        weights_early = [
            (We[0:PIX, :], tok_WT[:, :]), (We[PIX:PIX + 1, :], row1(tok_b)),
            (We[PIX + 2:PIX + 3, :], tok_cls.rearrange("a b p -> (a b) p")),
            (rhs_all[:, 0:128], WkT[:, :]), (rhs_all[:, 128:256], WvT[:, :]), (rhs_all[:, 256:384], WgT[:, :]),
            (rhs_all[:, 384:512], WqT[:, :]), (rhs_all[:, 512:513], WaT[:, :]), (rhs_all[:, 513:514], WbT[:, :]),
            (nat[:, 0, :], WoT[:, :]), (nat[:, 1, :], gfc1_wT[:, :]),
            (bias_row[:, 0:128], row1(bk)), (bias_row[:, 128:256], row1(bv)), (bias_row[:, 256:384], row1(bg)),
            (bias_row[:, 384:512], row1(bq)), (bias_row[:, 512:513], row1(ba)), (bias_row[:, 513:514], row1(bb)),
            (cb_row[:, 0:128], row1(cbk)), (cb_row[:, 128:256], row1(cbv)), (cb_row[:, 256:384], row1(cbq)),
            (cwT[:, 0:128], cwkT[:, :]), (cwT[:, 128:256], cwvT[:, :]), (cwT[:, 256:384], cwqT[:, :]),
            (nw_col, col1(norm_w)), (gfc1_bc[:, :], col1(gfc1_b)), (bo_rows[:, :], bo.partition_broadcast(D)),
        ]
        W_IN = 16 * len(weights_early)

        ffn = make_ffn(nc, ctx, sb, sem, work, locals())

        @block.sync
        def _(sp):
            sp.wait_ge(We_zero, 1)
            for dst, src in weights_early:
                sp.dma_start(dst, src).then_inc(w_in, 16)
            ffn["load"](sp)
            ffn["sync"](sp)

        @block.scalar
        def _(act):
            act.wait_ge(x_const, 2)
            for b in range(NB):
                act.dma_start(xc[0:PIX, b, 1:TOK], x[:, b, :]).then_inc(x_in, 16)

            def body(j, par):
                p = 1 - par
                if on(j, LF):
                    s = j + LF
                    act.wait_ge(hist_ready, s + 1)
                    act.wait_ge(xs_ready, s + 1)
                    need(act, q_ps, s - 1)
                    nc.scalar.copy(xs[p][64:64 + KX, :, 1:XW], xs[p][0:KX, :, 0:XW - 1]).then_inc(xs_shifted, 1)

                def inverse_out(k):
                    if not on(j, LI):
                        return
                    s = j + LI
                    if k < LEVELS - 1:
                        act.wait_ge(Yps_done, 6 * s + k + 1)
                        need(act, blk_ps_done, LEVELS * s + k)
                        if k == 0:
                            nc.scalar.copy(Y, by4(Y_ps)).then_inc(Y_ready, 1)
                        else:
                            nc.scalar.copy(half(Y, None, k, 0), half(by4(Y_ps), None, k, 0)).then_inc(Y_ready, 1)
                    act.wait_ge(Xps_done, LEVELS * s + k + 1)
                    if k == 0:
                        need(act, z_ps, s - 1)
                        nc.scalar.copy(X[par], by4(X_ps)).then_inc(X_ready, 1)
                    else:
                        nc.scalar.copy(half(X[par], None, k, 1), half(by4(X_ps), None, k, 1)).then_inc(X_ready, 1)

                def kvg_out(b):
                    if on(j, LF):
                        s = j + LF
                        act.wait_ge(kvg_ps, NB * s + b + 1)
                        if b == 0:
                            need(act, gate_ready, s - 1)
                            need(act, kd_ready, s - 1)
                            need(act, vt_ready, s - 1)
                        nc.scalar.activation(kvg[p][:, b, :], bank[4 - b % 2][:, 0:384], ACT.Silu).then_inc(kvg_ready, 1)

                inverse_out(0)
                if on(j, LH):
                    s = j + LH
                    act.wait_ge(hnT_ps, s + 1)
                    need(act, gf_ps, s)
                    nc.scalar.copy(hnT, by4(bank[6])).then_inc(hnT_ready, 1)
                kvg_out(0)
                kvg_out(1)
                inverse_out(1)
                if on(j, LC):
                    s = j + LC
                    act.wait_ge(z_ps, s + 1)
                    need(act, dm_ps, s)
                    nc.scalar.copy(Zn, by4(bank[5])).then_inc(Zn_ready, 1)
                kvg_out(2)
                kvg_out(3)
                if on(j, LF):
                    s = j + LF
                    act.wait_ge(logit_ps, s + 1)
                    need(act, expo_ready, s)
                    nc.scalar.mul(logit[:, :], small_ps[:, 0:8], -1.0).then_inc(logit_ready, 1)
                inverse_out(2)
                if on(j, LC):
                    s = j + LC
                    act.wait_ge(qm_ps, s + 1)
                    act.wait_ge(gs_ready, s + 1)
                    need(act, o_ready, s)
                    for b in range(NB):
                        ins = nc.scalar.activation(QMs[:, b, :], by4(bank[6])[:, b, :], ACT.Copy, scale=gs[p][:, b:b + 1])
                    ins.then_inc(QMs_ready, 1)
                if on(j, LH):
                    s = j + LH
                    act.wait_ge(gf_ps, s + 1)
                    need(act, gate_summed, s)
                    nc.scalar.activation(relu_h, by4(bank[5]), ACT.Relu, bias=gfc1_bc[:, 0:1]).then_inc(relu_ready, 1)
                inverse_out(3)
                if on(j, LF):
                    s = j + LF
                    act.wait_ge(q_ps, s + 1)
                    need(act, qm_ps, s - 1)
                    nc.scalar.activation(qT[p], by4(bank[4]), ACT.Silu).then_inc(qT_ready, 1)
                    act.wait_ge(kT_ps, s + 1)
                    nc.scalar.copy(kT[p], by4(bank[3])).then_inc(kT_ready, 1)
                inverse_out(4)
                if on(j, LE):
                    s = j + LE
                    act.wait_ge(h0_ps, s + 1)
                    act.wait_ge(xt_ready, s + 1)
                    nc.scalar.copy(h1buf[:, :, bass.ds(s, 1), :].rearrange("p b s c -> p b (s c)"), by4(bank[3])).then_inc(h0_kept, 1)
                inverse_out(5)
                if on(j, LC):
                    s = j + LC
                    act.wait_ge(ogT_ps, s + 1)
                    need(act, wo_ps, s)
                    nc.scalar.copy(ogT, by4(bank[6])).then_inc(ogT_ready, 1)
                inverse_out(6)

            iterations(act, body)
            ffn["scalar"](act)

        @block.gpsimd
        def _(pool):
            nc.gpsimd.memset(ones[:, :], 1.0).then_inc(ones_set, 1)
            nc.gpsimd.memset(masks[:, :, :], 1.0).then_inc(ones_set, 1)
            nc.gpsimd.memset(half_neg[:, :], -0.5)
            nc.gpsimd.memset(half_pos[:, :], 0.5)
            nc.gpsimd.memset(euler[:, :], 2.718281828459045).then_inc(ones_set, 1)
            pool.wait_ge(ones_set, 3)
            nc.gpsimd.affine_select(out=ident[:, :], in_=ones[:, :], pattern=[[-1, D]], compare_op=ALU.is_equal,
                                    fill=0.0, base=0, channel_multiplier=1).then_inc(con, 1)
            pool.wait_ge(con, 1)
            nc.gpsimd.affine_select(out=ident0[:, :], in_=ident[:, :], pattern=[[1, D]], compare_op=ALU.is_gt,
                                    fill=0.0, base=0, channel_multiplier=0)
            for b in range(NB):
                nc.gpsimd.tensor_copy(ident4[:, b, :], ident[:, :])
                nc.gpsimd.tensor_copy(ident_bf[:, b, :], ident[:, :])
            nc.gpsimd.affine_select(out=mask_1[:, :], in_=ones[:, 0:KX], pattern=[[1, KX]], compare_op=ALU.is_equal,
                                    fill=0.0, base=-(PIX + 1), channel_multiplier=0)
            nc.gpsimd.affine_select(out=mask_x[:, :], in_=ones[:, 0:KX], pattern=[[1, KX]], compare_op=ALU.not_equal,
                                    fill=0.0, base=-(PIX + 1), channel_multiplier=0)
            sel = ((selA, 3, 2), (selB, 1, 0))
            for t, low, high in sel:
                nc.gpsimd.affine_select(out=t[:, 0:64], in_=ones[0:TAPS, 0:64], pattern=[[0, 64]],
                                        compare_op=ALU.is_equal, fill=0.0, base=-low, channel_multiplier=1)
                nc.gpsimd.affine_select(out=t[:, 64:128], in_=ones[0:TAPS, 0:64], pattern=[[0, 64]],
                                        compare_op=ALU.is_equal, fill=0.0, base=-high, channel_multiplier=1)
            nc.gpsimd.affine_select(out=onehot2.rearrange("p (h c) -> p h c", h=2), in_=ones[0:1, :].rearrange("p (h c) -> p h c", h=2),
                                    pattern=[[0, 2], [1, 64]], compare_op=ALU.is_equal, fill=0.0, base=-(PIX + 1), channel_multiplier=0)
            nc.gpsimd.affine_select(out=onehot1, in_=ones[0:1, :], pattern=[[1, D]],
                                    compare_op=ALU.is_equal, fill=0.0, base=-(PIX + 1), channel_multiplier=0).then_inc(con, 1)
            for k in range(LEVELS):
                m = 1 << k
                n = D // (2 * m)
                v = masks[:, k, :].rearrange("p (n m) -> p n m", m=m)
                nc.gpsimd.affine_select(out=v, in_=v, pattern=[[-2 * m, n], [0, m]], compare_op=ALU.is_ge,
                                        fill=0.0, base=-m, channel_multiplier=1).then_inc(con, 1)
            pool.wait_ge(con, 2 + LEVELS)
            for k in range(LEVELS):
                m = 1 << k
                n = D // (2 * m)
                v = masks[:, k, :].rearrange("p (n m) -> p n m", m=m)
                nc.gpsimd.affine_select(out=v, in_=v, pattern=[[2 * m, n], [0, m]], compare_op=ALU.is_ge,
                                        fill=0.0, base=2 * m - 1, channel_multiplier=-1).then_inc(con, 1)
            pool.wait_ge(con, 2 + 2 * LEVELS)
            pool.wait_ge(x_const, 1)
            nc.gpsimd.affine_select(out=xc[32:KX, :, 0:1], in_=xc[32:KX, :, 0:1], pattern=[[0, NB], [0, 1]], compare_op=ALU.is_ge,
                                    fill=0.0, base=-(PIX + 1 - 32), channel_multiplier=1)
            nc.gpsimd.affine_select(out=xc[32:KX, :, 1:TOK], in_=xc[32:KX, :, 1:TOK], pattern=[[0, NB], [0, TOK - 1]],
                                    compare_op=ALU.is_ge, fill=0.0, base=PIX + 1 - 32, channel_multiplier=-1).then_inc(x_const, 1)

            pool.wait_ge(pro_dve, DVE_PRO)
            pool.wait_ge(x_in, 16 * NB)

            def body(j, par):
                p = 1 - par
                if on(j, LF):
                    s = j + LF
                    if not isinstance(s, int) or s > 0:
                        pool.wait_ge(xs_ready, s)
                        need(pool, q_ps, s - 1)
                        need(pool, xs_shifted, s - 1)
                        apart(pool)
                        nc.gpsimd.tensor_copy(xs[p][0:KX, :, 0:HIST], xs[1 - p][0:KX, :, C:XW]).then_inc(hist_ready, 1)
                    else:
                        nc.gpsimd.memset(xs[p][0:KX, :, 0:HIST], 0.0).then_inc(hist_ready, 1)
                if on(j, LF):
                    s = j + LF
                    pool.wait_ge(logit_ready, s + 1)
                    need(pool, expo1_ready, s)
                    nc.gpsimd.tensor_tensor(expo[:, :], euler[:, :], logit[:, :], ALU.pow).then_inc(expo_ready, 1)
                    pool.wait_ge(kvg_ready, NB * (s + 1))
                    need(pool, ssk_ready, s)
                    nc.gpsimd.tensor_tensor(sq, kvg[p][:, :, 0:D], kvg[p][:, :, 0:D], ALU.mult).then_inc(sqk_ready, 1)
                if on(j, LC):
                    s = j + LC
                    pool.wait_ge(o_ready, s + 1)
                    need(pool, so2_ready, s)
                    nc.gpsimd.tensor_tensor(sq_o, o, o, ALU.mult).then_inc(sqo_ready, 1)
                if on(j, LE):
                    s = j + LE
                    need(pool, xs_ready, s - 1)
                    need(pool, h0_ps, s - 1)
                    apart(pool)
                    nc.gpsimd.tensor_copy(xt[par][0:KX, :, :], xc[:, :, bass.ds(s * C, C)]).then_inc(xt_ready, 1)
                if on(j, LF):
                    s = j + LF
                    pool.wait_ge(kn2_ready, s + 1)
                    need(pool, vt_ready, s)
                    nc.gpsimd.tensor_tensor(knorm[:, :], kn2[:, :], half_pos[:, :], ALU.pow).then_inc(knorm_ready, 1)
                    pool.wait_ge(qT_ready, s + 1)
                    need(pool, qq_ps, s)
                    nc.gpsimd.tensor_tensor(sq_q, qT[p], qT[p], ALU.mult).then_inc(sqq_ready, 1)
                if on(j, LC):
                    s = j + LC
                    pool.wait_ge(ovar_ready, s + 1)
                    need(pool, og_ready, s)
                    nc.gpsimd.tensor_tensor(oscale[:, :], ovar[:, :], half_neg[:, :], ALU.pow).then_inc(oscale_ready, 1)
                if on(j, LF):
                    s = j + LF
                    pool.wait_ge(decay_ready, s + 1)
                    pool.wait_ge(cneg_ready, s + 1)
                    need(pool, P_ready, s)
                    need(pool, kd_ready, s)
                    nc.gpsimd.tensor_tensor(cdecay, decay, cneg[:, :].unsqueeze(2).broadcast_to([D, NB, C]),
                                            ALU.mult).then_inc(cdecay_ready, 1)
                if on(j, LE):
                    s = j + LE
                    pool.wait_ge(mv1_ready, s + 1)
                    need(pool, rstd1_ready, s)
                    apart(pool)
                    nc.gpsimd.tensor_scalar(var1e[:, :], mv1[:, :, 1], EPS, None, ALU.add).then_inc(var1e_ready, 1)
                    pool.wait_ge(var1e_ready, s + 1)
                    need(pool, rmask_done, s)
                    nc.gpsimd.tensor_tensor(rstd1[:, :], var1e[:, :], half_neg[:, :], ALU.pow).then_inc(rstd1_ready, 1)
                    pool.wait_ge(rstd1_ready, s + 1)
                    need(pool, rb_ps, s)
                    nc.gpsimd.tensor_tensor(rmat, mask_x[:, :].unsqueeze(1).broadcast_to([D, NB, KX]),
                                            rstd1[:, :].unsqueeze(2).broadcast_to([D, NB, KX]), ALU.mult).then_inc(rmask_done, 1)
                    pool.wait_ge(rmask_done, s + 1)
                    nc.gpsimd.tensor_tensor(rmat, rmat, mask_1[:, :].unsqueeze(1).broadcast_to([D, NB, KX]),
                                            ALU.add).then_inc(rmat_ready, 1)
                    pool.wait_ge(h0_kept, s + 1)
                    h = h1buf[:, :, bass.ds(s, 1), :].rearrange("p b s c -> p b (s c)")
                    apart(pool)
                    nc.gpsimd.tensor_tensor(h, h, bo_rows[:, :].unsqueeze(1).broadcast_to([D, NB, D]),
                                            ALU.add).then_inc(h0_biased, 1)
                if on(j, LI):
                    s = j + LI
                    pool.wait_ge(kvg_ready, NB * (s + 1))
                    need(pool, og_ready, s)
                    apart(pool)
                    nc.gpsimd.tensor_copy(gate_kept, kvg[par][:, :, 2 * D:3 * D]).then_inc(gate_ready, 1)
                if on(j, LH):
                    s = j + LH
                    pool.wait_ge(relu_ready, s + 1)
                    need(pool, gate_summed, s)
                    n = LAST if isinstance(s, int) and s == STEPS - 1 else C
                    nc.gpsimd.tensor_tensor(gate_sum[:, :, 0:n], gate_sum[:, :, 0:n], relu_h[:, :, 0:n],
                                            ALU.add).then_inc(gate_summed, 1)
                if on(j, LC):
                    s = j + LC
                    pool.wait_ge(mv2_ready, s + 1)
                    need(pool, rstd2_ready, s)
                    apart(pool)
                    nc.gpsimd.tensor_scalar(var2e[:, :], mv2[:, :, 1], EPS, None, ALU.add).then_inc(var2e_ready, 1)
                    pool.wait_ge(var2e_ready, s + 1)
                    need(pool, ln2_kept, s)
                    nc.gpsimd.tensor_tensor(rstd2[:, :], var2e[:, :], half_neg[:, :], ALU.pow).then_inc(rstd2_ready, 1)

            iterations(pool, body)
            ffn["gpsimd"](pool)

        @block.vector
        def _(dve):
            done = [0]

            def step_done(ins):
                done[0] += 1
                ins.then_inc(pro_dve, 1)
                dve.wait_ge(pro_dve, done[0])

            nc.vector.memset(We[:, :], 0.0).then_inc(We_zero, 1)
            ffn["vector_early"](dve)
            nc.vector.memset(xc[32:KX, :, 0:TOK], 1.0)
            nc.vector.memset(xc[0:32, :, 0:1], 0.0)
            nc.vector.memset(xc[0:KX, :, TOK:STEPS * C], 0.0).then_inc(x_const, 1)
            dve.wait_ge(w_in, W_IN)
            step_done(nc.vector.tensor_reduce(wsum[0:KX, :], We[0:KX, :], AX.X, ALU.add))
            step_done(nc.vector.tensor_scalar(wmean[0:KX, :], wsum[0:KX, :], 1.0 / D, None, ALU.mult))
            step_done(nc.vector.memset(Wc, 0.0))
            step_done(nc.vector.tensor_scalar(Wc[0:KX, :], We[0:KX, :], wmean[0:KX, :], None, ALU.subtract))
            step_done(nc.vector.tensor_scalar(Wo_T[:, :], nat[:, 0, :], nw_col, None, ALU.mult))
            step_done(nc.vector.tensor_copy(gfc1_T[:, :], nat[:, 1, :]))
            step_done(nc.vector.memset(WcT, 0.0))
            dve.wait_ge(pro_pe, 1)
            step_done(nc.vector.tensor_copy(WcT.rearrange("p (h c) -> p h c", h=2)[:, :, 0:KX],
                                            bank[3][:, 0:KX].unsqueeze(1).broadcast_to([D, 2, KX])))
            dve.wait_ge(pro_pe, 2)
            step_done(nc.vector.tensor_copy(fold[:, 0:512], bank[5][:, :]))
            step_done(nc.vector.tensor_copy(fold[:, 512:514], bank[6][:, 0:2]))
            dve.wait_ge(pro_pe, 3)
            for dst, taps in ((SA, bank[0]), (SB, bank[1])):
                step_done(nc.vector.tensor_tensor(dst[:, 0:256], taps[:, 0:256], fold[:, 0:256], ALU.mult))
                step_done(nc.vector.tensor_tensor(dst[:, 384:512], taps[:, 256:384], fold[:, 384:512], ALU.mult))
            step_done(nc.vector.tensor_tensor(SA[:, 0:256], bank[2][:, 0:256], SA[:, 0:256], ALU.add))
            step_done(nc.vector.tensor_tensor(SA[:, 384:512], bank[2][:, 256:384], SA[:, 384:512], ALU.add))
            nc.vector.memset(SA[64:128, 256:384], 0.0)
            nc.vector.memset(SA[64:128, 512:514], 0.0)
            nc.vector.tensor_copy(SA[0:64, 256:384], fold[0:64, 256:384])
            step_done(nc.vector.tensor_copy(SA[0:64, 512:514], fold[0:64, 512:514]))
            for t in newblk:
                nc.vector.memset(t, 0.0)
            nc.vector.memset(gate_sum, 0.0)
            nc.vector.memset(state, 0.0)
            nc.vector.memset(xs[0], 0.0)
            step_done(nc.vector.memset(xs[1], 0.0))
            assert done[0] == DVE_PRO

            def body(j, par):
                p = 1 - par
                if on(j, LF):
                    s = j + LF
                    dve.wait_ge(rb_ps, s + 1)
                    dve.wait_ge(xt_ready, s + 1)
                    need(dve, q_ps, s - 1)
                    need(dve, hist_ready, s)
                    nc.vector.tensor_tensor(xs[p][0:KX, :, HIST:XW], by4(bank[3])[0:KX], xt[p][0:KX, :, :],
                                            ALU.mult).then_inc(xs_ready, 1)

                def new_blocks(k):
                    if not on(j, LI):
                        return
                    s = j + LI
                    dve.wait_ge(blk_ps_done, LEVELS * s + k + 1)
                    need(dve, Xps_done, LEVELS * (s - 1) + k + 1)
                    src = blk_ps[:, 0:NB * 64].rearrange("p (b c) -> p b c", b=NB)
                    m = 1 << k
                    nc.vector.tensor_tensor(half(newblk[k], None, k, 0), src.rearrange("p b (n m) -> p b n m", m=m),
                                            masks[:, k, :].unsqueeze(1).broadcast_to([D, NB, 64]).rearrange("p b (n m) -> p b n m", m=m),
                                            ALU.mult).then_inc(blk_ready, 1)

                new_blocks(0)
                if on(j, LC):
                    s = j + LC
                    dve.wait_ge(km_ps, s + 1)
                    dve.wait_ge(gs_ready, s + 1)
                    dve.wait_ge(vt_ready, s + 1)
                    need(dve, z_ps, s)
                    for b in range(NB):
                        ins = nc.vector.scalar_tensor_tensor(Rn[:, b, :], by4(bank[5])[:, b, :], gs[p][:, b:b + 1], vt[p][:, b, :],
                                                             ALU.mult, ALU.subtract)
                    ins.then_inc(Rn_ready, 1)
                new_blocks(1)
                new_blocks(2)
                if on(j, LF):
                    s = j + LF
                    dve.wait_ge(expo_ready, s + 1)
                    need(dve, ab_ready, s)
                    nc.vector.tensor_scalar(expo1[:, :], expo[:, :], 1.0, None, ALU.add).then_inc(expo1_ready, 1)
                    dve.wait_ge(expo1_ready, s + 1)
                    need(dve, g_ps, s)
                    nc.vector.reciprocal(ab[:, :], expo1[:, :]).then_inc(ab_ready, 1)
                new_blocks(3)
                if on(j, LC):
                    s = j + LC
                    dve.wait_ge(pz_ps, s + 1)
                    dve.wait_ge(QMs_ready, s + 1)
                    need(dve, og_ready, s)
                    need(dve, sqo_ready, s)
                    nc.vector.tensor_tensor(o, by4(bank[6]), QMs, ALU.add).then_inc(o_ready, 1)
                    dve.wait_ge(dm_ps, s + 1)
                    for b in range(NB):
                        ins = nc.vector.scalar_tensor_tensor(state[:, b, :], state[:, b, :], gs[p][:, 4 + b:5 + b], by4(bank[5])[:, b, :],
                                                             ALU.mult, ALU.add)
                    ins.then_inc(state_ready, 1)
                if on(j, LF):
                    s = j + LF
                    dve.wait_ge(sqk_ready, s + 1)
                    need(dve, kn2_ready, s)
                    nc.vector.tensor_reduce(ssk[:, :], sq, AX.X, ALU.add).then_inc(ssk_ready, 1)
                    need(dve, vmean_ready, s)
                    nc.vector.tensor_reduce(vsum[:, :], kvg[p][:, :, D:2 * D], AX.X, ALU.add).then_inc(vsum_ready, 1)
                    dve.wait_ge(ssk_ready, s + 1)
                    need(dve, rk2_ready, s)
                    need(dve, knorm_ready, s)
                    nc.vector.tensor_scalar(kn2[:, :], ssk[:, :], 1e-24, None, ALU.max).then_inc(kn2_ready, 1)
                    dve.wait_ge(vsum_ready, s + 1)
                    need(dve, vt_ready, s)
                    nc.vector.tensor_scalar(vmean[:, :], vsum[:, :], 1.0 / D, None, ALU.mult).then_inc(vmean_ready, 1)
                    dve.wait_ge(kn2_ready, s + 1)
                    nc.vector.reciprocal(rk2[:, :], kn2[:, :]).then_inc(rk2_ready, 1)
                    dve.wait_ge(rk2_ready, s + 1)
                    need(dve, cdecay_ready, s)
                    nc.vector.scalar_tensor_tensor(cneg[:, :], rk2[:, :], -1.0, ab[:, 4:8], ALU.mult, ALU.mult).then_inc(cneg_ready, 1)
                new_blocks(4)
                if on(j, LF):
                    s = j + LF
                    dve.wait_ge(alpha_ps, s + 1)
                    need(dve, g_ps, s)
                    need(dve, cdecay_ready, s)
                    need(dve, glast_ready, s)
                    nc.vector.tensor_tensor_scan(decay.rearrange("p b c -> p (b c)"), bank[4][:, :],
                                                 ident4[:, :, :].rearrange("p b c -> p (b c)"), 0.0, ALU.mult, ALU.add).then_inc(decay_ready, 1)
                    dve.wait_ge(decay_ready, s + 1)
                    nc.vector.tensor_tensor(glast[:, :], decay[0:1, :, C - 1], ab[0:1, 0:4], ALU.mult).then_inc(glast_ready, 1)
                if on(j, LC):
                    s = j + LC
                    dve.wait_ge(sqo_ready, s + 1)
                    need(dve, ovar_ready, s)
                    nc.vector.tensor_reduce(so2[:, :], sq_o, AX.X, ALU.add).then_inc(so2_ready, 1)
                    dve.wait_ge(so2_ready, s + 1)
                    need(dve, oscale_ready, s)
                    nc.vector.scalar_tensor_tensor(ovar[:, :], so2[:, :], 1.0 / D, qn2e[p][:, :], ALU.mult, ALU.add).then_inc(ovar_ready, 1)
                if on(j, LE):
                    s = j + LE
                    dve.wait_ge(h0_kept, s + 1)
                    need(dve, mv1_ready, s)
                    apart(dve)
                    for b in range(NB):
                        ins = nc.vector.bn_stats(stats1[:, b, :], by4(bank[3])[:, b, :])
                    ins.then_inc(stats1_done, 1)
                    dve.wait_ge(stats1_done, s + 1)
                    need(dve, var1e_ready, s)
                    apart(dve)
                    for b in range(NB):
                        ins = nc.vector.bn_aggr(mv1[:, b, :], stats1[:, b, :])
                    ins.then_inc(mv1_ready, 1)
                new_blocks(5)
                if on(j, LC):
                    s = j + LC
                    dve.wait_ge(oscale_ready, s + 1)
                    dve.wait_ge(gate_ready, s + 1)
                    need(dve, ogT_ps, s)
                    for b in range(NB):
                        ins = nc.vector.scalar_tensor_tensor(og[:, b, :], o[:, b, :], oscale[:, b:b + 1], gate_kept[:, b, :],
                                                             ALU.mult, ALU.mult)
                    ins.then_inc(og_ready, 1)
                if on(j, LF):
                    s = j + LF
                    dve.wait_ge(kk_ps, s + 1)
                    dve.wait_ge(cdecay_ready, s + 1)
                    need(dve, blk_ps_done, LEVELS * (s - 1))
                    nc.vector.tensor_tensor(Bm[p], by4(bank[4]), cdecay, ALU.mult).then_inc(B_ready, 1)
                new_blocks(6)
                if on(j, LF):
                    s = j + LF
                    dve.wait_ge(kq_ps, s + 1)
                    need(dve, pz_ps, s - 1)
                    nc.vector.tensor_tensor(Pm[p], by4(bank[3]), cdecay, ALU.mult).then_inc(P_ready, 1)
                    dve.wait_ge(qq_ps, s + 1)
                    need(dve, ovar_ready, s - 1)
                    nc.vector.tensor_scalar(qn2e[p][:, :], small_ps[:, 8:12], 1e-24, EPS, ALU.max, ALU.mult).then_inc(qn2_ready, 1)
                    need(dve, dm_ps, s - 1)
                    for b in range(NB):
                        ins = nc.vector.tensor_scalar(kd[p][:, b, :], kvg[p][:, b, 0:D], cdecay[:, b, C - 1:C], None, ALU.mult)
                    ins.then_inc(kd_ready, 1)
                    dve.wait_ge(knorm_ready, s + 1)
                    dve.wait_ge(vmean_ready, s + 1)
                    need(dve, Rn_ready, s - 1)
                    for b in range(NB):
                        ins = nc.vector.tensor_scalar(vt[p][:, b, :], kvg[p][:, b, D:2 * D], vmean[:, b:b + 1], knorm[:, b:b + 1],
                                                      ALU.subtract, ALU.mult)
                    ins.then_inc(vt_ready, 1)
                    dve.wait_ge(g_ps, s + 1)
                    need(dve, state_ready, s - 1)
                    need(dve, QMs_ready, s - 1)
                    nc.vector.tensor_copy(gs[p][:, :], small_ps[:, 16:24]).then_inc(gs_ready, 1)
                if on(j, LC):
                    s = j + LC
                    h = h1buf[:, :, bass.ds(s, 1), :].rearrange("p b s c -> p b (s c)")
                    dve.wait_ge(wo_ps, s + 1)
                    dve.wait_ge(h0_biased, s + 1)
                    nc.vector.tensor_tensor(h, by4(bank[5]), h, ALU.add).then_inc(h1_ready, 1)
                    dve.wait_ge(h1_ready, s + 1)
                    need(dve, mv2_ready, s)
                    apart(dve)
                    for b in range(NB):
                        ins = nc.vector.bn_stats(stats2[:, b, :], h[:, b, :])
                    ins.then_inc(stats2_done, 1)
                    dve.wait_ge(stats2_done, s + 1)
                    need(dve, hn_ready, s)
                    apart(dve)
                    for b in range(NB):
                        ins = nc.vector.bn_aggr(mv2[:, b, :], stats2[:, b, :])
                    ins.then_inc(mv2_ready, 1)
                    dve.wait_ge(mv2_ready, s + 1)
                    kept = ln2[:, bass.ds(s, 1), :, :].rearrange("p s b m -> p (s b) m")
                    nc.vector.tensor_copy(kept[:, :, 0], mv2[:, :, 0])
                    dve.wait_ge(rstd2_ready, s + 1)
                    nc.vector.tensor_copy(kept[:, :, 1], rstd2[:, :]).then_inc(ln2_kept, 1)
                    need(dve, hnT_ps, s)
                    for b in range(NB):
                        ins = nc.vector.tensor_scalar(hn[:, b, :], h[:, b, :], mv2[:, b, 0:1], rstd2[:, b:b + 1],
                                                      ALU.subtract, ALU.mult)
                    ins.then_inc(hn_ready, 1)

            iterations(dve, body)
            ffn["vector"](dve)

        @block.tensor
        def _(pe):
            mm = nc.tensor.matmul
            tr = nc.tensor.transpose
            pe.wait_ge(con, 2)
            pe.wait_ge(pro_dve, 4)
            tr(bank[3][:, 0:D], Wc, ident[:, :]).then_inc(pro_pe, 1)
            pe.wait_ge(pro_dve, 8)
            mm(bank[5][:, :], WcT, rhs_all[:, 0:512], start=True, stop=False)
            mm(bank[5][:, :], onehot2, bias_row[:, 0:512], start=False, stop=True)
            mm(bank[6][:, 0:2], WcT, rhs_all[:, 512:514], start=True, stop=False)
            mm(bank[6][:, 0:2], onehot2, bias_row[:, 512:514], start=False, stop=True).then_inc(pro_pe, 1)
            mm(bank[0][:, 0:384], selA, cwT, start=True, stop=True)
            mm(bank[1][:, 0:384], selB, cwT, start=True, stop=True)
            mm(bank[2][:, 0:384], onehot1, cb_row[:, 0:384], start=True, stop=True).then_inc(pro_pe, 1)
            pe.wait_ge(pro_dve, DVE_PRO)
            pe.wait_ge(con, 2 + 2 * LEVELS)

            def body(j, par):
                p = 1 - par
                F_, I_, C_, H_, E_ = on(j, LF), on(j, LI), on(j, LC), on(j, LH), on(j, LE)
                s1, s0, c, h, e = j + LF, j + LI, j + LC, j + LH, j + LE

                def level_blocks(k):
                    if not I_:
                        return
                    if k == 0:
                        pe.wait_ge(B_ready, s0 + 1)
                    else:
                        pe.wait_ge(Y_ready, 6 * s0 + k)
                    need(pe, blk_ready, LEVELS * s0 + k)
                    for b in range(NB):
                        rhs = half(ident4, 0, k, 0) if k == 0 else half(Y, b, k, 0)
                        ins = mm(blk_ps[:, b * 64:(b + 1) * 64], Bm[par][:, b, :], rhs, start=True, stop=True)
                    ins.then_inc(blk_ps_done, 1)

                def level_update(k):
                    if not I_:
                        return
                    if k == 0:
                        need(pe, Y_ready, 6 * s0)
                        need(pe, X_ready, LEVELS * s0)
                        mm(Y_ps[:, :], ident_bf[:, 0, :], ident_bf[:, :, :].rearrange("p b c -> p (b c)"), start=True, stop=False, skip_group_check=True)
                        mm(X_ps[:, :], ident_bf[:, 0, :], ident_bf[:, :, :].rearrange("p b c -> p (b c)"), start=True, stop=False, skip_group_check=True)
                    else:
                        pe.wait_ge(X_ready, LEVELS * s0 + k)
                    pe.wait_ge(blk_ready, LEVELS * s0 + k + 1)
                    if k < LEVELS - 1:
                        for b in range(NB):
                            lhsT = ident[:, :] if k == 0 else X[par][:, b, :]
                            ins = mm(half(by4(Y_ps), b, k, 0), lhsT, half(newblk[k], b, k, 0), start=False, stop=False, skip_group_check=True)
                        ins.then_inc(Yps_done, 1)
                    for b in range(NB):
                        rhs = half(ident4, 0, k, 1) if k == 0 else half(X[par], b, k, 1)
                        ins = mm(half(by4(X_ps), b, k, 1), newblk[k][:, b, :], rhs, start=False, stop=False, skip_group_check=True)
                    ins.then_inc(Xps_done, 1)

                def kvg_rows(b):
                    t = bank[4 - b % 2]
                    mm(t[:, 0:384], xs[p][:, b, HIST:XW], SA[:, 0:384], start=True, stop=False)
                    mm(t[:, 0:256], xs[p][:, b, 1:1 + C], SB[:, 0:256], start=False, stop=True).then_inc(kvg_ps, 1)

                if F_:
                    pe.wait_ge(rmat_ready, s1 + 1)
                    need(pe, P_ready, s1)
                    for b in range(NB):
                        ins = mm(by4(bank[3])[0:KX, b, :], rmat[:, b, :], ident[:, :], start=True, stop=True)
                    ins.then_inc(rb_ps, 1)
                level_blocks(0)
                if C_:
                    need(pe, state_ready, c)
                    need(pe, h1_ready, c)
                    for b in range(NB):
                        ins = mm(by4(bank[5])[:, b, :], kT[p][:, b, :], state[:, b, :], start=True, stop=True)
                    ins.then_inc(km_ps, 1)
                level_update(0)
                if H_:
                    pe.wait_ge(hn_ready, h + 1)
                    pe.wait_ge(ogT_ready, h + 1)
                    for b in range(NB):
                        ins = tr(by4(bank[6])[:, b, :], hn[:, b, :], ident[:, :])
                    ins.then_inc(hnT_ps, 1)
                level_blocks(1)
                if F_:
                    pe.wait_ge(xs_ready, s1 + 1)
                    pe.wait_ge(xs_shifted, s1 + 1)
                    need(pe, B_ready, s1)
                    kvg_rows(0)
                    kvg_rows(1)
                level_update(1)
                if C_:
                    pe.wait_ge(Rn_ready, c + 1)
                    pe.wait_ge(X_ready, LEVELS * (c + 1))
                    for b in range(NB):
                        ins = mm(by4(bank[5])[:, b, :], X[p][:, b, :], Rn[:, b, :], start=True, stop=True)
                    ins.then_inc(z_ps, 1)
                level_blocks(2)
                if F_:
                    pe.wait_ge(kvg_ready, NB * s1 + 1)
                    kvg_rows(2)
                    pe.wait_ge(kvg_ready, NB * s1 + 2)
                    kvg_rows(3)
                    need(pe, gs_ready, s1)
                    for b in range(NB):
                        ins = mm(small_ps[:, b:b + 5:4], xs[p][:, b, HIST:XW], SA[:, 512:514], start=True, stop=True)
                    ins.then_inc(logit_ps, 1)
                level_update(2)
                if H_:
                    pe.wait_ge(hnT_ready, h + 1)
                if C_:
                    for b in range(NB):
                        ins = mm(by4(bank[6])[:, b, :], qT[p][:, b, :], state[:, b, :], start=True, stop=True)
                    ins.then_inc(qm_ps, 1)
                if H_:
                    if C_:
                        pe.wait_ge(Zn_ready, c + 1)
                    mm(bank[5][:, :], gfc1_T[:, :], hnT.rearrange("p b c -> p (b c)"), start=True, stop=True).then_inc(gf_ps, 1)
                level_blocks(3)
                if C_:
                    pe.wait_ge(Zn_ready, c + 1)
                    pe.wait_ge(QMs_ready, c + 1)
                    for b in range(NB):
                        ins = mm(by4(bank[6])[:, b, :], Pm[p][:, b, :], Zn[:, b, :], start=True, stop=True)
                    ins.then_inc(pz_ps, 1)
                    need(pe, relu_ready, h + 1)
                    for b in range(NB):
                        ins = mm(by4(bank[5])[:, b, :], kd[p][:, b, :], Zn[:, b, :], start=True, stop=True)
                    ins.then_inc(dm_ps, 1)
                level_update(3)
                if F_:
                    pe.wait_ge(kvg_ready, NB * s1 + 3)
                    mm(bank[4][:, :], SA[:, 384:512], xs[p][:, :, HIST:XW], start=True, stop=False)
                    mm(bank[4][:, :], SB[:, 384:512], xs[p][:, :, 1:1 + C], start=False, stop=True).then_inc(q_ps, 1)
                level_blocks(4)
                if F_:
                    pe.wait_ge(kvg_ready, NB * s1 + 4)
                    for b in range(NB):
                        ins = tr(by4(bank[3])[:, b, :], kvg[p][:, b, 0:D], ident[:, :])
                    ins.then_inc(kT_ps, 1)
                    pe.wait_ge(ab_ready, s1 + 1)
                    pe.wait_ge(qT_ready, s1 + 1)
                    for b in range(NB):
                        ins = mm(by4(bank[4])[:, b, :], ab[:, b:b + 1].broadcast_to([D, D]), ident0[:, :], start=True, stop=True)
                    ins.then_inc(alpha_ps, 1)
                level_update(4)
                if E_:
                    pe.wait_ge(xt_ready, e + 1)
                    if F_:
                        pe.wait_ge(kT_ready, s1 + 1)
                    for b in range(NB):
                        ins = mm(by4(bank[3])[:, b, :], xt[par][0:KX, b, :], We[0:KX, :], start=True, stop=True)
                    ins.then_inc(h0_ps, 1)
                level_blocks(5)
                if F_:
                    pe.wait_ge(kT_ready, s1 + 1)
                    pe.wait_ge(decay_ready, s1 + 1)
                    for b in range(NB):
                        ins = mm(by4(bank[4])[:, b, :], kT[p][:, b, :], kT[p][:, b, :], start=True, stop=True)
                    ins.then_inc(kk_ps, 1)
                level_update(5)
                if F_:
                    if E_:
                        pe.wait_ge(stats1_done, e + 1)
                        pe.wait_ge(h0_kept, e + 1)
                    for b in range(NB):
                        ins = mm(by4(bank[3])[:, b, :], kT[p][:, b, :], qT[p][:, b, :], start=True, stop=True)
                    ins.then_inc(kq_ps, 1)
                    pe.wait_ge(sqq_ready, s1 + 1)
                    pe.wait_ge(logit_ready, s1 + 1)
                    for b in range(NB):
                        ins = mm(small_ps[:, 8 + b:9 + b], sq_q[:, b, :], ones[:, 0:1], start=True, stop=True)
                    ins.then_inc(qq_ps, 1)
                if C_:
                    pe.wait_ge(og_ready, c + 1)
                    for b in range(NB):
                        ins = tr(by4(bank[6])[:, b, :], og[:, b, :], ident[:, :])
                    ins.then_inc(ogT_ps, 1)
                level_blocks(6)
                if F_:
                    pe.wait_ge(glast_ready, s1 + 1)
                    pe.wait_ge(qn2_ready, s1 + 1)
                    for b in range(NB):
                        mm(small_ps[:, 16 + b:17 + b], decay[0:1, b, :], ab[0:1, b:b + 1], start=True, stop=True)
                    mm(small_ps[:, 20:24], ones[0:1, :], glast[:, :], start=True, stop=True).then_inc(g_ps, 1)
                level_update(6)
                if C_:
                    pe.wait_ge(ogT_ready, c + 1)
                    pe.wait_ge(state_ready, c + 1)
                    for b in range(NB):
                        ins = mm(by4(bank[5])[:, b, :], ogT[:, b, :], Wo_T[:, :], start=True, stop=True)
                    ins.then_inc(wo_ps, 1)

            iterations(pe, body)
            ffn["tensor"](pe)


def make_ffn(nc, ctx, sb, sem, work, A):
    bank, h1buf, ln2, ident, ones = A["bank"], A["h1buf"], A["ln2"], A["ident"], A["ones"]
    gate_sum, by4 = A["gate_sum"], A["by4"]
    W1, b1, W2, b2, out = A["W1"], A["b1"], A["W2"], A["b2"], A["out"]
    tv_W1, tv_b1, tv_W2, tv_b2 = A["tv_W1"], A["tv_b1"], A["tv_W2"], A["tv_b2"]

    at = [0]

    def tile(*shape):
        n = 1
        for k in shape:
            n *= k
        t = work[:, at[0]:at[0] + n]
        at[0] += n
        if len(shape) == 2:
            t = t.rearrange("p (a c) -> p a c", a=shape[0])
        if len(shape) == 3:
            t = t.rearrange("p (a b c) -> p a b c", a=shape[0], b=shape[1])
        return t

    w1T = [tile(FB, D) for _ in range(2)]
    w2T = [tile(FB, D) for _ in range(2)]
    b2mix = tile(NB, D)
    ghT = [tile(GROUP, C) for _ in range(2)]
    hid = [tile(GROUP * C) for _ in range(FB)]
    fhn = [tile(GROUP, D) for _ in range(2)]
    fhnb = [tile(GROUP, D) for _ in range(2)]
    res = tile(GROUP, D)
    nrm = tile(GROUP, D)
    y = [tile(GROUP, D) for _ in range(2)]
    assert at[0] <= A["attention_end"] - 2 * NB * D
    tv1 = sb("tv1", [D, NE, FB, D])
    tv2 = sb("tv2", [D, NE, FB, D])
    w1nat = sb("w1nat", [D, FB, D])
    w2nat = sb("w2nat", [D, FB, D])
    tvb1 = sb("tvb1", [NE, F])
    tvb2 = sb("tvb2", [NE, D])
    tvln = sb("tvln", [NE, 2, D])
    ln_rows = sb("ln_rows", [1, 3, D])
    merge_w = sb("merge_w", [NE, 2, D])
    lng_lnb = sb("lng_lnb", [D, 2, D])
    lng, lnb = lng_lnb[:, 0, :], lng_lnb[:, 1, :]
    b1nat = sb("b1nat", [D, FB])
    b1mix = sb("b1mix", [D, NB, FB])
    gh = sb("gh", [D, NB])
    ghm = sb("ghm", [D, NB])
    gfc2T = sb("gfc2T", [D, NE])
    gfc2b = sb("gfc2b", [D, NE])
    gfc2b_col = sb("gfc2b_col", [NE, 1])
    g_all = sb("g_all", [D, NB, NE])
    g_T = sb("g_T", [NE, NB])
    fst = sb("fst", [D, GROUP, 6])
    fmv = sb("fmv", [D, GROUP, 2])
    fve = sb("fve", [D, GROUP])
    frs = sb("frs", [D, GROUP])
    half_neg = A["half_neg"]

    fw_in = sem("fw_in")
    merge_set = sem("merge_set")
    ln_ps = sem("ln_ps")
    ln_ready = sem("ln_ready")
    gh_sum = sem("gh_sum")
    gh_ready = sem("gh_ready")
    g_ps2 = sem("g_ps2")
    g_ready = sem("g_ready")
    bias_ps = sem("bias_ps")
    mix_step = sem("mix_step")
    b1_ready = sem("b1_ready")
    b2_ready = sem("b2_ready")
    fhn_ready = sem("fhn_ready")
    fhnb_ready = sem("fhnb_ready")
    fhT_ps = sem("fhT_ps")
    fhT_ready = sem("fhT_ready")
    hid_ps = sem("hid_ps")
    hid_ready = sem("hid_ready")
    out_ps = sem("out_ps")
    res_ready = sem("res_ready")
    fst_done = sem("fst_done")
    fmv_ready = sem("fmv_ready")
    fve_ready = sem("fve_ready")
    frs_ready = sem("frs_ready")
    nrm_ready = sem("nrm_ready")
    y1 = sem("y1")
    y2 = sem("y2")
    y_ready = sem("y_ready")
    y_out = [sem("y_out0"), sem("y_out1")]

    def row1(v):
        return v.rearrange("(a n) -> a n", a=1)

    def row(v):
        return v.partition_broadcast(D)

    loads = [
        (tvln[:, 0, :], A["tv_ln_g"][:, :]), (tvln[:, 1, :], A["tv_ln_b"][:, :]),
        (ln_rows[:, 0, :], row1(A["ln_g"])), (ln_rows[:, 1, :], row1(A["ln_b"])), (ln_rows[:, 2, :], row1(b2)),
        (gfc2T[:, :], A["gfc2_wT"][:, :]), (gfc2b[:, :], row(A["gfc2_b"])),
        (gfc2b_col[:, :], A["gfc2_b"].rearrange("(p a) -> p a", a=1)),
        (w1nat[:, :, :].rearrange("p a c -> p (a c)"), W1[:, :]), (w2nat[:, :, :], W2.rearrange("(a p) d -> p a d", p=D)),
        (b1nat[:, :], b1[:, :]), (tvb1[:, :], tv_b1[:, :]), (tvb2[:, :], tv_b2[:, :]),
    ]
    loads += [(tv1[:, e].rearrange("p a c -> p (a c)"), tv_W1[e]) for e in range(NE)]
    loads += [(tv2[:, e], tv_W2[e].rearrange("(a p) d -> p a d", p=D)) for e in range(NE)]
    LOADED = 16 * len(loads)

    def units(engine, body, image_start=None):
        for b in range(NB):
            if image_start is not None:
                image_start(b)
            u0, par = b * UNITS, b % 2
            start = 0
            if b == 0:
                body(0, 0, 0, 0, GROUP, (0, 1, GROUP))
                body(0, 1, 1, 1, GROUP, (0, 2, GROUP))
                start = 2
            with engine.Fori(start, GROUPS - 3, 2) as g:
                body(b, g, u0 + g, par, GROUP, (b, g + 1, GROUP))
                body(b, g + 1, u0 + g + 1, 1 - par, GROUP, (b, g + 2, GROUP))
            body(b, GROUPS - 2, u0 + GROUPS - 2, par, GROUP, (b, GROUPS - 1, GROUP))
            body(b, GROUPS - 1, u0 + GROUPS - 1, 1 - par, GROUP, (b, GROUPS, 1))
            body(b, GROUPS, u0 + GROUPS, par, 1, (b + 1, 0, GROUP) if b + 1 < NB else None)

    def load(sp):
        for dst, src in loads:
            sp.dma_start(dst, src).then_inc(fw_in, 16)

    def sync(sp):
        def body(b, g, u, par, n, nxt):
            sp.wait_ge(y_ready, u + 1)
            if n == GROUP:
                dst = out[b, bass.ds(g * (GROUP * C), GROUP * C), :].rearrange("(t p) d -> p t d", p=C)
                sp.dma_start(dst, y[par][:, :, :]).then_inc(y_out[par], 16)
            else:
                sp.dma_start(out[b, (STEPS - 1) * C:TOK, :], y[par][0:LAST, 0, :]).then_inc(y_out[par], 16)
        units(sp, body)
        sp.wait_ge(y_out[0], 16 * (NB * UNITS // 2))
        sp.wait_ge(y_out[1], 16 * (NB * UNITS // 2))

    def vector_early(dve):
        nc.vector.memset(merge_w[:, 0, :], LN_MERGE)
        nc.vector.memset(merge_w[0:1, 1, :], 1.0 - NE * LN_MERGE).then_inc(merge_set, 1)

    def tensor_early(pe):
        pe.wait_ge(merge_set, 1)
        pe.wait_ge(fw_in, LOADED)
        for i in range(2):
            t = bank[4][:, i * D:(i + 1) * D]
            nc.tensor.matmul(t, merge_w[:, 0, :], tvln[:, i, :], start=True, stop=False)
            ins = nc.tensor.matmul(t, merge_w[0:1, 1, :], ln_rows[:, i, :], start=False, stop=True)
        ins.then_inc(ln_ps, 1)

    def mix(dve, b, e, first):
        n = 2 * NE * b + (0 if first else 2 * e + 2)
        if first:
            if b >= 2:
                dve.wait_ge(out_ps, UNITS * (b - 1))
        else:
            dve.wait_ge(mix_step, n)
        ex = bass.ds(e, 1)
        for t, tv, nat in ((w1T[b % 2], tv1, w1nat), (w2T[b % 2], tv2, w2nat)):
            nc.vector.scalar_tensor_tensor(t.rearrange("p a c -> p (a c)"), tv[:, ex, :, :].rearrange("p e a c -> p (e a c)"),
                                           g_all[:, b, ex], (nat[:, :, :] if first else t).rearrange("p a c -> p (a c)"),
                                           ALU.mult, ALU.add).then_inc(mix_step, 1)

    def vector(dve):
        def normed(b, g, u, par, n):
            need(dve, fhT_ps, u - 1)
            need(dve, fhnb_ready, u - 1)
            for t in range(n):
                s = g * GROUP + t
                st = ln2[:, bass.ds(s, 1), b, :].rearrange("p s m -> p (s m)")
                ins = nc.vector.tensor_scalar(fhn[par][:, t, :], h1buf[:, b, bass.ds(s, 1), :].rearrange("p s c -> p (s c)"),
                                              st[:, 0:1], st[:, 1:2], ALU.subtract, ALU.mult)
            ins.then_inc(fhn_ready, 1)

        dve.wait_ge(A["gate_summed"], STEPS)
        nc.vector.tensor_reduce(gh[:, :], gate_sum, AX.X, ALU.add).then_inc(gh_sum, 1)
        dve.wait_ge(gh_sum, 1)
        nc.vector.tensor_scalar(ghm[:, :], gh[:, :], 1.0 / TOK, None, ALU.mult).then_inc(gh_ready, 1)
        dve.wait_ge(A["og_ready"], STEPS)
        dve.wait_ge(A["ln2_kept"], STEPS)
        normed(0, 0, 0, 0, GROUP)
        dve.wait_ge(g_ps2, 1)
        dve.wait_ge(fw_in, LOADED)
        nc.vector.tensor_tensor(g_all[:, :, :], bank[0][:, 0:NB * NE].rearrange("p (b e) -> p b e", b=NB),
                                gfc2b[:, :].unsqueeze(1).broadcast_to([D, NB, NE]), ALU.add)
        nc.vector.tensor_scalar(g_T[:, :], bank[0][0:NE, 64:64 + NB], gfc2b_col[:, :], None, ALU.add).then_inc(g_ready, 1)
        dve.wait_ge(g_ready, 1)
        mix(dve, 0, NE - 1, True)
        for e in range(NE - 1):
            mix(dve, 0, e, False)
        dve.wait_ge(bias_ps, 1)
        nc.vector.tensor_tensor(b1mix[:, :, :], bank[6][:, 0:NB * FB].rearrange("p (f b) -> p b f", b=NB),
                                b1nat[:, :].unsqueeze(1).broadcast_to([D, NB, FB]), ALU.add).then_inc(b1_ready, 1)
        nc.vector.tensor_copy(b2mix, by4(bank[7])).then_inc(b2_ready, 1)

        def image_start(b):
            if b + 1 < NB:
                mix(dve, b + 1, NE - 1, True)

        def body(b, g, u, par, n, nxt):
            if nxt is not None:
                normed(nxt[0], nxt[1], u + 1, 1 - par, nxt[2])
            if b + 1 < NB:
                mix(dve, b + 1, g, False)
            dve.wait_ge(out_ps, u + 1)
            dve.wait_ge(fhnb_ready, u + 1)
            nc.vector.tensor_tensor(res[:, 0:n, :], by4(bank[2])[:, 0:n, :], fhnb[par][:, 0:n, :], ALU.add).then_inc(res_ready, 1)
            dve.wait_ge(res_ready, u + 1)
            for t in range(n):
                ins = nc.vector.bn_stats(fst[:, t, :], res[:, t, :])
            ins.then_inc(fst_done, 1)
            dve.wait_ge(fst_done, u + 1)
            apart(dve)
            for t in range(n):
                ins = nc.vector.bn_aggr(fmv[:, t, :], fst[:, t, :])
            ins.then_inc(fmv_ready, 1)
            dve.wait_ge(frs_ready, u + 1)
            need(dve, y1, u)
            for t in range(n):
                ins = nc.vector.tensor_scalar(nrm[:, t, :], res[:, t, :], fmv[:, t, 0:1], frs[:, t:t + 1], ALU.subtract, ALU.mult)
            ins.then_inc(nrm_ready, 1)

        units(dve, body, image_start)

    def scalar(act):
        act.wait_ge(ln_ps, 1)
        nc.scalar.copy(lng_lnb[:, :, :], bank[4][:, 0:2 * D].rearrange("p (a c) -> p a c", a=2)).then_inc(ln_ready, 1)
        act.wait_ge(A["gate_summed"], STEPS)
        act.wait_ge(A["wo_ps"], STEPS)

        def cols_out(u, par, n):
            act.wait_ge(fhT_ps, u + 1)
            need(act, hid_ps, FB * (u - 1))
            nc.scalar.copy(ghT[par][:, 0:n, :], by4(bank[3])[:, 0:n, :]).then_inc(fhT_ready, 1)

        cols_out(0, 0, GROUP)
        act.wait_ge(b1_ready, 1)

        def body(b, g, u, par, n, nxt):
            for f in range(FB):
                act.wait_ge(hid_ps, FB * u + f + 1)
                if f == 0:
                    need(act, out_ps, u)
                nc.scalar.activation(hid[f][:, 0:n * C], bank[(0, 1, 4, 5)[f]][:, 0:n * C], ACT.Relu, bias=b1mix[:, b, f:f + 1]).then_inc(hid_ready, 1)
            if nxt is not None:
                cols_out(u + 1, 1 - par, nxt[2])

        units(act, body)

    def gpsimd(pool):
        pool.wait_ge(b2_ready, 1)
        pool.wait_ge(ln_ready, 1)

        def body(b, g, u, par, n, nxt):
            pool.wait_ge(fhn_ready, u + 1)
            need(pool, res_ready, u - 1)
            nc.gpsimd.tensor_tensor(fhnb[par][:, 0:n, :], fhn[par][:, 0:n, :], b2mix[:, b, :].unsqueeze(1).broadcast_to([D, n, D]), ALU.add).then_inc(fhnb_ready, 1)
            pool.wait_ge(fmv_ready, u + 1)
            apart(pool)
            nc.gpsimd.tensor_scalar(fve[:, 0:n], fmv[:, 0:n, 1], EPS, None, ALU.add).then_inc(fve_ready, 1)
            pool.wait_ge(fve_ready, u + 1)
            need(pool, nrm_ready, u)
            nc.gpsimd.tensor_tensor(frs[:, 0:n], fve[:, 0:n], half_neg[:, 0:n], ALU.pow).then_inc(frs_ready, 1)
            pool.wait_ge(nrm_ready, u + 1)
            need(pool, y_out[par], (u - par) * 8)
            nc.gpsimd.tensor_tensor(y[par][:, 0:n, :], nrm[:, 0:n, :], lng.unsqueeze(1).broadcast_to([D, n, D]), ALU.mult).then_inc(y1, 1)
            pool.wait_ge(y1, u + 1)
            nc.gpsimd.tensor_tensor(y[par][:, 0:n, :], y[par][:, 0:n, :], lnb.unsqueeze(1).broadcast_to([D, n, D]), ALU.add).then_inc(y2, 1)
            pool.wait_ge(y2, u + 1)
            apart(pool)
            nc.gpsimd.tensor_tensor(y[par][:, 0:n, :], y[par][:, 0:n, :], h1buf[:, b, bass.ds(g * GROUP, n), :], ALU.add).then_inc(y_ready, 1)

        units(pool, body)

    def tensor(pe):
        mm, tr = nc.tensor.matmul, nc.tensor.transpose

        def to_cols(u, par, n):
            pe.wait_ge(fhn_ready, u + 1)
            need(pe, fhT_ready, u)
            for t in range(n):
                ins = tr(by4(bank[3])[:, t, :], fhn[par][:, t, :], ident[:, :])
            ins.then_inc(fhT_ps, 1)

        tensor_early(pe)
        pe.wait_ge(gh_ready, 1)
        for b in range(NB):
            mm(bank[0][:, b * NE:(b + 1) * NE], ghm[:, b:b + 1].broadcast_to([D, D]), gfc2T[:, :], start=True, stop=True)
        mm(bank[0][0:NE, 64:64 + NB], gfc2T[:, :], ghm[:, :], start=True, stop=True).then_inc(g_ps2, 1)
        to_cols(0, 0, GROUP)
        pe.wait_ge(g_ready, 1)
        for f in range(FB):
            mm(bank[6][:, f * NB:(f + 1) * NB], tvb1[:, f * D:(f + 1) * D], g_T[:, :], start=True, stop=True)
        for b in range(NB):
            mm(by4(bank[7])[:, b, :], g_T[:, b:b + 1].broadcast_to([NE, D]), tvb2[:, :], start=True, stop=False)
            ins = mm(by4(bank[7])[:, b, :], ones[0:1, :], ln_rows[:, 2, :], start=False, stop=True)
        ins.then_inc(bias_ps, 1)

        pe.wait_ge(ln_ready, 1)

        def body(b, g, u, par, n, nxt):
            pe.wait_ge(fhT_ready, u + 1)
            w1, w2 = w1T[b % 2], w2T[b % 2]

            def hidden(f):
                need(pe, hid_ready, FB * (u - 1) + f + 1)
                mm(bank[(0, 1, 4, 5)[f]][:, 0:n * C], w1[:, f, :], ghT[par][:, 0:n, :].rearrange("p t c -> p (t c)"), start=True, stop=True).then_inc(hid_ps, 1)

            def project(f):
                pe.wait_ge(hid_ready, FB * u + f + 1)
                if f == 0:
                    need(pe, res_ready, u)
                for t in range(n):
                    ins = mm(by4(bank[2])[:, t, :], hid[f][:, t * C:(t + 1) * C], w2[:, f, :], start=(f == 0 and t == 0),
                             stop=(f == FB - 1), skip_group_check=True)
                if f == FB - 1:
                    ins.then_inc(out_ps, 1)

            for f in range(FB):
                hidden(f)
            project(0)
            project(1)
            if nxt is not None:
                to_cols(u + 1, 1 - par, nxt[2])
            project(2)
            project(3)

        units(pe, body, lambda b: pe.wait_ge(mix_step, 2 * NE * (b + 1)))

    return {"sync": sync, "vector": vector, "scalar": scalar, "gpsimd": gpsimd, "tensor": tensor,
            "load": load, "vector_early": vector_early}


_INS = ['x'] + ['L0_tok_' + n for n in ('W', 'b', 'cls')] + ['L0_attn_' + n for n in (
    'Wq', 'bq', 'Wk', 'bk', 'Wv', 'bv', 'Wa', 'ba', 'Wb', 'bb', 'cwq', 'cbq', 'cwk', 'cbk', 'cwv', 'cbv', 'norm_w',
    'Wg', 'bg', 'Wo', 'bo')] + ['L0_ffn_' + n for n in (
        'gfc1_w', 'gfc1_b', 'gfc2_w', 'gfc2_b', 'W1', 'b1', 'W2', 'b2', 'ln_g', 'ln_b', 'tv_W1', 'tv_b1', 'tv_W2',
        'tv_b2', 'tv_ln_g', 'tv_ln_b')]
_TRANSPOSED = ['L0_tok_W'] + ['L0_attn_' + n for n in ('Wq', 'Wk', 'Wv', 'Wa', 'Wb', 'Wg', 'Wo')] + [
    'L0_ffn_gfc1_w', 'L0_ffn_gfc2_w', 'L0_ffn_W1', 'L0_ffn_W2']


def kernel(**inputs):
    import numpy as _np
    import concourse.bacc as _bacc
    from concourse import mybir as _mybir
    from concourse.bass_utils import run_bass_kernel_spmd as _run

    nc = _bacc.Bacc("TRN2", target_bir_lowering=False, num_devices=1)
    arrays, args = {}, []
    for name in _INS:
        a = _np.asarray(inputs[name])
        if name == 'x':
            a = a.reshape(NB, 3, GRID, PATCH, GRID, PATCH).transpose(1, 3, 5, 0, 2, 4).reshape(PIX, NB, GRID * GRID)
        elif name in _TRANSPOSED:
            a = a.T
        elif name in ('L0_ffn_tv_W1', 'L0_ffn_tv_W2'):
            a = a.transpose(0, 2, 1)
        elif name.startswith('L0_attn_cw'):
            a = a.reshape(D, TAPS).T
        elif name == 'L0_ffn_b1':
            a = a.reshape(FB, D).T
        a = _np.ascontiguousarray(a)
        arrays[f"in_{name}_dram"] = a
        args.append(nc.dram_tensor(f"in_{name}_dram", a.shape, _mybir.dt.from_np(a.dtype), kind="ExternalInput").ap())
    args.append(nc.dram_tensor("out_0_dram", (NB, TOK, D), _mybir.dt.float32, kind="ExternalOutput").ap())
    vit_tower(nc, *args)
    r = _run(nc, [arrays], core_ids=[0])
    return r.results[0]["out_0_dram"]
```

```python
import concourse.bass as bass
from concourse import mybir
from contextlib import ExitStack

F32 = mybir.dt.float32
BF16 = mybir.dt.bfloat16
ALU = mybir.AluOpType
ACT = mybir.ActivationFunctionType
AX = mybir.AxisListType

NB = 4
IMG, PATCH = 224, 4
GRID = IMG // PATCH
TOK = GRID * GRID + 1
D = 128
C = 128
STEPS = -(-TOK // C)
LAST = TOK - C * (STEPS - 1)
PIX = 3 * PATCH * PATCH
KX = PIX + 3
TAPS = 4
HIST = TAPS - 1
LEVELS = 7
EPS = 1e-5
F = 512
FB = F // D
NE = 8
LN_MERGE = 0.03
GROUP = 4
GROUPS = STEPS // GROUP
UNITS = GROUPS + 1


def need(engine, semaphore, value):
    if not isinstance(value, int) or value > 0:
        engine.wait_ge(semaphore, value)


def apart(engine):
    engine.nop(nofuse=True)


def vit_tower(nc, x, tok_WT, tok_b, tok_cls, WqT, bq, WkT, bk, WvT, bv, WaT, ba, WbT, bb, cwqT, cbq, cwkT, cbk,
              cwvT, cbv, norm_w, WgT, bg, WoT, bo, gfc1_wT, gfc1_b, gfc2_wT, gfc2_b, W1, b1, W2, b2, ln_g, ln_b,
              tv_W1, tv_b1, tv_W2, tv_b2, tv_ln_g, tv_ln_b, out):
    ctx = ExitStack()
    with ctx:
        def sb(name, shape, dt=F32):
            return ctx.enter_context(nc.sbuf_tensor(name, shape, dt))

        def sem(name):
            return ctx.enter_context(nc.semaphore(name))

        ident = sb("ident", [D, D])
        ident4 = sb("ident4", [D, NB, D])
        ident_bf = sb("ident_bf", [D, NB, D], BF16)
        ident0 = sb("ident0", [D, D])
        masks = sb("masks", [D, LEVELS, D // 2])
        mask_x = sb("mask_x", [D, KX])
        mask_1 = sb("mask_1", [D, KX])
        ones = sb("ones", [D, D])
        half_neg = sb("half_neg", [D, 4])
        half_pos = sb("half_pos", [D, 4])
        euler = sb("euler", [D, 8])

        We = sb("We", [D, D])
        SA = sb("SA", [D, 516])
        SB = sb("SB", [D, 512])
        Wo_T = sb("Wo_T", [D, D])
        gfc1_T = sb("gfc1_T", [D, D])
        gfc1_bc = sb("gfc1_bc", [D, 1])
        bo_rows = sb("bo_rows", [D, D])

        h1buf = sb("h1buf", [D, NB, STEPS, C])
        xc = h1buf[0:KX, :, :, :].rearrange("p b s c -> p b (s c)")
        ln2 = sb("ln2", [D, STEPS, NB, 2])

        work = sb("work", [D, 25420])
        offset = [0]

        def tile(n, *shape):
            at = offset[0]
            offset[0] += n
            t = work[:, at:at + n]
            if len(shape) == 2:
                return t.rearrange("p (a c) -> p a c", a=shape[0])
            if len(shape) == 3:
                return t.rearrange("p (a b c) -> p a b c", a=shape[0], b=shape[1])
            return t

        xt = [tile(NB * C, NB, C) for _ in range(2)]
        XW = HIST + C
        xs = [tile(NB * XW, NB, XW) for _ in range(2)]
        rmat = tile(NB * KX, NB, KX)
        kvg = [tile(NB * 3 * D, NB, 3 * D) for _ in range(2)]
        gate_kept = tile(NB * D, NB, D)
        kT = [tile(NB * D, NB, D) for _ in range(2)]
        qT = [tile(NB * D, NB, D) for _ in range(2)]
        decay = tile(NB * C, NB, C)
        cdecay = tile(NB * C, NB, C)
        Bm = [tile(NB * C, NB, C) for _ in range(2)]
        Pm = [tile(NB * C, NB, C) for _ in range(2)]
        kd = [tile(NB * D, NB, D) for _ in range(2)]
        vt = [tile(NB * D, NB, D) for _ in range(2)]
        newblk = {k: tile(NB * C, NB, C) for k in range(1, 5)}
        N5 = tile(NB * 32, NB, 32)
        N6 = tile(NB * 64, NB, 64)
        pairs = tile(NB * 64, NB, 64)
        Y = [tile(NB * C, NB, C) for _ in range(2)]
        X = [tile(NB * C, NB, C) for _ in range(2)]
        state = tile(NB * D, NB, D)
        Rn = tile(NB * D, NB, D)
        Zn = tile(NB * D, NB, D)
        QMs = tile(NB * D, NB, D)
        o = tile(NB * D, NB, D)
        sq = tile(NB * D, NB, D)
        sq_q = tile(NB * D, NB, D)
        sq_o = tile(NB * D, NB, D)
        og = tile(NB * D, NB, D)
        ogT = tile(NB * D, NB, D)
        hn = tile(NB * D, NB, D)
        hnT = tile(NB * D, NB, D)
        relu_h = tile(NB * D, NB, D)
        gate_sum = tile(NB * D, NB, D)
        attention_end = offset[0]

        stats1 = sb("stats1", [D, NB, 6])
        mv1 = sb("mv1", [D, NB, 2])
        var1e = sb("var1e", [D, NB])
        rstd1 = sb("rstd1", [D, NB])
        logit = sb("logit", [D, 8])
        expo = sb("expo", [D, 8])
        expo1 = sb("expo1", [D, 8])
        ab = sb("ab", [D, 8])
        ssk = sb("ssk", [D, NB])
        kn2 = sb("kn2", [D, NB])
        rk2 = sb("rk2", [D, NB])
        cneg = sb("cneg", [D, NB])
        knorm = sb("knorm", [D, NB])
        vsum = sb("vsum", [D, NB])
        vmean = sb("vmean", [D, NB])
        qn2e = [sb(f"qn2e{i}", [D, NB]) for i in range(2)]
        glast = sb("glast", [1, NB])
        gs = [sb(f"gs{i}", [D, 8]) for i in range(2)]
        so2 = sb("so2", [D, NB])
        ovar = sb("ovar", [D, NB])
        oscale = sb("oscale", [D, NB])
        stats2 = sb("stats2", [D, NB, 6])
        mv2 = sb("mv2", [D, NB, 2])
        var2e = sb("var2e", [D, NB])
        rstd2 = sb("rstd2", [D, NB])

        bank = [ctx.enter_context(nc.psum_tensor(f"bank{i}", [D, 512], F32)) for i in range(8)]
        blk_ps, X_ps, small_ps = bank[0], bank[2], bank[7]

        def by4(t):
            return t[:, :].rearrange("p (b c) -> p b c", b=NB)

        def by32(t):
            return t[:, 0:NB * 32].rearrange("p (b c) -> p b c", b=NB)

        def by64(t):
            return t[:, 0:NB * 64].rearrange("p (b c) -> p b c", b=NB)

        offset[0] = 0
        pro = tile(12288)
        nat = pro[:, 128:128 + 2 * D].rearrange("p (a c) -> p a c", a=2)
        Wc = pro[:, 1664:1664 + D]
        wmean = pro[:, 1792:1793]
        wsum = pro[:, 1794:1795]
        WcT = pro[:, 1920:1920 + D]
        rhs_all = pro[:, 2048:2048 + 516]
        fold = pro[:, 2580:2580 + 516]
        bias_row = pro[0:1, 3100:3100 + 516]
        cb_row = pro[0:1, 3620:3620 + 512]
        onehot2 = pro[0:1, 4140:4140 + D]
        onehot1 = pro[0:1, 4268:4268 + D]
        cwT = pro[0:TAPS, 4410:4410 + 384]
        selA = pro[0:TAPS, 4800:4800 + D]
        selB = pro[0:TAPS, 4930:4930 + D]
        nw_col = pro[:, 5060:5061]
        cwA = pro[:, 5100:5100 + 384]
        cwB = pro[:, 5500:5500 + 384]
        tmpf = pro[:, 5900:5900 + 516]
        cbs = pro[:, 6420:6420 + 384]

        x_in = sem("x_in")
        x_const = sem("x_const")
        w_in = sem("w_in")
        con = sem("con")
        pro_pe = sem("pro_pe")
        pro_dve = sem("pro_dve")
        We_zero = sem("We_zero")
        ones_set = sem("ones_set")

        xt_ready = sem("xt_ready")
        h0_ps = sem("h0_ps")
        h0_kept = sem("h0_kept")
        h0_biased = sem("h0_biased")
        stats1_done = sem("stats1_done")
        mv1_ready = sem("mv1_ready")
        var1e_ready = sem("var1e_ready")
        rstd1_ready = sem("rstd1_ready")
        rmask_done = sem("rmask_done")
        rmat_ready = sem("rmat_ready")
        rb_ps = sem("rb_ps")
        hist_ready = sem("hist_ready")
        xs_ready = sem("xs_ready")
        xs_shifted = sem("xs_shifted")
        kvg_ps = sem("kvg_ps")
        kvg_ready = sem("kvg_ready")
        logit_ps = sem("logit_ps")
        logit_ready = sem("logit_ready")
        expo_ready = sem("expo_ready")
        expo1_ready = sem("expo1_ready")
        ab_ready = sem("ab_ready")
        q_ps = sem("q_ps")
        qT_ready = sem("qT_ready")
        kT_ps = sem("kT_ps")
        kT_ready = sem("kT_ready")
        alpha_ps = sem("alpha_ps")
        decay_ready = sem("decay_ready")
        glast_ready = sem("glast_ready")
        ssk_ready = sem("ssk_ready")
        kn2_ready = sem("kn2_ready")
        rk2_ready = sem("rk2_ready")
        cneg_ready = sem("cneg_ready")
        knorm_ready = sem("knorm_ready")
        vsum_ready = sem("vsum_ready")
        vmean_ready = sem("vmean_ready")
        vt_ready = sem("vt_ready")
        cdecay_ready = sem("cdecay_ready")
        kd_ready = sem("kd_ready")
        kk_ps = sem("kk_ps")
        kq_ps = sem("kq_ps")
        B_ready = sem("B_ready")
        P_ready = sem("P_ready")
        sqq_ready = sem("sqq_ready")
        qq_ps = sem("qq_ps")
        qn2_ready = sem("qn2_ready")
        g_ps = sem("g_ps")
        gs_ready = sem("gs_ready")
        gate_ready = sem("gate_ready")
        blk_ps_done = sem("blk_ps_done")
        blk_ready = sem("blk_ready")
        Xps_done = sem("Xps_done")
        Y5ps_done = sem("Y5ps_done")
        pairs_ready = sem("pairs_ready")
        X_ready = sem("X_ready")
        Y_ready = sem("Y_ready")
        Y5_ready = sem("Y5_ready")
        X5_ready = sem("X5_ready")
        X6_ready = sem("X6_ready")
        X_reset = sem("X_reset")
        km_ps = sem("km_ps")
        Rn_ready = sem("Rn_ready")
        z_ps = sem("z_ps")
        Zn_ready = sem("Zn_ready")
        qm_ps = sem("qm_ps")
        QMs_ready = sem("QMs_ready")
        pz_ps = sem("pz_ps")
        o_ready = sem("o_ready")
        dm_ps = sem("dm_ps")
        state_ready = sem("state_ready")
        so2_ready = sem("so2_ready")
        ovar_ready = sem("ovar_ready")
        oscale_ready = sem("oscale_ready")
        og_ready = sem("og_ready")
        ogT_ps = sem("ogT_ps")
        ogT_ready = sem("ogT_ready")
        wo_ps = sem("wo_ps")
        h1_ready = sem("h1_ready")
        stats2_done = sem("stats2_done")
        mv2_ready = sem("mv2_ready")
        var2e_ready = sem("var2e_ready")
        rstd2_ready = sem("rstd2_ready")
        hn_ready = sem("hn_ready")
        hnT_ps = sem("hnT_ps")
        hnT_ready = sem("hnT_ready")
        gf_ps = sem("gf_ps")
        relu_ready = sem("relu_ready")
        gate_summed = sem("gate_summed")
        ln2_kept = sem("ln2_kept")

        def half(t, b, k, second):
            m = 1 << k
            if b is None:
                return t.rearrange("p b (n h m) -> p b n h m", h=2, m=m)[:, :, :, second, :]
            return t[:, b, :].rearrange("p (n h m) -> p n h m", h=2, m=m)[:, :, second, :]

        def on(j, lag):
            return not isinstance(j, int) or 0 <= j + lag < STEPS

        first, last = -2, STEPS + 1
        LOOP = (4, STEPS - 3)
        assert (LOOP[1] - LOOP[0]) % 2 == 0

        def iterations(engine, body):
            for j in range(first, LOOP[0]):
                body(j, j % 2)
            with engine.Fori(LOOP[0], LOOP[1] - 1, 2) as j:
                body(j, 0)
                body(j + 1, 1)
            for j in range(LOOP[1], last + 1):
                body(j, j % 2)

        DVE_PRO = 18
        LE, LF, LI, LC, LH = 2, 1, 0, -1, -2
        block = ctx.enter_context(nc.Block())

        def row1(v):
            return v.rearrange("(a n) -> a n", a=1)

        def col1(v):
            return v.rearrange("(p a) -> p a", a=1)

        weights_early = [
            (We[0:PIX, :], tok_WT[:, :]), (We[PIX:PIX + 1, :], row1(tok_b)),
            (We[PIX + 2:PIX + 3, :], tok_cls.rearrange("a b p -> (a b) p")),
            (rhs_all[:, 0:128], WkT[:, :]), (rhs_all[:, 128:256], WvT[:, :]), (rhs_all[:, 256:384], WgT[:, :]),
            (rhs_all[:, 384:512], WqT[:, :]), (rhs_all[:, 512:513], WaT[:, :]), (rhs_all[:, 513:514], WbT[:, :]),
            (nat[:, 0, :], WoT[:, :]), (nat[:, 1, :], gfc1_wT[:, :]),
            (bias_row[:, 0:128], row1(bk)), (bias_row[:, 128:256], row1(bv)), (bias_row[:, 256:384], row1(bg)),
            (bias_row[:, 384:512], row1(bq)), (bias_row[:, 512:513], row1(ba)), (bias_row[:, 513:514], row1(bb)),
            (cb_row[:, 0:128], row1(cbk)), (cb_row[:, 128:256], row1(cbv)), (cb_row[:, 256:384], row1(cbq)),
            (cwT[:, 0:128], cwkT[:, :]), (cwT[:, 128:256], cwvT[:, :]), (cwT[:, 256:384], cwqT[:, :]),
            (nw_col, col1(norm_w)), (gfc1_bc[:, :], col1(gfc1_b)), (bo_rows[:, :], bo.partition_broadcast(D)),
        ]
        W_IN = 16 * len(weights_early)

        ffn = make_ffn(nc, ctx, sb, sem, work, locals())

        @block.sync
        def _(sp):
            sp.wait_ge(We_zero, 1)
            for dst, src in weights_early:
                sp.dma_start(dst, src).then_inc(w_in, 16)
            ffn["load"](sp)
            ffn["sync"](sp)

        @block.scalar
        def _(act):
            act.wait_ge(x_const, 2)
            for b in range(NB):
                act.dma_start(xc[0:PIX, b, 1:TOK], x[:, b, :]).then_inc(x_in, 16)

            def body(j, par):
                p = 1 - par

                def kvg_out(b):
                    if on(j, LF):
                        s = j + LF
                        act.wait_ge(kvg_ps, NB * s + b + 1)
                        if b == 0:
                            need(act, gate_ready, s - 1)
                            need(act, kd_ready, s - 1)
                            need(act, vt_ready, s - 1)
                            need(act, expo_ready, s)
                        ins = nc.scalar.mul(logit[:, b:b + 5:4], bank[4 - b % 2][:, 384:386], -1.0)
                        if b == NB - 1:
                            ins.then_inc(logit_ready, 1)
                        nc.scalar.activation(kvg[p][:, b, :], bank[4 - b % 2][:, 0:384], ACT.Silu).then_inc(kvg_ready, 1)

                kvg_out(0)
                kvg_out(1)
                if on(j, LC):
                    s = j + LC
                    act.wait_ge(z_ps, s + 1)
                    need(act, dm_ps, s)
                    nc.scalar.copy(Zn, by4(bank[5])).then_inc(Zn_ready, 1)
                    nc.scalar.copy(X[p], ident4[:, :, :]).then_inc(X_reset, 1)
                if on(j, LE):
                    s = j + LE
                    act.wait_ge(h0_ps, s + 1)
                    act.wait_ge(xt_ready, s + 1)
                    nc.scalar.copy(h1buf[:, :, bass.ds(s, 1), :].rearrange("p b s c -> p b (s c)"), by4(bank[1])).then_inc(h0_kept, 1)
                kvg_out(2)
                if on(j, LC):
                    s = j + LC
                    act.wait_ge(qm_ps, s + 1)
                    act.wait_ge(gs_ready, s + 1)
                    need(act, o_ready, s)
                    for b in range(NB):
                        ins = nc.scalar.activation(QMs[:, b, :], by4(bank[6])[:, b, :], ACT.Copy, scale=gs[p][:, b:b + 1])
                    ins.then_inc(QMs_ready, 1)
                kvg_out(3)
                if on(j, LF):
                    s = j + LF
                    act.wait_ge(kvg_ready, NB * (s + 1))
                    need(act, kn2_ready, s)
                    for b in range(NB):
                        ins = nc.scalar.activation(sq[:, b, :], kvg[p][:, b, 0:D], ACT.Square, accum_out=ssk[:, b:b + 1])
                    ins.then_inc(ssk_ready, 1)
                    act.wait_ge(q_ps, s + 1)
                    need(act, qm_ps, s - 1)
                    nc.scalar.activation(qT[p], by4(bank[4]), ACT.Silu).then_inc(qT_ready, 1)
                    act.wait_ge(kT_ps, s + 1)
                    nc.scalar.copy(kT[p], by4(bank[3])).then_inc(kT_ready, 1)
                if on(j, LC):
                    s = j + LC
                    act.wait_ge(o_ready, s + 1)
                    need(act, ovar_ready, s)
                    for b in range(NB):
                        ins = nc.scalar.activation(sq_o[:, b, :], o[:, b, :], ACT.Square, accum_out=so2[:, b:b + 1])
                    ins.then_inc(so2_ready, 1)
                if on(j, LH):
                    s = j + LH
                    act.wait_ge(hnT_ps, s + 1)
                    need(act, gf_ps, s)
                    nc.scalar.copy(hnT, by4(bank[6])).then_inc(hnT_ready, 1)
                if on(j, LI):
                    s = j + LI
                    s = j + LI
                    act.wait_ge(Y5ps_done, s + 1)
                    for r in (0, 64):
                        ins = nc.scalar.copy(Y[par][r + 32:r + 64, :, r:r + 32], by32(bank[1])[r + 32:r + 64])
                    ins.then_inc(Y5_ready, 1)
                    act.wait_ge(Xps_done, 6 * s + 5)
                    for r in (0, 64):
                        ins = nc.scalar.copy(X[par][r:r + 32, :, r + 32:r + 64], by32(X_ps)[r:r + 32])
                    ins.then_inc(X5_ready, 1)
                if on(j, LH):
                    s = j + LH
                    act.wait_ge(gf_ps, s + 1)
                    need(act, gate_summed, s)
                    nc.scalar.activation(relu_h, by4(bank[5]), ACT.Relu, bias=gfc1_bc[:, 0:1]).then_inc(relu_ready, 1)
                if on(j, LI):
                    s = j + LI
                    act.wait_ge(Xps_done, 6 * s + 6)
                    nc.scalar.copy(X[par][0:64, :, 64:128], by64(X_ps)[0:64]).then_inc(X6_ready, 1)
                if on(j, LC):
                    s = j + LC
                    act.wait_ge(ogT_ps, s + 1)
                    need(act, wo_ps, s)
                    nc.scalar.copy(ogT, by4(bank[5])).then_inc(ogT_ready, 1)
                if on(j, LE):
                    s = j + LE
                    act.wait_ge(hist_ready, s + 1)
                    act.wait_ge(xs_ready, s + 1)
                    need(act, q_ps, s - 1)
                    nc.scalar.copy(xs[par][64:64 + KX, :, 1:XW], xs[par][0:KX, :, 0:XW - 1]).then_inc(xs_shifted, 1)

            iterations(act, body)
            ffn["scalar"](act)

        @block.gpsimd
        def _(pool):
            nc.gpsimd.memset(ones[:, :], 1.0).then_inc(ones_set, 1)
            nc.gpsimd.memset(masks[:, :, :], 1.0).then_inc(ones_set, 1)
            nc.gpsimd.memset(half_neg[:, :], -0.5)
            nc.gpsimd.memset(half_pos[:, :], 0.5)
            nc.gpsimd.memset(euler[:, :], 2.718281828459045).then_inc(ones_set, 1)
            pool.wait_ge(ones_set, 3)
            nc.gpsimd.affine_select(out=ident[:, :], in_=ones[:, :], pattern=[[-1, D]], compare_op=ALU.is_equal,
                                    fill=0.0, base=0, channel_multiplier=1).then_inc(con, 1)
            pool.wait_ge(con, 1)
            nc.gpsimd.affine_select(out=ident0[:, :], in_=ident[:, :], pattern=[[1, D]], compare_op=ALU.is_gt,
                                    fill=0.0, base=0, channel_multiplier=0)
            for b in range(NB):
                nc.gpsimd.tensor_copy(ident4[:, b, :], ident[:, :])
                nc.gpsimd.tensor_copy(ident_bf[:, b, :], ident[:, :])
            nc.gpsimd.affine_select(out=mask_1[:, :], in_=ones[:, 0:KX], pattern=[[1, KX]], compare_op=ALU.is_equal,
                                    fill=0.0, base=-(PIX + 1), channel_multiplier=0)
            nc.gpsimd.affine_select(out=mask_x[:, :], in_=ones[:, 0:KX], pattern=[[1, KX]], compare_op=ALU.not_equal,
                                    fill=0.0, base=-(PIX + 1), channel_multiplier=0)
            sel = ((selA, 3, 2), (selB, 1, 0))
            for t, low, high in sel:
                nc.gpsimd.affine_select(out=t[:, 0:64], in_=ones[0:TAPS, 0:64], pattern=[[0, 64]],
                                        compare_op=ALU.is_equal, fill=0.0, base=-low, channel_multiplier=1)
                nc.gpsimd.affine_select(out=t[:, 64:128], in_=ones[0:TAPS, 0:64], pattern=[[0, 64]],
                                        compare_op=ALU.is_equal, fill=0.0, base=-high, channel_multiplier=1)
            nc.gpsimd.affine_select(out=onehot2.rearrange("p (h c) -> p h c", h=2), in_=ones[0:1, :].rearrange("p (h c) -> p h c", h=2),
                                    pattern=[[0, 2], [1, 64]], compare_op=ALU.is_equal, fill=0.0, base=-(PIX + 1), channel_multiplier=0)
            nc.gpsimd.affine_select(out=onehot1, in_=ones[0:1, :], pattern=[[1, D]],
                                    compare_op=ALU.is_equal, fill=0.0, base=-(PIX + 1), channel_multiplier=0).then_inc(con, 1)
            for k in range(LEVELS):
                m = 1 << k
                n = D // (2 * m)
                v = masks[:, k, :].rearrange("p (n m) -> p n m", m=m)
                nc.gpsimd.affine_select(out=v, in_=v, pattern=[[-2 * m, n], [0, m]], compare_op=ALU.is_ge,
                                        fill=0.0, base=-m, channel_multiplier=1).then_inc(con, 1)
            pool.wait_ge(con, 2 + LEVELS)
            for k in range(LEVELS):
                m = 1 << k
                n = D // (2 * m)
                v = masks[:, k, :].rearrange("p (n m) -> p n m", m=m)
                nc.gpsimd.affine_select(out=v, in_=v, pattern=[[2 * m, n], [0, m]], compare_op=ALU.is_ge,
                                        fill=0.0, base=2 * m - 1, channel_multiplier=-1).then_inc(con, 1)
            pool.wait_ge(con, 2 + 2 * LEVELS)
            pool.wait_ge(x_const, 1)
            nc.gpsimd.affine_select(out=xc[32:KX, :, 0:1], in_=xc[32:KX, :, 0:1], pattern=[[0, NB], [0, 1]], compare_op=ALU.is_ge,
                                    fill=0.0, base=-(PIX + 1 - 32), channel_multiplier=1)
            nc.gpsimd.affine_select(out=xc[32:KX, :, 1:TOK], in_=xc[32:KX, :, 1:TOK], pattern=[[0, NB], [0, TOK - 1]],
                                    compare_op=ALU.is_ge, fill=0.0, base=PIX + 1 - 32, channel_multiplier=-1).then_inc(x_const, 1)

            pool.wait_ge(pro_dve, DVE_PRO)
            pool.wait_ge(x_in, 16 * NB)

            def body(j, par):
                p = 1 - par
                if on(j, LE):
                    s = j + LE
                    need(pool, xs_ready, s - 1)
                    need(pool, h0_ps, s - 1)
                    apart(pool)
                    nc.gpsimd.tensor_copy(xt[par][0:KX, :, :], xc[:, :, bass.ds(s * C, C)]).then_inc(xt_ready, 1)
                if on(j, LE):
                    s = j + LE
                    if not isinstance(s, int) or s > 0:
                        pool.wait_ge(xs_ready, s)
                        need(pool, q_ps, s - 1)
                        need(pool, xs_shifted, s - 1)
                        apart(pool)
                        nc.gpsimd.tensor_copy(xs[par][0:KX, :, 0:HIST], xs[p][0:KX, :, C:XW]).then_inc(hist_ready, 1)
                    else:
                        nc.gpsimd.memset(xs[par][0:KX, :, 0:HIST], 0.0).then_inc(hist_ready, 1)
                if on(j, LH):
                    s = j + LH
                    pool.wait_ge(mv2_ready, s + 1)
                    need(pool, rstd2_ready, s)
                    apart(pool)
                    nc.gpsimd.tensor_scalar(var2e[:, :], mv2[:, :, 1], EPS, None, ALU.add).then_inc(var2e_ready, 1)
                    pool.wait_ge(var2e_ready, s + 1)
                    need(pool, ln2_kept, s)
                    nc.gpsimd.tensor_tensor(rstd2[:, :], var2e[:, :], half_neg[:, :], ALU.pow).then_inc(rstd2_ready, 1)
                if on(j, LE):
                    s = j + LE
                    pool.wait_ge(mv1_ready, s + 1)
                    need(pool, rstd1_ready, s)
                    apart(pool)
                    nc.gpsimd.tensor_scalar(var1e[:, :], mv1[:, :, 1], EPS, None, ALU.add).then_inc(var1e_ready, 1)
                    pool.wait_ge(var1e_ready, s + 1)
                    need(pool, rmask_done, s)
                    nc.gpsimd.tensor_tensor(rstd1[:, :], var1e[:, :], half_neg[:, :], ALU.pow).then_inc(rstd1_ready, 1)
                    pool.wait_ge(rstd1_ready, s + 1)
                    need(pool, rb_ps, s)
                    nc.gpsimd.tensor_tensor(rmat, mask_x[:, :].unsqueeze(1).broadcast_to([D, NB, KX]),
                                            rstd1[:, :].unsqueeze(2).broadcast_to([D, NB, KX]), ALU.mult).then_inc(rmask_done, 1)
                    pool.wait_ge(rmask_done, s + 1)
                    nc.gpsimd.tensor_tensor(rmat, rmat, mask_1[:, :].unsqueeze(1).broadcast_to([D, NB, KX]),
                                            ALU.add).then_inc(rmat_ready, 1)
                if on(j, LF):
                    s = j + LF
                    pool.wait_ge(logit_ready, s + 1)
                    need(pool, expo1_ready, s)
                    nc.gpsimd.tensor_tensor(expo[:, :], euler[:, :], logit[:, :], ALU.pow).then_inc(expo_ready, 1)
                    pool.wait_ge(qT_ready, s + 1)
                    need(pool, qq_ps, s)
                    nc.gpsimd.tensor_tensor(sq_q, qT[p], qT[p], ALU.mult).then_inc(sqq_ready, 1)
                    pool.wait_ge(kn2_ready, s + 1)
                    need(pool, vt_ready, s)
                    nc.gpsimd.tensor_tensor(knorm[:, :], kn2[:, :], half_pos[:, :], ALU.pow).then_inc(knorm_ready, 1)
                if on(j, LC):
                    s = j + LC
                    pool.wait_ge(ovar_ready, s + 1)
                    need(pool, og_ready, s)
                    nc.gpsimd.tensor_tensor(oscale[:, :], ovar[:, :], half_neg[:, :], ALU.pow).then_inc(oscale_ready, 1)
                if on(j, LF):
                    s = j + LF
                    pool.wait_ge(decay_ready, s + 1)
                    pool.wait_ge(cneg_ready, s + 1)
                    need(pool, P_ready, s)
                    need(pool, kd_ready, s)
                    nc.gpsimd.tensor_tensor(cdecay, decay, cneg[:, :].unsqueeze(2).broadcast_to([D, NB, C]),
                                            ALU.mult).then_inc(cdecay_ready, 1)
                if on(j, LH):
                    s = j + LH
                    pool.wait_ge(relu_ready, s + 1)
                    need(pool, gate_summed, s)
                    n = LAST if isinstance(s, int) and s == STEPS - 1 else C
                    nc.gpsimd.tensor_tensor(gate_sum[:, :, 0:n], gate_sum[:, :, 0:n], relu_h[:, :, 0:n],
                                            ALU.add).then_inc(gate_summed, 1)
                if on(j, LI):
                    s = j + LI
                    pool.wait_ge(kvg_ready, NB * (s + 1))
                    need(pool, og_ready, s)
                    apart(pool)
                    nc.gpsimd.tensor_copy(gate_kept, kvg[par][:, :, 2 * D:3 * D]).then_inc(gate_ready, 1)
                if on(j, LE):
                    s = j + LE
                    pool.wait_ge(h0_kept, s + 1)
                    h = h1buf[:, :, bass.ds(s, 1), :].rearrange("p b s c -> p b (s c)")
                    apart(pool)
                    nc.gpsimd.tensor_tensor(h, h, bo_rows[:, :].unsqueeze(1).broadcast_to([D, NB, D]),
                                            ALU.add).then_inc(h0_biased, 1)

            iterations(pool, body)
            ffn["gpsimd"](pool)

        @block.vector
        def _(dve):
            done = [0]

            def step_done(ins):
                done[0] += 1
                ins.then_inc(pro_dve, 1)
                dve.wait_ge(pro_dve, done[0])

            nc.vector.memset(We[:, :], 0.0).then_inc(We_zero, 1)
            ffn["vector_early"](dve)
            nc.vector.memset(xc[32:KX, :, 0:TOK], 1.0)
            nc.vector.memset(xc[0:32, :, 0:1], 0.0)
            nc.vector.memset(xc[0:KX, :, TOK:STEPS * C], 0.0).then_inc(x_const, 1)
            dve.wait_ge(w_in, W_IN)
            step_done(nc.vector.tensor_reduce(wsum[0:KX, :], We[0:KX, :], AX.X, ALU.add))
            step_done(nc.vector.tensor_scalar(wmean[0:KX, :], wsum[0:KX, :], 1.0 / D, None, ALU.mult))
            step_done(nc.vector.memset(Wc, 0.0))
            step_done(nc.vector.tensor_scalar(Wc[0:KX, :], We[0:KX, :], wmean[0:KX, :], None, ALU.subtract))
            step_done(nc.vector.tensor_scalar(Wo_T[:, :], nat[:, 0, :], nw_col, None, ALU.mult))
            step_done(nc.vector.tensor_copy(gfc1_T[:, :], nat[:, 1, :]))
            step_done(nc.vector.memset(WcT, 0.0))
            dve.wait_ge(pro_pe, 1)
            step_done(nc.vector.tensor_copy(WcT.rearrange("p (h c) -> p h c", h=2)[:, :, 0:KX],
                                            bank[3][:, 0:KX].unsqueeze(1).broadcast_to([D, 2, KX])))
            dve.wait_ge(pro_pe, 2)
            step_done(nc.vector.tensor_copy(fold[:, 0:512], bank[5][:, :]))
            step_done(nc.vector.tensor_copy(fold[:, 512:514], bank[6][:, 0:2]))
            dve.wait_ge(pro_pe, 3)
            for dst, taps in ((SA, bank[0]), (SB, bank[1])):
                step_done(nc.vector.tensor_tensor(dst[:, 0:256], taps[:, 0:256], fold[:, 0:256], ALU.mult))
                dst_q = dst[:, 386:514] if dst is SA else dst[:, 384:512]
                step_done(nc.vector.tensor_tensor(dst_q, taps[:, 256:384], fold[:, 384:512], ALU.mult))
            step_done(nc.vector.tensor_tensor(SA[:, 0:256], bank[2][:, 0:256], SA[:, 0:256], ALU.add))
            step_done(nc.vector.tensor_tensor(SA[:, 386:514], bank[2][:, 256:384], SA[:, 386:514], ALU.add))
            nc.vector.memset(SA[64:128, 256:386], 0.0)
            nc.vector.tensor_copy(SA[0:64, 256:384], fold[0:64, 256:384])
            step_done(nc.vector.tensor_copy(SA[0:64, 384:386], fold[0:64, 512:514]))
            for t in newblk.values():
                nc.vector.memset(t, 0.0)
            dve.wait_ge(con, 2)
            for t in X:
                nc.vector.tensor_copy(t, ident4[:, :, :])
            nc.vector.memset(gate_sum, 0.0)
            nc.vector.memset(state, 0.0)
            nc.vector.memset(xs[0], 0.0)
            step_done(nc.vector.memset(xs[1], 0.0))
            assert done[0] == DVE_PRO

            def body(j, par):
                p = 1 - par

                def new_blocks(k):
                    if not on(j, LI):
                        return
                    s = j + LI
                    dve.wait_ge(blk_ps_done, 6 * s + k)
                    need(dve, Xps_done, 6 * (s - 1) + k)
                    if k == 6:
                        nc.vector.tensor_copy(N6[64:128], by64(blk_ps)[64:128]).then_inc(blk_ready, 1)
                    elif k == 5:
                        for r in (32, 96):
                            ins = nc.vector.tensor_copy(N5[r:r + 32], by32(blk_ps)[r:r + 32])
                        ins.then_inc(blk_ready, 1)
                    else:
                        m = 1 << k
                        nc.vector.tensor_tensor(half(newblk[k], None, k, 0), by64(blk_ps).rearrange("p b (n m) -> p b n m", m=m),
                                                masks[:, k, :].unsqueeze(1).broadcast_to([D, NB, 64]).rearrange("p b (n m) -> p b n m", m=m),
                                                ALU.mult).then_inc(blk_ready, 1)

                def grow(k):
                    if not on(j, LI):
                        return
                    s = j + LI
                    dve.wait_ge(Xps_done, 6 * s + k)
                    x = half(X[par], None, k, 1)
                    nc.vector.tensor_tensor(x, by64(X_ps).rearrange("p b (n m) -> p b n m", m=1 << k), x, ALU.add).then_inc(X_ready, 1)
                    dve.wait_ge(X_ready, 5 * s + k + 1)
                    nc.vector.transpose(Y[par].rearrange("p b c -> p (b c)"), X[par].rearrange("p b c -> p (b c)")).then_inc(Y_ready, 1)

                new_blocks(1)
                if on(j, LH):
                    s = j + LH
                    h = h1buf[:, :, bass.ds(s, 1), :].rearrange("p b s c -> p b (s c)")
                    dve.wait_ge(wo_ps, s + 1)
                    dve.wait_ge(h0_biased, s + 1)
                    nc.vector.tensor_tensor(h, by4(bank[6]), h, ALU.add).then_inc(h1_ready, 1)
                if on(j, LC):
                    s = j + LC
                    dve.wait_ge(km_ps, s + 1)
                    dve.wait_ge(gs_ready, s + 1)
                    dve.wait_ge(vt_ready, s + 1)
                    need(dve, z_ps, s)
                    for b in range(NB):
                        ins = nc.vector.scalar_tensor_tensor(Rn[:, b, :], by4(bank[5])[:, b, :], gs[p][:, b:b + 1], vt[p][:, b, :],
                                                             ALU.mult, ALU.subtract)
                    ins.then_inc(Rn_ready, 1)
                grow(1)
                if on(j, LH):
                    s = j + LH
                    h = h1buf[:, :, bass.ds(s, 1), :].rearrange("p b s c -> p b (s c)")
                    dve.wait_ge(h1_ready, s + 1)
                    need(dve, mv2_ready, s)
                    apart(dve)
                    for b in range(NB):
                        ins = nc.vector.bn_stats(stats2[:, b, :], h[:, b, :])
                    ins.then_inc(stats2_done, 1)
                    dve.wait_ge(stats2_done, s + 1)
                    need(dve, hn_ready, s)
                    apart(dve)
                    for b in range(NB):
                        ins = nc.vector.bn_aggr(mv2[:, b, :], stats2[:, b, :])
                    ins.then_inc(mv2_ready, 1)
                new_blocks(2)
                grow(2)
                if on(j, LE):
                    s = j + LE
                    dve.wait_ge(h0_kept, s + 1)
                    need(dve, mv1_ready, s)
                    apart(dve)
                    for b in range(NB):
                        ins = nc.vector.bn_stats(stats1[:, b, :], by4(bank[1])[:, b, :])
                    ins.then_inc(stats1_done, 1)
                    dve.wait_ge(stats1_done, s + 1)
                    need(dve, var1e_ready, s)
                    apart(dve)
                    for b in range(NB):
                        ins = nc.vector.bn_aggr(mv1[:, b, :], stats1[:, b, :])
                    ins.then_inc(mv1_ready, 1)
                new_blocks(3)
                if on(j, LH):
                    s = j + LH
                    h = h1buf[:, :, bass.ds(s, 1), :].rearrange("p b s c -> p b (s c)")
                    dve.wait_ge(mv2_ready, s + 1)
                    kept = ln2[:, bass.ds(s, 1), :, :].rearrange("p s b m -> p (s b) m")
                    nc.vector.tensor_copy(kept[:, :, 0], mv2[:, :, 0])
                    dve.wait_ge(rstd2_ready, s + 1)
                    nc.vector.tensor_copy(kept[:, :, 1], rstd2[:, :]).then_inc(ln2_kept, 1)
                    need(dve, hnT_ps, s)
                    for b in range(NB):
                        ins = nc.vector.tensor_scalar(hn[:, b, :], h[:, b, :], mv2[:, b, 0:1], rstd2[:, b:b + 1],
                                                      ALU.subtract, ALU.mult)
                    ins.then_inc(hn_ready, 1)

                grow(3)
                if on(j, LF):
                    s = j + LF
                    dve.wait_ge(expo_ready, s + 1)
                    need(dve, ab_ready, s)
                    nc.vector.tensor_scalar(expo1[:, :], expo[:, :], 1.0, None, ALU.add).then_inc(expo1_ready, 1)
                    dve.wait_ge(expo1_ready, s + 1)
                    need(dve, g_ps, s)
                    nc.vector.reciprocal(ab[:, :], expo1[:, :]).then_inc(ab_ready, 1)
                new_blocks(4)
                grow(4)
                if on(j, LC):
                    s = j + LC
                    dve.wait_ge(pz_ps, s + 1)
                    dve.wait_ge(QMs_ready, s + 1)
                    need(dve, og_ready, s)
                    need(dve, so2_ready, s)
                    nc.vector.tensor_tensor(o, by4(bank[6]), QMs, ALU.add).then_inc(o_ready, 1)
                new_blocks(5)
                if on(j, LF):
                    s = j + LF
                    dve.wait_ge(kvg_ready, NB * (s + 1))
                    need(dve, vmean_ready, s)
                    nc.vector.tensor_reduce(vsum[:, :], kvg[p][:, :, D:2 * D], AX.X, ALU.add).then_inc(vsum_ready, 1)
                    dve.wait_ge(ssk_ready, s + 1)
                    need(dve, rk2_ready, s)
                    need(dve, knorm_ready, s)
                    nc.vector.tensor_scalar(kn2[:, :], ssk[:, :], 1e-24, None, ALU.max).then_inc(kn2_ready, 1)
                    dve.wait_ge(vsum_ready, s + 1)
                    need(dve, vt_ready, s)
                    nc.vector.tensor_scalar(vmean[:, :], vsum[:, :], 1.0 / D, None, ALU.mult).then_inc(vmean_ready, 1)
                    dve.wait_ge(kn2_ready, s + 1)
                    nc.vector.reciprocal(rk2[:, :], kn2[:, :]).then_inc(rk2_ready, 1)
                    dve.wait_ge(rk2_ready, s + 1)
                    need(dve, cdecay_ready, s)
                    nc.vector.scalar_tensor_tensor(cneg[:, :], rk2[:, :], -1.0, ab[:, 4:8], ALU.mult, ALU.mult).then_inc(cneg_ready, 1)
                if on(j, LF):
                    s = j + LF
                    dve.wait_ge(alpha_ps, s + 1)
                    need(dve, g_ps, s)
                    need(dve, cdecay_ready, s)
                    need(dve, glast_ready, s)
                    nc.vector.tensor_tensor_scan(decay.rearrange("p b c -> p (b c)"), bank[4][:, :],
                                                 ident4[:, :, :].rearrange("p b c -> p (b c)"), 0.0, ALU.mult, ALU.add).then_inc(decay_ready, 1)
                    dve.wait_ge(decay_ready, s + 1)
                    nc.vector.tensor_tensor(glast[:, :], decay[0:1, :, C - 1], ab[0:1, 0:4], ALU.mult).then_inc(glast_ready, 1)
                if on(j, LC):
                    s = j + LC
                    dve.wait_ge(so2_ready, s + 1)
                    need(dve, oscale_ready, s)
                    nc.vector.scalar_tensor_tensor(ovar[:, :], so2[:, :], 1.0 / D, qn2e[p][:, :], ALU.mult, ALU.add).then_inc(ovar_ready, 1)
                if on(j, LF):
                    s = j + LF
                    dve.wait_ge(qq_ps, s + 1)
                    need(dve, ovar_ready, s - 1)
                    nc.vector.tensor_scalar(qn2e[p][:, :], small_ps[:, 8:12], 1e-24, EPS, ALU.max, ALU.mult).then_inc(qn2_ready, 1)
                if on(j, LC):
                    s = j + LC
                    dve.wait_ge(dm_ps, s + 1)
                    for b in range(NB):
                        ins = nc.vector.scalar_tensor_tensor(state[:, b, :], state[:, b, :], gs[p][:, 4 + b:5 + b], by4(bank[5])[:, b, :],
                                                             ALU.mult, ALU.add)
                    ins.then_inc(state_ready, 1)
                if on(j, LF):
                    s = j + LF
                    dve.wait_ge(kk_ps, s + 1)
                    dve.wait_ge(cdecay_ready, s + 1)
                    need(dve, blk_ps_done, 6 * (s - 1))
                    nc.vector.tensor_tensor(Bm[p], by4(bank[4]), cdecay, ALU.mult).then_inc(B_ready, 1)
                    dve.wait_ge(B_ready, s + 1)
                    nc.vector.tensor_tensor(pairs, Bm[p][:, :, 1:C:2], ident4[:, :, 0:C:2], ALU.mult).then_inc(pairs_ready, 1)
                    dve.wait_ge(pairs_ready, s + 1)
                    need(dve, X_reset, s - 1)
                    nc.vector.tensor_tensor(X[p][:, :, 1:C:2], X[p][:, :, 1:C:2], pairs, ALU.add).then_inc(X_ready, 1)
                    dve.wait_ge(X_ready, 5 * s + 1)
                    nc.vector.transpose(Y[p].rearrange("p b c -> p (b c)"), X[p].rearrange("p b c -> p (b c)")).then_inc(Y_ready, 1)
                new_blocks(6)
                if on(j, LC):
                    s = j + LC
                    dve.wait_ge(oscale_ready, s + 1)
                    dve.wait_ge(gate_ready, s + 1)
                    need(dve, ogT_ps, s)
                    for b in range(NB):
                        ins = nc.vector.scalar_tensor_tensor(og[:, b, :], o[:, b, :], oscale[:, b:b + 1], gate_kept[:, b, :],
                                                             ALU.mult, ALU.mult)
                    ins.then_inc(og_ready, 1)
                if on(j, LE):
                    s = j + LE
                    dve.wait_ge(rb_ps, s + 1)
                    dve.wait_ge(xt_ready, s + 1)
                    need(dve, q_ps, s - 1)
                    need(dve, hist_ready, s)
                    nc.vector.tensor_tensor(xs[par][0:KX, :, HIST:XW], by4(bank[1])[0:KX], xt[par][0:KX, :, :],
                                            ALU.mult).then_inc(xs_ready, 1)
                if on(j, LF):
                    s = j + LF
                    dve.wait_ge(kq_ps, s + 1)
                    need(dve, pz_ps, s - 1)
                    nc.vector.tensor_tensor(Pm[p], by4(bank[3]), cdecay, ALU.mult).then_inc(P_ready, 1)
                    need(dve, dm_ps, s - 1)
                    for b in range(NB):
                        ins = nc.vector.tensor_scalar(kd[p][:, b, :], kvg[p][:, b, 0:D], cdecay[:, b, C - 1:C], None, ALU.mult)
                    ins.then_inc(kd_ready, 1)
                    dve.wait_ge(knorm_ready, s + 1)
                    dve.wait_ge(vmean_ready, s + 1)
                    need(dve, Rn_ready, s - 1)
                    for b in range(NB):
                        ins = nc.vector.tensor_scalar(vt[p][:, b, :], kvg[p][:, b, D:2 * D], vmean[:, b:b + 1], knorm[:, b:b + 1],
                                                      ALU.subtract, ALU.mult)
                    ins.then_inc(vt_ready, 1)
                    dve.wait_ge(g_ps, s + 1)
                    need(dve, state_ready, s - 1)
                    need(dve, QMs_ready, s - 1)
                    nc.vector.tensor_copy(gs[p][:, :], small_ps[:, 16:24]).then_inc(gs_ready, 1)

            iterations(dve, body)
            ffn["vector"](dve)

        @block.tensor
        def _(pe):
            mm = nc.tensor.matmul
            tr = nc.tensor.transpose
            pe.wait_ge(con, 2)
            pe.wait_ge(pro_dve, 4)
            tr(bank[3][:, 0:D], Wc, ident[:, :]).then_inc(pro_pe, 1)
            pe.wait_ge(pro_dve, 8)
            mm(bank[5][:, :], WcT, rhs_all[:, 0:512], start=True, stop=False)
            mm(bank[5][:, :], onehot2, bias_row[:, 0:512], start=False, stop=True)
            mm(bank[6][:, 0:2], WcT, rhs_all[:, 512:514], start=True, stop=False)
            mm(bank[6][:, 0:2], onehot2, bias_row[:, 512:514], start=False, stop=True).then_inc(pro_pe, 1)
            mm(bank[0][:, 0:384], selA, cwT, start=True, stop=True)
            mm(bank[1][:, 0:384], selB, cwT, start=True, stop=True)
            mm(bank[2][:, 0:384], onehot1, cb_row[:, 0:384], start=True, stop=True).then_inc(pro_pe, 1)
            pe.wait_ge(pro_dve, DVE_PRO)
            pe.wait_ge(con, 2 + 2 * LEVELS)

            def body(j, par):
                p = 1 - par
                F_, I_, C_, H_, E_ = on(j, LF), on(j, LI), on(j, LC), on(j, LH), on(j, LE)
                s1, s0, c, h, e = j + LF, j + LI, j + LC, j + LH, j + LE

                def level_blocks(k):
                    if not I_:
                        return
                    if k <= 5:
                        pe.wait_ge(Y_ready, 5 * s0 + k)
                    else:
                        pe.wait_ge(Y5_ready, s0 + 1)
                    need(pe, blk_ready, 6 * s0 + k - 1)
                    if k >= 5:
                        apart(pe)
                    for b in range(NB):
                        if k < 5:
                            ins = mm(by64(blk_ps)[:, b], Bm[par][:, b, :], half(Y[par], b, k, 0), start=True, stop=True)
                        elif k == 5:
                            for r in (0, 64):
                                ins = mm(by32(blk_ps)[r + 32:r + 64, b], Bm[par][r:r + 32, b, r + 32:r + 64],
                                         Y[par][r:r + 32, b, r:r + 32], start=True, stop=True)
                        else:
                            ins = mm(by64(blk_ps)[64:128, b], Bm[par][0:64, b, 64:128], Y[par][0:64, b, 0:64], start=True, stop=True)
                    ins.then_inc(blk_ps_done, 1)

                def level_update(k):
                    if not I_:
                        return
                    pe.wait_ge(blk_ready, 6 * s0 + k)
                    if k == 6:
                        pe.wait_ge(X5_ready, s0 + 1)
                    if k >= 5:
                        apart(pe)
                    if k == 5:
                        for b in range(NB):
                            for r in (0, 64):
                                ins = mm(by32(bank[1])[r + 32:r + 64, b], X[par][r + 32:r + 64, b, r + 32:r + 64],
                                         N5[r + 32:r + 64, b, :], start=True, stop=True)
                        ins.then_inc(Y5ps_done, 1)
                    if k == 1:
                        need(pe, X6_ready, s0)
                    for b in range(NB):
                        if k < 5:
                            ins = mm(by64(X_ps)[:, b], newblk[k][:, b, :], half(X[par], b, k, 1), start=True, stop=True)
                        elif k == 5:
                            for r in (0, 64):
                                ins = mm(by32(X_ps)[r:r + 32, b], N5[r + 32:r + 64, b, :],
                                         X[par][r + 32:r + 64, b, r + 32:r + 64], start=True, stop=True)
                        else:
                            ins = mm(by64(X_ps)[0:64, b], N6[64:128, b, :], X[par][64:128, b, 64:128], start=True, stop=True)
                    ins.then_inc(Xps_done, 1)

                def kvg_rows(b):
                    t = bank[4 - b % 2]
                    mm(t[:, 0:386], xs[p][:, b, HIST:XW], SA[:, 0:386], start=True, stop=False)
                    mm(t[:, 0:256], xs[p][:, b, 1:1 + C], SB[:, 0:256], start=False, stop=True).then_inc(kvg_ps, 1)

                level_blocks(1)
                if C_:
                    need(pe, state_ready, c)
                    need(pe, ogT_ready, c)
                    for b in range(NB):
                        ins = mm(by4(bank[5])[:, b, :], kT[p][:, b, :], state[:, b, :], start=True, stop=True)
                    ins.then_inc(km_ps, 1)
                level_update(1)
                if F_:
                    pe.wait_ge(xs_ready, s1 + 1)
                    pe.wait_ge(xs_shifted, s1 + 1)
                    need(pe, B_ready, s1)
                    kvg_rows(0)
                    need(pe, P_ready, s1)
                    kvg_rows(1)
                level_blocks(2)
                if C_:
                    pe.wait_ge(Rn_ready, c + 1)
                    pe.wait_ge(X6_ready, c + 1)
                    for b in range(NB):
                        ins = mm(by4(bank[5])[:, b, :], X[p][:, b, :], Rn[:, b, :], start=True, stop=True)
                    ins.then_inc(z_ps, 1)
                level_update(2)
                if E_:
                    pe.wait_ge(xt_ready, e + 1)
                    need(pe, xs_ready, e)
                    for b in range(NB):
                        ins = mm(by4(bank[1])[:, b, :], xt[par][0:KX, b, :], We[0:KX, :], start=True, stop=True)
                    ins.then_inc(h0_ps, 1)
                if F_:
                    pe.wait_ge(kvg_ready, NB * s1 + 1)
                    kvg_rows(2)
                level_blocks(3)
                if C_:
                    need(pe, h1_ready, c)
                    for b in range(NB):
                        ins = mm(by4(bank[6])[:, b, :], qT[p][:, b, :], state[:, b, :], start=True, stop=True)
                    ins.then_inc(qm_ps, 1)
                level_update(3)
                if F_:
                    pe.wait_ge(kvg_ready, NB * s1 + 2)
                    kvg_rows(3)
                if F_:
                    pe.wait_ge(kvg_ready, NB * s1 + 3)
                    mm(bank[4][:, :], SA[:, 386:514], xs[p][:, :, HIST:XW], start=True, stop=False)
                    mm(bank[4][:, :], SB[:, 384:512], xs[p][:, :, 1:1 + C], start=False, stop=True).then_inc(q_ps, 1)
                level_blocks(4)
                if C_:
                    pe.wait_ge(Zn_ready, c + 1)
                    pe.wait_ge(QMs_ready, c + 1)
                    for b in range(NB):
                        ins = mm(by4(bank[6])[:, b, :], Pm[p][:, b, :], Zn[:, b, :], start=True, stop=True)
                    ins.then_inc(pz_ps, 1)
                level_update(4)
                if C_:
                    for b in range(NB):
                        ins = mm(by4(bank[5])[:, b, :], kd[p][:, b, :], Zn[:, b, :], start=True, stop=True)
                    ins.then_inc(dm_ps, 1)
                if F_:
                    pe.wait_ge(kvg_ready, NB * s1 + 4)
                    for b in range(NB):
                        ins = tr(by4(bank[3])[:, b, :], kvg[p][:, b, 0:D], ident[:, :])
                    ins.then_inc(kT_ps, 1)
                if F_:
                    pe.wait_ge(ab_ready, s1 + 1)
                    pe.wait_ge(qT_ready, s1 + 1)
                    for b in range(NB):
                        ins = mm(by4(bank[4])[:, b, :], ab[:, b:b + 1].broadcast_to([D, D]), ident0[:, :], start=True, stop=True)
                    ins.then_inc(alpha_ps, 1)
                level_blocks(5)
                if H_:
                    pe.wait_ge(hn_ready, h + 1)
                    if C_:
                        pe.wait_ge(o_ready, c + 1)
                    for b in range(NB):
                        ins = tr(by4(bank[6])[:, b, :], hn[:, b, :], ident[:, :])
                    ins.then_inc(hnT_ps, 1)
                if F_:
                    pe.wait_ge(sqq_ready, s1 + 1)
                    need(pe, gs_ready, s1)
                    for b in range(NB):
                        ins = mm(small_ps[:, 8 + b:9 + b], sq_q[:, b, :], ones[:, 0:1], start=True, stop=True)
                    ins.then_inc(qq_ps, 1)
                level_update(5)
                if F_:
                    pe.wait_ge(kT_ready, s1 + 1)
                    pe.wait_ge(decay_ready, s1 + 1)
                    for b in range(NB):
                        ins = mm(by4(bank[4])[:, b, :], kT[p][:, b, :], kT[p][:, b, :], start=True, stop=True)
                    ins.then_inc(kk_ps, 1)
                if F_:
                    for b in range(NB):
                        ins = mm(by4(bank[3])[:, b, :], kT[p][:, b, :], qT[p][:, b, :], start=True, stop=True)
                    ins.then_inc(kq_ps, 1)
                level_blocks(6)
                if H_:
                    pe.wait_ge(hnT_ready, h + 1)
                    if C_:
                        pe.wait_ge(state_ready, c + 1)
                    mm(bank[5][:, :], gfc1_T[:, :], hnT.rearrange("p b c -> p (b c)"), start=True, stop=True).then_inc(gf_ps, 1)
                if F_:
                    pe.wait_ge(glast_ready, s1 + 1)
                    pe.wait_ge(qn2_ready, s1 + 1)
                    for b in range(NB):
                        mm(small_ps[:, 16 + b:17 + b], decay[0:1, b, :], ab[0:1, b:b + 1], start=True, stop=True)
                    mm(small_ps[:, 20:24], ones[0:1, :], glast[:, :], start=True, stop=True).then_inc(g_ps, 1)
                level_update(6)
                if E_:
                    pe.wait_ge(rmat_ready, e + 1)
                    need(pe, Y5_ready, s0 + 1)
                    for b in range(NB):
                        ins = mm(by4(bank[1])[0:KX, b, :], rmat[:, b, :], ident[:, :], start=True, stop=True)
                    ins.then_inc(rb_ps, 1)
                if C_:
                    pe.wait_ge(og_ready, c + 1)
                    pe.wait_ge(state_ready, c + 1)
                    need(pe, relu_ready, h + 1)
                    for b in range(NB):
                        ins = tr(by4(bank[5])[:, b, :], og[:, b, :], ident[:, :])
                    ins.then_inc(ogT_ps, 1)
                if C_:
                    pe.wait_ge(ogT_ready, c + 1)
                    need(pe, hnT_ready, h + 1)
                    pe.wait_ge(o_ready, c + 1)
                    for b in range(NB):
                        ins = mm(by4(bank[6])[:, b, :], ogT[:, b, :], Wo_T[:, :], start=True, stop=True)
                    ins.then_inc(wo_ps, 1)

            iterations(pe, body)
            ffn["tensor"](pe)


def make_ffn(nc, ctx, sb, sem, work, A):
    bank, h1buf, ln2, ident, ones = A["bank"], A["h1buf"], A["ln2"], A["ident"], A["ones"]
    gate_sum, by4 = A["gate_sum"], A["by4"]
    W1, b1, W2, b2, out = A["W1"], A["b1"], A["W2"], A["b2"], A["out"]
    tv_W1, tv_b1, tv_W2, tv_b2 = A["tv_W1"], A["tv_b1"], A["tv_W2"], A["tv_b2"]

    at = [0]

    def tile(*shape):
        n = 1
        for k in shape:
            n *= k
        t = work[:, at[0]:at[0] + n]
        at[0] += n
        if len(shape) == 2:
            t = t.rearrange("p (a c) -> p a c", a=shape[0])
        if len(shape) == 3:
            t = t.rearrange("p (a b c) -> p a b c", a=shape[0], b=shape[1])
        return t

    w1T = [tile(FB, D) for _ in range(2)]
    w2T = [tile(FB, D) for _ in range(2)]
    b2mix = tile(NB, D)
    ghT = [tile(GROUP, C) for _ in range(2)]
    hid = [tile(GROUP * C) for _ in range(FB)]
    fhn = [tile(GROUP, D) for _ in range(2)]
    fhnb = [tile(GROUP, D) for _ in range(2)]
    res = tile(GROUP, D)
    nrm = tile(GROUP, D)
    y = [tile(GROUP, D) for _ in range(2)]
    assert at[0] <= A["attention_end"] - 2 * NB * D
    tv1 = sb("tv1", [D, NE, FB, D])
    tv2 = sb("tv2", [D, NE, FB, D])
    w1nat = sb("w1nat", [D, FB, D])
    w2nat = sb("w2nat", [D, FB, D])
    tvb1 = sb("tvb1", [NE, F])
    tvb2 = sb("tvb2", [NE, D])
    tvln = sb("tvln", [NE, 2, D])
    ln_rows = sb("ln_rows", [1, 3, D])
    merge_w = sb("merge_w", [NE, 2, D])
    lng_lnb = sb("lng_lnb", [D, 2, D])
    lng, lnb = lng_lnb[:, 0, :], lng_lnb[:, 1, :]
    b1nat = sb("b1nat", [D, FB])
    b1mix = sb("b1mix", [D, NB, FB])
    gh = sb("gh", [D, NB])
    ghm = sb("ghm", [D, NB])
    gfc2T = sb("gfc2T", [D, NE])
    gfc2b = sb("gfc2b", [D, NE])
    gfc2b_col = sb("gfc2b_col", [NE, 1])
    g_all = sb("g_all", [D, NB, NE])
    g_T = sb("g_T", [NE, NB])
    fst = sb("fst", [D, GROUP, 6])
    fmv = sb("fmv", [D, GROUP, 2])
    fve = sb("fve", [D, GROUP])
    frs = sb("frs", [D, GROUP])
    half_neg = A["half_neg"]

    fw_in = sem("fw_in")
    merge_set = sem("merge_set")
    ln_ps = sem("ln_ps")
    ln_ready = sem("ln_ready")
    gh_sum = sem("gh_sum")
    gh_ready = sem("gh_ready")
    g_ps2 = sem("g_ps2")
    g_ready = sem("g_ready")
    bias_ps = sem("bias_ps")
    mix_step = sem("mix_step")
    b1_ready = sem("b1_ready")
    b2_ready = sem("b2_ready")
    fhn_ready = sem("fhn_ready")
    fhnb_ready = sem("fhnb_ready")
    fhT_ps = sem("fhT_ps")
    fhT_ready = sem("fhT_ready")
    hid_ps = sem("hid_ps")
    hid_ready = sem("hid_ready")
    out_ps = sem("out_ps")
    res_ready = sem("res_ready")
    fst_done = sem("fst_done")
    fmv_ready = sem("fmv_ready")
    fve_ready = sem("fve_ready")
    frs_ready = sem("frs_ready")
    nrm_ready = sem("nrm_ready")
    y1 = sem("y1")
    y2 = sem("y2")
    y_ready = sem("y_ready")
    y_out = [sem("y_out0"), sem("y_out1")]

    def row1(v):
        return v.rearrange("(a n) -> a n", a=1)

    def row(v):
        return v.partition_broadcast(D)

    loads = [
        (tvln[:, 0, :], A["tv_ln_g"][:, :]), (tvln[:, 1, :], A["tv_ln_b"][:, :]),
        (ln_rows[:, 0, :], row1(A["ln_g"])), (ln_rows[:, 1, :], row1(A["ln_b"])), (ln_rows[:, 2, :], row1(b2)),
        (gfc2T[:, :], A["gfc2_wT"][:, :]), (gfc2b[:, :], row(A["gfc2_b"])),
        (gfc2b_col[:, :], A["gfc2_b"].rearrange("(p a) -> p a", a=1)),
        (w1nat[:, :, :].rearrange("p a c -> p (a c)"), W1[:, :]), (w2nat[:, :, :], W2.rearrange("(a p) d -> p a d", p=D)),
        (b1nat[:, :], b1[:, :]), (tvb1[:, :], tv_b1[:, :]), (tvb2[:, :], tv_b2[:, :]),
    ]
    loads += [(tv1[:, e].rearrange("p a c -> p (a c)"), tv_W1[e]) for e in range(NE)]
    loads += [(tv2[:, e], tv_W2[e].rearrange("(a p) d -> p a d", p=D)) for e in range(NE)]
    LOADED = 16 * len(loads)

    def units(engine, body, image_start=None):
        for b in range(NB):
            if image_start is not None:
                image_start(b)
            u0, par = b * UNITS, b % 2
            start = 0
            if b == 0:
                body(0, 0, 0, 0, GROUP, (0, 1, GROUP))
                body(0, 1, 1, 1, GROUP, (0, 2, GROUP))
                start = 2
            with engine.Fori(start, GROUPS - 3, 2) as g:
                body(b, g, u0 + g, par, GROUP, (b, g + 1, GROUP))
                body(b, g + 1, u0 + g + 1, 1 - par, GROUP, (b, g + 2, GROUP))
            body(b, GROUPS - 2, u0 + GROUPS - 2, par, GROUP, (b, GROUPS - 1, GROUP))
            body(b, GROUPS - 1, u0 + GROUPS - 1, 1 - par, GROUP, (b, GROUPS, 1))
            body(b, GROUPS, u0 + GROUPS, par, 1, (b + 1, 0, GROUP) if b + 1 < NB else None)

    def load(sp):
        for dst, src in loads:
            sp.dma_start(dst, src).then_inc(fw_in, 16)

    def sync(sp):
        def body(b, g, u, par, n, nxt):
            sp.wait_ge(y_ready, u + 1)
            if n == GROUP:
                dst = out[b, bass.ds(g * (GROUP * C), GROUP * C), :].rearrange("(t p) d -> p t d", p=C)
                sp.dma_start(dst, y[par][:, :, :]).then_inc(y_out[par], 16)
            else:
                sp.dma_start(out[b, (STEPS - 1) * C:TOK, :], y[par][0:LAST, 0, :]).then_inc(y_out[par], 16)
        units(sp, body)
        sp.wait_ge(y_out[0], 16 * (NB * UNITS // 2))
        sp.wait_ge(y_out[1], 16 * (NB * UNITS // 2))

    def vector_early(dve):
        nc.vector.memset(merge_w[:, 0, :], LN_MERGE)
        nc.vector.memset(merge_w[0:1, 1, :], 1.0 - NE * LN_MERGE).then_inc(merge_set, 1)

    def tensor_early(pe):
        pe.wait_ge(merge_set, 1)
        pe.wait_ge(fw_in, LOADED)
        for i in range(2):
            t = bank[4][:, i * D:(i + 1) * D]
            nc.tensor.matmul(t, merge_w[:, 0, :], tvln[:, i, :], start=True, stop=False)
            ins = nc.tensor.matmul(t, merge_w[0:1, 1, :], ln_rows[:, i, :], start=False, stop=True)
        ins.then_inc(ln_ps, 1)

    def mix(dve, b, e, first):
        n = 2 * NE * b + (0 if first else 2 * e + 2)
        if first:
            if b >= 2:
                dve.wait_ge(out_ps, UNITS * (b - 1))
        else:
            dve.wait_ge(mix_step, n)
        ex = bass.ds(e, 1)
        for t, tv, nat in ((w1T[b % 2], tv1, w1nat), (w2T[b % 2], tv2, w2nat)):
            nc.vector.scalar_tensor_tensor(t.rearrange("p a c -> p (a c)"), tv[:, ex, :, :].rearrange("p e a c -> p (e a c)"),
                                           g_all[:, b, ex], (nat[:, :, :] if first else t).rearrange("p a c -> p (a c)"),
                                           ALU.mult, ALU.add).then_inc(mix_step, 1)

    def vector(dve):
        def normed(b, g, u, par, n):
            need(dve, fhT_ps, u - 1)
            need(dve, fhnb_ready, u - 1)
            for t in range(n):
                s = g * GROUP + t
                st = ln2[:, bass.ds(s, 1), b, :].rearrange("p s m -> p (s m)")
                ins = nc.vector.tensor_scalar(fhn[par][:, t, :], h1buf[:, b, bass.ds(s, 1), :].rearrange("p s c -> p (s c)"),
                                              st[:, 0:1], st[:, 1:2], ALU.subtract, ALU.mult)
            ins.then_inc(fhn_ready, 1)

        dve.wait_ge(A["gate_summed"], STEPS)
        nc.vector.tensor_reduce(gh[:, :], gate_sum, AX.X, ALU.add).then_inc(gh_sum, 1)
        dve.wait_ge(gh_sum, 1)
        nc.vector.tensor_scalar(ghm[:, :], gh[:, :], 1.0 / TOK, None, ALU.mult).then_inc(gh_ready, 1)
        dve.wait_ge(A["og_ready"], STEPS)
        dve.wait_ge(A["ln2_kept"], STEPS)
        normed(0, 0, 0, 0, GROUP)
        dve.wait_ge(g_ps2, 1)
        dve.wait_ge(fw_in, LOADED)
        nc.vector.tensor_tensor(g_all[:, :, :], bank[0][:, 0:NB * NE].rearrange("p (b e) -> p b e", b=NB),
                                gfc2b[:, :].unsqueeze(1).broadcast_to([D, NB, NE]), ALU.add)
        nc.vector.tensor_scalar(g_T[:, :], bank[0][0:NE, 64:64 + NB], gfc2b_col[:, :], None, ALU.add).then_inc(g_ready, 1)
        dve.wait_ge(g_ready, 1)
        mix(dve, 0, NE - 1, True)
        for e in range(NE - 1):
            mix(dve, 0, e, False)
        dve.wait_ge(bias_ps, 1)
        nc.vector.tensor_tensor(b1mix[:, :, :], bank[6][:, 0:NB * FB].rearrange("p (f b) -> p b f", b=NB),
                                b1nat[:, :].unsqueeze(1).broadcast_to([D, NB, FB]), ALU.add).then_inc(b1_ready, 1)
        nc.vector.tensor_copy(b2mix, by4(bank[7])).then_inc(b2_ready, 1)

        def image_start(b):
            if b + 1 < NB:
                mix(dve, b + 1, NE - 1, True)

        def body(b, g, u, par, n, nxt):
            if nxt is not None:
                normed(nxt[0], nxt[1], u + 1, 1 - par, nxt[2])
            if b + 1 < NB:
                mix(dve, b + 1, g, False)
            dve.wait_ge(out_ps, u + 1)
            dve.wait_ge(fhnb_ready, u + 1)
            nc.vector.tensor_tensor(res[:, 0:n, :], by4(bank[2])[:, 0:n, :], fhnb[par][:, 0:n, :], ALU.add).then_inc(res_ready, 1)
            dve.wait_ge(res_ready, u + 1)
            for t in range(n):
                ins = nc.vector.bn_stats(fst[:, t, :], res[:, t, :])
            ins.then_inc(fst_done, 1)
            dve.wait_ge(fst_done, u + 1)
            apart(dve)
            for t in range(n):
                ins = nc.vector.bn_aggr(fmv[:, t, :], fst[:, t, :])
            ins.then_inc(fmv_ready, 1)
            dve.wait_ge(frs_ready, u + 1)
            need(dve, y1, u)
            for t in range(n):
                ins = nc.vector.tensor_scalar(nrm[:, t, :], res[:, t, :], fmv[:, t, 0:1], frs[:, t:t + 1], ALU.subtract, ALU.mult)
            ins.then_inc(nrm_ready, 1)

        units(dve, body, image_start)

    def scalar(act):
        act.wait_ge(ln_ps, 1)
        nc.scalar.copy(lng_lnb[:, :, :], bank[4][:, 0:2 * D].rearrange("p (a c) -> p a c", a=2)).then_inc(ln_ready, 1)
        act.wait_ge(A["gate_summed"], STEPS)
        act.wait_ge(A["wo_ps"], STEPS)

        def cols_out(u, par, n):
            act.wait_ge(fhT_ps, u + 1)
            need(act, hid_ps, FB * (u - 1))
            nc.scalar.copy(ghT[par][:, 0:n, :], by4(bank[3])[:, 0:n, :]).then_inc(fhT_ready, 1)

        cols_out(0, 0, GROUP)
        act.wait_ge(b1_ready, 1)

        def body(b, g, u, par, n, nxt):
            for f in range(FB):
                act.wait_ge(hid_ps, FB * u + f + 1)
                if f == 0:
                    need(act, out_ps, u)
                nc.scalar.activation(hid[f][:, 0:n * C], bank[(0, 1, 4, 5)[f]][:, 0:n * C], ACT.Relu, bias=b1mix[:, b, f:f + 1]).then_inc(hid_ready, 1)
            if nxt is not None:
                cols_out(u + 1, 1 - par, nxt[2])

        units(act, body)

    def gpsimd(pool):
        pool.wait_ge(b2_ready, 1)
        pool.wait_ge(ln_ready, 1)

        def body(b, g, u, par, n, nxt):
            pool.wait_ge(fhn_ready, u + 1)
            need(pool, res_ready, u - 1)
            nc.gpsimd.tensor_tensor(fhnb[par][:, 0:n, :], fhn[par][:, 0:n, :], b2mix[:, b, :].unsqueeze(1).broadcast_to([D, n, D]), ALU.add).then_inc(fhnb_ready, 1)
            pool.wait_ge(fmv_ready, u + 1)
            apart(pool)
            nc.gpsimd.tensor_scalar(fve[:, 0:n], fmv[:, 0:n, 1], EPS, None, ALU.add).then_inc(fve_ready, 1)
            pool.wait_ge(fve_ready, u + 1)
            need(pool, nrm_ready, u)
            nc.gpsimd.tensor_tensor(frs[:, 0:n], fve[:, 0:n], half_neg[:, 0:n], ALU.pow).then_inc(frs_ready, 1)
            pool.wait_ge(nrm_ready, u + 1)
            need(pool, y_out[par], (u - par) * 8)
            nc.gpsimd.tensor_tensor(y[par][:, 0:n, :], nrm[:, 0:n, :], lng.unsqueeze(1).broadcast_to([D, n, D]), ALU.mult).then_inc(y1, 1)
            pool.wait_ge(y1, u + 1)
            nc.gpsimd.tensor_tensor(y[par][:, 0:n, :], y[par][:, 0:n, :], lnb.unsqueeze(1).broadcast_to([D, n, D]), ALU.add).then_inc(y2, 1)
            pool.wait_ge(y2, u + 1)
            apart(pool)
            nc.gpsimd.tensor_tensor(y[par][:, 0:n, :], y[par][:, 0:n, :], h1buf[:, b, bass.ds(g * GROUP, n), :], ALU.add).then_inc(y_ready, 1)

        units(pool, body)

    def tensor(pe):
        mm, tr = nc.tensor.matmul, nc.tensor.transpose

        def to_cols(u, par, n):
            pe.wait_ge(fhn_ready, u + 1)
            need(pe, fhT_ready, u)
            for t in range(n):
                ins = tr(by4(bank[3])[:, t, :], fhn[par][:, t, :], ident[:, :])
            ins.then_inc(fhT_ps, 1)

        tensor_early(pe)
        pe.wait_ge(gh_ready, 1)
        for b in range(NB):
            mm(bank[0][:, b * NE:(b + 1) * NE], ghm[:, b:b + 1].broadcast_to([D, D]), gfc2T[:, :], start=True, stop=True)
        mm(bank[0][0:NE, 64:64 + NB], gfc2T[:, :], ghm[:, :], start=True, stop=True).then_inc(g_ps2, 1)
        to_cols(0, 0, GROUP)
        pe.wait_ge(g_ready, 1)
        for f in range(FB):
            mm(bank[6][:, f * NB:(f + 1) * NB], tvb1[:, f * D:(f + 1) * D], g_T[:, :], start=True, stop=True)
        for b in range(NB):
            mm(by4(bank[7])[:, b, :], g_T[:, b:b + 1].broadcast_to([NE, D]), tvb2[:, :], start=True, stop=False)
            ins = mm(by4(bank[7])[:, b, :], ones[0:1, :], ln_rows[:, 2, :], start=False, stop=True)
        ins.then_inc(bias_ps, 1)

        pe.wait_ge(ln_ready, 1)

        def body(b, g, u, par, n, nxt):
            pe.wait_ge(fhT_ready, u + 1)
            w1, w2 = w1T[b % 2], w2T[b % 2]

            def hidden(f):
                need(pe, hid_ready, FB * (u - 1) + f + 1)
                mm(bank[(0, 1, 4, 5)[f]][:, 0:n * C], w1[:, f, :], ghT[par][:, 0:n, :].rearrange("p t c -> p (t c)"), start=True, stop=True).then_inc(hid_ps, 1)

            def project(f):
                pe.wait_ge(hid_ready, FB * u + f + 1)
                if f == 0:
                    need(pe, res_ready, u)
                for t in range(n):
                    ins = mm(by4(bank[2])[:, t, :], hid[f][:, t * C:(t + 1) * C], w2[:, f, :], start=(f == 0 and t == 0),
                             stop=(f == FB - 1), skip_group_check=True)
                if f == FB - 1:
                    ins.then_inc(out_ps, 1)

            for f in range(FB):
                hidden(f)
            project(0)
            project(1)
            if nxt is not None:
                to_cols(u + 1, 1 - par, nxt[2])
            project(2)
            project(3)

        units(pe, body, lambda b: pe.wait_ge(mix_step, 2 * NE * (b + 1)))

    return {"sync": sync, "vector": vector, "scalar": scalar, "gpsimd": gpsimd, "tensor": tensor,
            "load": load, "vector_early": vector_early}


_INS = ['x'] + ['L0_tok_' + n for n in ('W', 'b', 'cls')] + ['L0_attn_' + n for n in (
    'Wq', 'bq', 'Wk', 'bk', 'Wv', 'bv', 'Wa', 'ba', 'Wb', 'bb', 'cwq', 'cbq', 'cwk', 'cbk', 'cwv', 'cbv', 'norm_w',
    'Wg', 'bg', 'Wo', 'bo')] + ['L0_ffn_' + n for n in (
        'gfc1_w', 'gfc1_b', 'gfc2_w', 'gfc2_b', 'W1', 'b1', 'W2', 'b2', 'ln_g', 'ln_b', 'tv_W1', 'tv_b1', 'tv_W2',
        'tv_b2', 'tv_ln_g', 'tv_ln_b')]
_TRANSPOSED = ['L0_tok_W'] + ['L0_attn_' + n for n in ('Wq', 'Wk', 'Wv', 'Wa', 'Wb', 'Wg', 'Wo')] + [
    'L0_ffn_gfc1_w', 'L0_ffn_gfc2_w', 'L0_ffn_W1', 'L0_ffn_W2']


def kernel(**inputs):
    import numpy as _np
    import concourse.bacc as _bacc
    from concourse import mybir as _mybir
    from concourse.bass_utils import run_bass_kernel_spmd as _run

    nc = _bacc.Bacc("TRN2", target_bir_lowering=False, num_devices=1)
    arrays, args = {}, []
    for name in _INS:
        a = _np.asarray(inputs[name])
        if name == 'x':
            a = a.reshape(NB, 3, GRID, PATCH, GRID, PATCH).transpose(1, 3, 5, 0, 2, 4).reshape(PIX, NB, GRID * GRID)
        elif name in _TRANSPOSED:
            a = a.T
        elif name in ('L0_ffn_tv_W1', 'L0_ffn_tv_W2'):
            a = a.transpose(0, 2, 1)
        elif name.startswith('L0_attn_cw'):
            a = a.reshape(D, TAPS).T
        elif name == 'L0_ffn_b1':
            a = a.reshape(FB, D).T
        a = _np.ascontiguousarray(a)
        arrays[f"in_{name}_dram"] = a
        args.append(nc.dram_tensor(f"in_{name}_dram", a.shape, _mybir.dt.from_np(a.dtype), kind="ExternalInput").ap())
    args.append(nc.dram_tensor("out_0_dram", (NB, TOK, D), _mybir.dt.float32, kind="ExternalOutput").ap())
    vit_tower(nc, *args)
    r = _run(nc, [arrays], core_ids=[0])
    return r.results[0]["out_0_dram"]
```

```python
import concourse.bass as bass
from concourse import mybir
from contextlib import ExitStack

F32 = mybir.dt.float32
ALU = mybir.AluOpType
ACT = mybir.ActivationFunctionType
AX = mybir.AxisListType

NB = 4
IMG, PATCH = 224, 4
GRID = IMG // PATCH
TOK = GRID * GRID + 1
D = 128
C = 128
STEPS = -(-TOK // C)
LAST = TOK - C * (STEPS - 1)
PIX = 3 * PATCH * PATCH
KX = PIX + 3
TAPS = 4
HIST = TAPS - 1
MASKED = (1, 2, 3, 4)
EPS = 1e-5
F = 512
FB = F // D
NE = 8
LN_MERGE = 0.03
GROUP = 4
GROUPS = STEPS // GROUP
UNITS = GROUPS + 1


def need(engine, semaphore, value):
    if not isinstance(value, int) or value > 0:
        engine.wait_ge(semaphore, value)


def apart(engine):
    engine.nop(nofuse=True)


def vit_tower(nc, x, tok_WT, tok_b, tok_cls, projections, biases, taps_kvq, norm_w, WoT, bo, gfc1_wT, gfc1_b, gfc2_wT, gfc2_b, W1, b1, W2, b2, ln_g, ln_b,
              tv_W1, tv_b1, tv_W2, tv_b2, tv_ln_g, tv_ln_b, out):
    ctx = ExitStack()
    with ctx:
        def sb(name, shape, dt=F32):
            return ctx.enter_context(nc.sbuf_tensor(name, shape, dt))

        def sem(name):
            return ctx.enter_context(nc.semaphore(name))

        ident = sb("ident", [D, D])
        ident4 = sb("ident4", [D, NB, D])
        not_first = sb("not_first", [D, NB])
        masks = sb("masks", [D, len(MASKED), D // 2])
        mask_x = sb("mask_x", [D, KX])
        mask_1 = sb("mask_1", [D, KX])
        ones = sb("ones", [D, D])
        half_neg = sb("half_neg", [D, 4])
        half_pos = sb("half_pos", [D, 4])
        euler = sb("euler", [D, 8])

        We = sb("We", [D, D])
        SA = sb("SA", [D, 516])
        SB = sb("SB", [D, 512])
        Wo_T = sb("Wo_T", [D, D])
        gfc1_T = sb("gfc1_T", [D, D])
        gfc1_bc = sb("gfc1_bc", [D, 1])
        bo_rows = sb("bo_rows", [D, D])

        h1buf = sb("h1buf", [D, NB, STEPS, C])
        xc = h1buf[0:KX, :, :, :].rearrange("p b s c -> p b (s c)")
        ln2 = sb("ln2", [D, STEPS, NB, 2])

        work = sb("work", [D, 25420])
        offset = [0]

        def tile(n, *shape):
            at = offset[0]
            offset[0] += n
            t = work[:, at:at + n]
            if len(shape) == 2:
                return t.rearrange("p (a c) -> p a c", a=shape[0])
            if len(shape) == 3:
                return t.rearrange("p (a b c) -> p a b c", a=shape[0], b=shape[1])
            return t

        xt = [tile(NB * C, NB, C) for _ in range(2)]
        XW = HIST + C
        xs = [tile(NB * XW, NB, XW) for _ in range(2)]
        rmat = tile(NB * KX, NB, KX)
        prologue_start = offset[0]
        kvg = [tile(NB * 3 * D, NB, 3 * D) for _ in range(2)]
        gate_kept = tile(NB * D, NB, D)
        kT = [tile(NB * D, NB, D) for _ in range(2)]
        qT = [tile(NB * D, NB, D) for _ in range(2)]
        decay = tile(NB * C, NB, C)
        cdecay = tile(NB * C, NB, C)
        Bm = [tile(NB * C, NB, C) for _ in range(2)]
        Pm = [tile(NB * C, NB, C) for _ in range(2)]
        kd = [tile(NB * D, NB, D) for _ in range(2)]
        vt = [tile(NB * D, NB, D) for _ in range(2)]
        prologue_end = offset[0]
        newblk = {k: tile(NB * C, NB, C) for k in range(1, 5)}
        N5 = tile(NB * 32, NB, 32)
        N6 = tile(NB * 64, NB, 64)
        pairs = tile(NB * 64, NB, 64)
        Y = [tile(NB * C, NB, C) for _ in range(2)]
        X = [tile(NB * C, NB, C) for _ in range(2)]
        state = tile(NB * D, NB, D)
        Rn = tile(NB * D, NB, D)
        Zn = tile(NB * D, NB, D)
        QMs = tile(NB * D, NB, D)
        o = tile(NB * D, NB, D)
        sq = tile(NB * D, NB, D)
        sq_q = tile(NB * D, NB, D)
        sq_o = tile(NB * D, NB, D)
        og = tile(NB * D, NB, D)
        ogT = tile(NB * D, NB, D)
        hn = tile(NB * D, NB, D)
        hnT = tile(NB * D, NB, D)
        relu_h = tile(NB * D, NB, D)
        gate_sum = tile(NB * D, NB, D)
        attention_end = offset[0]

        stats1 = sb("stats1", [D, NB, 6])
        mv1 = sb("mv1", [D, NB, 2])
        var1e = sb("var1e", [D, NB])
        rstd1 = sb("rstd1", [D, NB])
        logit = sb("logit", [D, 8])
        expo = sb("expo", [D, 8])
        expo1 = sb("expo1", [D, 8])
        ab = sb("ab", [D, 8])
        ab0 = sb("ab0", [D, NB])
        ssq = sb("ssq", [D, NB])
        ssk = sb("ssk", [D, NB])
        kn2 = sb("kn2", [D, NB])
        rk2 = sb("rk2", [D, NB])
        cneg = sb("cneg", [D, NB])
        knorm = sb("knorm", [D, NB])
        vsum = sb("vsum", [D, NB])
        vmean = sb("vmean", [D, NB])
        qn2e = [sb(f"qn2e{i}", [D, NB]) for i in range(2)]
        glast = sb("glast", [1, 2 * NB])
        gs = [sb(f"gs{i}", [D, 12]) for i in range(2)]
        so2 = sb("so2", [D, NB])
        ovar = sb("ovar", [D, NB])
        oscale = sb("oscale", [D, NB])
        stats2 = sb("stats2", [D, NB, 6])
        mv2 = sb("mv2", [D, NB, 2])
        var2e = sb("var2e", [D, NB])
        rstd2 = sb("rstd2", [D, NB])

        bank = [ctx.enter_context(nc.psum_tensor(f"bank{i}", [D, 512], F32)) for i in range(8)]
        blk_ps, X_ps, small_ps = bank[0], bank[2], bank[7]

        def by4(t):
            return t[:, :].rearrange("p (b c) -> p b c", b=NB)

        def by32(t):
            return t[:, 0:NB * 32].rearrange("p (b c) -> p b c", b=NB)

        def by64(t):
            return t[:, 0:NB * 64].rearrange("p (b c) -> p b c", b=NB)

        PRO = 7000
        pro = work[:, prologue_start:prologue_start + PRO]
        assert prologue_start + PRO <= prologue_end
        nat = pro[:, 128:128 + 2 * D].rearrange("p (a c) -> p a c", a=2)
        Wc = pro[:, 1664:1664 + D]
        wmean = pro[:, 1792:1793]
        wsum = pro[:, 1794:1795]
        WcT = pro[:, 1920:1920 + D]
        rhs_all = pro[:, 2048:2048 + 516]
        fold = pro[:, 2580:2580 + 516]
        bias_row = pro[0:1, 3100:3100 + 516]
        cb_row = pro[0:1, 3620:3620 + 512]
        onehot2 = pro[0:1, 4140:4140 + D]
        onehot1 = pro[0:1, 4268:4268 + D]
        cwT = pro[0:TAPS, 4410:4410 + 384]
        selA = pro[0:TAPS, 4800:4800 + D]
        selB = pro[0:TAPS, 4930:4930 + D]
        nw_col = pro[:, 5060:5061]
        cwA = pro[:, 5100:5100 + 384]
        cwB = pro[:, 5500:5500 + 384]
        tmpf = pro[:, 5900:5900 + 516]
        cbs = pro[:, 6420:6420 + 384]

        x_first_in = sem("x_first_in")
        x_in = sem("x_in")
        we_in = sem("we_in")
        w_in = sem("w_in")
        zeroed = sem("zeroed")
        con = sem("con")
        pro_pe = sem("pro_pe")
        pro_dve = sem("pro_dve")
        We_zero = sem("We_zero")
        ones_set = sem("ones_set")

        xt_ready = sem("xt_ready")
        h0_ps = sem("h0_ps")
        h0_kept = sem("h0_kept")
        h0_biased = sem("h0_biased")
        stats1_done = sem("stats1_done")
        mv1_ready = sem("mv1_ready")
        var1e_ready = sem("var1e_ready")
        rstd1_ready = sem("rstd1_ready")
        rmask_done = sem("rmask_done")
        rmat_ready = sem("rmat_ready")
        rb_ps = sem("rb_ps")
        hist_ready = sem("hist_ready")
        xs_ready = sem("xs_ready")
        xs_shifted = sem("xs_shifted")
        kvg_ps = sem("kvg_ps")
        kvg_ready = sem("kvg_ready")
        logit_ready = sem("logit_ready")
        expo_ready = sem("expo_ready")
        expo1_ready = sem("expo1_ready")
        ab_ready = sem("ab_ready")
        ab0_ready = sem("ab0_ready")
        q_ps = sem("q_ps")
        qT_ready = sem("qT_ready")
        kT_ps = sem("kT_ps")
        kT_ready = sem("kT_ready")
        alpha_ps = sem("alpha_ps")
        decay_ready = sem("decay_ready")
        glast_ready = sem("glast_ready")
        ssk_ready = sem("ssk_ready")
        kn2_ready = sem("kn2_ready")
        rk2_ready = sem("rk2_ready")
        cneg_ready = sem("cneg_ready")
        knorm_ready = sem("knorm_ready")
        vsum_ready = sem("vsum_ready")
        vmean_ready = sem("vmean_ready")
        vt_ready = sem("vt_ready")
        cdecay_ready = sem("cdecay_ready")
        kd_ready = sem("kd_ready")
        kk_ps = sem("kk_ps")
        kq_ps = sem("kq_ps")
        B_ready = sem("B_ready")
        P_ready = sem("P_ready")
        qrows_ps = sem("qrows_ps")
        ssq_ready = sem("ssq_ready")
        qn2_ready = sem("qn2_ready")
        g_ps = sem("g_ps")
        gs_ready = sem("gs_ready")
        alpha0_kept = sem("alpha0_kept")
        gate_ready = sem("gate_ready")
        blk_ps_done = sem("blk_ps_done")
        blk_ready = sem("blk_ready")
        Xps_done = sem("Xps_done")
        Y5ps_done = sem("Y5ps_done")
        pairs_ready = sem("pairs_ready")
        X_ready = sem("X_ready")
        Y_ready = sem("Y_ready")
        Y5_ready = sem("Y5_ready")
        X5_ready = sem("X5_ready")
        X6_ready = sem("X6_ready")
        X_reset = sem("X_reset")
        km_ps = sem("km_ps")
        Rn_ready = sem("Rn_ready")
        z_ps = sem("z_ps")
        Zn_ready = sem("Zn_ready")
        qm_ps = sem("qm_ps")
        QMs_ready = sem("QMs_ready")
        pz_ps = sem("pz_ps")
        o_ready = sem("o_ready")
        dm_ps = sem("dm_ps")
        state_ready = sem("state_ready")
        so2_ready = sem("so2_ready")
        ovar_ready = sem("ovar_ready")
        oscale_ready = sem("oscale_ready")
        og_ready = sem("og_ready")
        ogT_ps = sem("ogT_ps")
        ogT_ready = sem("ogT_ready")
        wo_ps = sem("wo_ps")
        h1_ready = sem("h1_ready")
        stats2_done = sem("stats2_done")
        mv2_ready = sem("mv2_ready")
        var2e_ready = sem("var2e_ready")
        rstd2_ready = sem("rstd2_ready")
        hn_ready = sem("hn_ready")
        hnT_ps = sem("hnT_ps")
        hnT_ready = sem("hnT_ready")
        gf_ps = sem("gf_ps")
        relu_ready = sem("relu_ready")
        gate_summed = sem("gate_summed")
        ln2_kept = sem("ln2_kept")

        def half(t, b, k, second):
            m = 1 << k
            if b is None:
                return t.rearrange("p b (n h m) -> p b n h m", h=2, m=m)[:, :, :, second, :]
            return t[:, b, :].rearrange("p (n h m) -> p n h m", h=2, m=m)[:, :, second, :]

        def on(j, lag):
            return not isinstance(j, int) or 0 <= j + lag < STEPS

        first, last = -2, STEPS + 1
        LOOP = (4, STEPS - 3)
        assert (LOOP[1] - LOOP[0]) % 2 == 0

        def iterations(engine, body):
            for j in range(first, LOOP[0]):
                body(j, j % 2)
            with engine.Fori(LOOP[0], LOOP[1] - 1, 2) as j:
                body(j, 0)
                body(j + 1, 1)
            for j in range(LOOP[1], last + 1):
                body(j, j % 2)

        DVE_PRO = 15
        LE, LF, LI, LC, LH = 2, 1, 0, -1, -2
        X_FIRST = 4
        block = ctx.enter_context(nc.Block())

        def row1(v):
            return v.rearrange("(a n) -> a n", a=1)

        def col1(v):
            return v.rearrange("(p a) -> p a", a=1)

        embedding = [
            (We[0:PIX, :], tok_WT[:, :]), (We[PIX:PIX + 1, :], row1(tok_b)),
            (We[PIX + 2:PIX + 3, :], tok_cls.rearrange("a b p -> (a b) p")), (bo_rows[:, :], bo.partition_broadcast(D)),
        ]
        weights_early = [
            (cwT, taps_kvq[:, :]), (bias_row[:, 0:514], row1(biases[0:514])), (cb_row[:, 0:384], row1(biases[514:898])),
            (rhs_all[:, 0:514], projections[:, :]), (nat[:, 0, :], WoT[:, :]), (nat[:, 1, :], gfc1_wT[:, :]),
            (nw_col, col1(norm_w)), (gfc1_bc[:, :], col1(gfc1_b)),
        ]
        W_IN = 16 * len(weights_early)

        ffn = make_ffn(nc, ctx, sb, sem, work, locals())

        @block.sync
        def _(sp):
            sp.wait_ge(We_zero, 1)
            for dst, src in embedding:
                sp.dma_start(dst, src).then_inc(we_in, 16)
            for dst, src in weights_early[0::2]:
                sp.dma_start(dst, src).then_inc(w_in, 16)
            ffn["load"](sp)
            ffn["sync"](sp)

        @block.scalar
        def _(act):
            act.dma_start(xc[:, :, 0:X_FIRST * C], x[:, :, 0:X_FIRST * C]).then_inc(x_first_in, 16)
            for dst, src in weights_early[1::2]:
                act.dma_start(dst, src).then_inc(w_in, 16)
            for b in range(NB):
                act.dma_start(xc[:, b, X_FIRST * C:], x[:, b, X_FIRST * C:]).then_inc(x_in, 16)

            def body(j, par):
                p = 1 - par

                def kvg_out(b):
                    if on(j, LF):
                        s = j + LF
                        act.wait_ge(kvg_ps, NB * s + b + 1)
                        if b == 0:
                            need(act, gate_ready, s - 1)
                            need(act, kd_ready, s - 1)
                            need(act, vt_ready, s - 1)
                            need(act, expo_ready, s)
                        ins = nc.scalar.mul(logit[:, b:b + 5:4], bank[4 - b % 2][:, 384:386], -1.0)
                        if b == NB - 1:
                            ins.then_inc(logit_ready, 1)
                        nc.scalar.activation(kvg[p][:, b, :], bank[4 - b % 2][:, 0:384], ACT.Silu).then_inc(kvg_ready, 1)

                kvg_out(0)
                kvg_out(1)
                if on(j, LC):
                    s = j + LC
                    act.wait_ge(z_ps, s + 1)
                    need(act, dm_ps, s)
                    nc.scalar.copy(Zn, by4(bank[5])).then_inc(Zn_ready, 1)
                    nc.scalar.copy(X[p], ident4[:, :, :]).then_inc(X_reset, 1)
                if on(j, LE):
                    s = j + LE
                    act.wait_ge(h0_ps, s + 1)
                    act.wait_ge(xt_ready, s + 1)
                    nc.scalar.copy(h1buf[:, :, bass.ds(s, 1), :].rearrange("p b s c -> p b (s c)"), by4(bank[1])).then_inc(h0_kept, 1)
                kvg_out(2)
                if on(j, LC):
                    s = j + LC
                    act.wait_ge(qm_ps, s + 1)
                    act.wait_ge(gs_ready, s + 1)
                    need(act, o_ready, s)
                    for b in range(NB):
                        ins = nc.scalar.activation(QMs[:, b, :], by4(bank[6])[:, b, :], ACT.Copy, scale=gs[p][:, b:b + 1])
                    ins.then_inc(QMs_ready, 1)
                kvg_out(3)
                if on(j, LF):
                    s = j + LF
                    act.wait_ge(kvg_ready, NB * (s + 1))
                    need(act, kn2_ready, s)
                    for b in range(NB):
                        ins = nc.scalar.activation(sq[:, b, :], kvg[p][:, b, 0:D], ACT.Square, accum_out=ssk[:, b:b + 1])
                    ins.then_inc(ssk_ready, 1)
                    act.wait_ge(q_ps, s + 1)
                    need(act, qm_ps, s - 1)
                    nc.scalar.activation(qT[p], by4(bank[4]), ACT.Silu).then_inc(qT_ready, 1)
                    act.wait_ge(qrows_ps, s + 1)
                    need(act, qn2_ready, s)
                    for b in range(NB):
                        ins = nc.scalar.activation(sq_q[:, b, :], by4(bank[1])[:, b, :], ACT.Square, accum_out=ssq[:, b:b + 1])
                    ins.then_inc(ssq_ready, 1)
                    act.wait_ge(kT_ps, s + 1)
                    nc.scalar.copy(kT[p], by4(bank[3])).then_inc(kT_ready, 1)
                if on(j, LC):
                    s = j + LC
                    act.wait_ge(o_ready, s + 1)
                    need(act, ovar_ready, s)
                    for b in range(NB):
                        ins = nc.scalar.activation(sq_o[:, b, :], o[:, b, :], ACT.Square, accum_out=so2[:, b:b + 1])
                    ins.then_inc(so2_ready, 1)
                if on(j, LH):
                    s = j + LH
                    act.wait_ge(hnT_ps, s + 1)
                    need(act, gf_ps, s)
                    nc.scalar.copy(hnT, by4(bank[6])).then_inc(hnT_ready, 1)
                if on(j, LI):
                    s = j + LI
                    s = j + LI
                    act.wait_ge(Y5ps_done, s + 1)
                    for r in (0, 64):
                        ins = nc.scalar.copy(Y[par][r + 32:r + 64, :, r:r + 32], by32(bank[1])[r + 32:r + 64])
                    ins.then_inc(Y5_ready, 1)
                    act.wait_ge(Xps_done, 6 * s + 5)
                    for r in (0, 64):
                        ins = nc.scalar.copy(X[par][r:r + 32, :, r + 32:r + 64], by32(X_ps)[r:r + 32])
                    ins.then_inc(X5_ready, 1)
                if on(j, LH):
                    s = j + LH
                    act.wait_ge(gf_ps, s + 1)
                    need(act, gate_summed, s)
                    nc.scalar.activation(relu_h, by4(bank[1]), ACT.Relu, bias=gfc1_bc[:, 0:1]).then_inc(relu_ready, 1)
                if on(j, LI):
                    s = j + LI
                    act.wait_ge(Xps_done, 6 * s + 6)
                    nc.scalar.copy(X[par][0:64, :, 64:128], by64(X_ps)[0:64]).then_inc(X6_ready, 1)
                if on(j, LC):
                    s = j + LC
                    act.wait_ge(ogT_ps, s + 1)
                    need(act, wo_ps, s)
                    nc.scalar.copy(ogT, by4(bank[5])).then_inc(ogT_ready, 1)
                if on(j, LE):
                    s = j + LE
                    act.wait_ge(hist_ready, s + 1)
                    act.wait_ge(xs_ready, s + 1)
                    need(act, q_ps, s - 1)
                    nc.scalar.copy(xs[par][64:64 + KX, :, 1:XW], xs[par][0:KX, :, 0:XW - 1]).then_inc(xs_shifted, 1)

            iterations(act, body)
            ffn["scalar"](act)

        @block.gpsimd
        def _(pool):
            nc.gpsimd.memset(ones[:, :], 1.0).then_inc(ones_set, 1)
            nc.gpsimd.memset(masks[:, :, :], 1.0).then_inc(ones_set, 1)
            nc.gpsimd.memset(half_neg[:, :], -0.5)
            nc.gpsimd.memset(half_pos[:, :], 0.5)
            nc.gpsimd.memset(euler[:, :], 2.718281828459045).then_inc(ones_set, 1)
            pool.wait_ge(ones_set, 3)
            nc.gpsimd.affine_select(out=ident[:, :], in_=ones[:, :], pattern=[[-1, D]], compare_op=ALU.is_equal,
                                    fill=0.0, base=0, channel_multiplier=1).then_inc(con, 1)
            pool.wait_ge(con, 1)
            nc.gpsimd.affine_select(out=not_first[:, :], in_=ones[:, 0:NB], pattern=[[0, NB]], compare_op=ALU.is_gt,
                                    fill=0.0, base=0, channel_multiplier=1)
            for b in range(NB):
                nc.gpsimd.tensor_copy(ident4[:, b, :], ident[:, :])
            nc.gpsimd.affine_select(out=mask_1[:, :], in_=ones[:, 0:KX], pattern=[[1, KX]], compare_op=ALU.is_equal,
                                    fill=0.0, base=-(PIX + 1), channel_multiplier=0)
            nc.gpsimd.affine_select(out=mask_x[:, :], in_=ones[:, 0:KX], pattern=[[1, KX]], compare_op=ALU.not_equal,
                                    fill=0.0, base=-(PIX + 1), channel_multiplier=0)
            sel = ((selA, 3, 2), (selB, 1, 0))
            for t, low, high in sel:
                nc.gpsimd.affine_select(out=t[:, 0:64], in_=ones[0:TAPS, 0:64], pattern=[[0, 64]],
                                        compare_op=ALU.is_equal, fill=0.0, base=-low, channel_multiplier=1)
                nc.gpsimd.affine_select(out=t[:, 64:128], in_=ones[0:TAPS, 0:64], pattern=[[0, 64]],
                                        compare_op=ALU.is_equal, fill=0.0, base=-high, channel_multiplier=1)
            nc.gpsimd.affine_select(out=onehot2.rearrange("p (h c) -> p h c", h=2), in_=ones[0:1, :].rearrange("p (h c) -> p h c", h=2),
                                    pattern=[[0, 2], [1, 64]], compare_op=ALU.is_equal, fill=0.0, base=-(PIX + 1), channel_multiplier=0)
            nc.gpsimd.affine_select(out=onehot1, in_=ones[0:1, :], pattern=[[1, D]],
                                    compare_op=ALU.is_equal, fill=0.0, base=-(PIX + 1), channel_multiplier=0).then_inc(con, 1)
            pool.wait_ge(con, 2)
            pool.wait_ge(zeroed, 1)
            pool.wait_ge(x_first_in, 16)
            pool.wait_ge(we_in, 16 * len(embedding))

            def level_masks():
                for i, k in enumerate(MASKED):
                    m = 1 << k
                    n = D // (2 * m)
                    v = masks[:, i, :].rearrange("p (n m) -> p n m", m=m)
                    nc.gpsimd.affine_select(out=v, in_=v, pattern=[[-2 * m, n], [0, m]], compare_op=ALU.is_ge,
                                            fill=0.0, base=-m, channel_multiplier=1).then_inc(con, 1)
                pool.wait_ge(con, 2 + len(MASKED))
                for i, k in enumerate(MASKED):
                    m = 1 << k
                    n = D // (2 * m)
                    v = masks[:, i, :].rearrange("p (n m) -> p n m", m=m)
                    nc.gpsimd.affine_select(out=v, in_=v, pattern=[[2 * m, n], [0, m]], compare_op=ALU.is_ge,
                                            fill=0.0, base=2 * m - 1, channel_multiplier=-1).then_inc(con, 1)

            def body(j, par):
                p = 1 - par
                if on(j, LE):
                    s = j + LE
                    if isinstance(s, int) and s == X_FIRST:
                        pool.wait_ge(x_in, 16 * NB)
                    need(pool, xs_ready, s - 1)
                    need(pool, h0_ps, s - 1)
                    apart(pool)
                    nc.gpsimd.tensor_copy(xt[par][0:KX, :, :], xc[:, :, bass.ds(s * C, C)]).then_inc(xt_ready, 1)
                if on(j, LE):
                    s = j + LE
                    if not isinstance(s, int) or s > 0:
                        pool.wait_ge(xs_ready, s)
                        need(pool, q_ps, s - 1)
                        need(pool, xs_shifted, s - 1)
                        apart(pool)
                        nc.gpsimd.tensor_copy(xs[par][0:KX, :, 0:HIST], xs[p][0:KX, :, C:XW]).then_inc(hist_ready, 1)
                    else:
                        nc.gpsimd.memset(xs[par][0:KX, :, 0:HIST], 0.0).then_inc(hist_ready, 1)
                if on(j, LH):
                    s = j + LH
                    pool.wait_ge(mv2_ready, s + 1)
                    need(pool, rstd2_ready, s)
                    apart(pool)
                    nc.gpsimd.tensor_scalar(var2e[:, :], mv2[:, :, 1], EPS, None, ALU.add).then_inc(var2e_ready, 1)
                    pool.wait_ge(var2e_ready, s + 1)
                    need(pool, ln2_kept, s)
                    nc.gpsimd.tensor_tensor(rstd2[:, :], var2e[:, :], half_neg[:, :], ALU.pow).then_inc(rstd2_ready, 1)
                if on(j, LF):
                    s = j + LF
                    pool.wait_ge(logit_ready, s + 1)
                    need(pool, expo1_ready, s)
                    nc.gpsimd.tensor_tensor(expo[:, :], euler[:, :], logit[:, :], ALU.pow).then_inc(expo_ready, 1)
                if on(j, LE):
                    s = j + LE
                    pool.wait_ge(mv1_ready, s + 1)
                    need(pool, rstd1_ready, s)
                    apart(pool)
                    nc.gpsimd.tensor_scalar(var1e[:, :], mv1[:, :, 1], EPS, None, ALU.add).then_inc(var1e_ready, 1)
                    pool.wait_ge(var1e_ready, s + 1)
                    need(pool, rmask_done, s)
                    nc.gpsimd.tensor_tensor(rstd1[:, :], var1e[:, :], half_neg[:, :], ALU.pow).then_inc(rstd1_ready, 1)
                    pool.wait_ge(rstd1_ready, s + 1)
                    need(pool, rb_ps, s)
                    nc.gpsimd.tensor_tensor(rmat, mask_x[:, :].unsqueeze(1).broadcast_to([D, NB, KX]),
                                            rstd1[:, :].unsqueeze(2).broadcast_to([D, NB, KX]), ALU.mult).then_inc(rmask_done, 1)
                    pool.wait_ge(rmask_done, s + 1)
                    nc.gpsimd.tensor_tensor(rmat, rmat, mask_1[:, :].unsqueeze(1).broadcast_to([D, NB, KX]),
                                            ALU.add).then_inc(rmat_ready, 1)
                if on(j, LC):
                    s = j + LC
                    pool.wait_ge(ovar_ready, s + 1)
                    need(pool, og_ready, NB * s)
                    nc.gpsimd.tensor_tensor(oscale[:, :], ovar[:, :], half_neg[:, :], ALU.pow).then_inc(oscale_ready, 1)
                if on(j, LF):
                    s = j + LF
                    pool.wait_ge(decay_ready, s + 1)
                    pool.wait_ge(cneg_ready, s + 1)
                    need(pool, P_ready, s)
                    need(pool, kd_ready, s)
                    nc.gpsimd.tensor_tensor(cdecay, decay, cneg[:, :].unsqueeze(2).broadcast_to([D, NB, C]),
                                            ALU.mult).then_inc(cdecay_ready, 1)
                if on(j, LF):
                    s = j + LF
                    pool.wait_ge(kn2_ready, s + 1)
                    need(pool, vt_ready, s)
                    nc.gpsimd.tensor_tensor(knorm[:, :], kn2[:, :], half_pos[:, :], ALU.pow).then_inc(knorm_ready, 1)
                if on(j, LH):
                    s = j + LH
                    pool.wait_ge(relu_ready, s + 1)
                    need(pool, gate_summed, s)
                    n = LAST if isinstance(s, int) and s == STEPS - 1 else C
                    nc.gpsimd.tensor_tensor(gate_sum[:, :, 0:n], gate_sum[:, :, 0:n], relu_h[:, :, 0:n],
                                            ALU.add).then_inc(gate_summed, 1)
                if on(j, LI):
                    s = j + LI
                    pool.wait_ge(kvg_ready, NB * (s + 1))
                    need(pool, og_ready, NB * s)
                    apart(pool)
                    nc.gpsimd.tensor_copy(gate_kept, kvg[par][:, :, 2 * D:3 * D]).then_inc(gate_ready, 1)
                if isinstance(j, int) and j == first:
                    level_masks()
                if on(j, LE):
                    s = j + LE
                    pool.wait_ge(h0_kept, s + 1)
                    h = h1buf[:, :, bass.ds(s, 1), :].rearrange("p b s c -> p b (s c)")
                    apart(pool)
                    nc.gpsimd.tensor_tensor(h, h, bo_rows[:, :].unsqueeze(1).broadcast_to([D, NB, D]),
                                            ALU.add).then_inc(h0_biased, 1)

            iterations(pool, body)
            ffn["gpsimd"](pool)

        @block.vector
        def _(dve):
            done = [0]

            def step_done(ins):
                done[0] += 1
                ins.then_inc(pro_dve, 1)
                dve.wait_ge(pro_dve, done[0])

            nc.vector.memset(We[:, :], 0.0).then_inc(We_zero, 1)
            ffn["vector_early"](dve)
            nc.vector.memset(Wc, 0.0)
            nc.vector.memset(WcT, 0.0)
            nc.vector.memset(xs[0], 0.0)
            nc.vector.memset(xs[1], 0.0)
            for t in newblk.values():
                nc.vector.memset(t, 0.0)
            nc.vector.memset(gate_sum, 0.0)
            nc.vector.memset(state, 0.0).then_inc(zeroed, 1)

            def fold_weights():
                dve.wait_ge(con, 2)
                dve.wait_ge(zeroed, 1)
                for t in X:
                    nc.vector.tensor_copy(t, ident4[:, :, :])
                dve.wait_ge(we_in, 16 * len(embedding))
                dve.wait_ge(w_in, W_IN)
                step_done(nc.vector.tensor_reduce(wsum[0:KX, :], We[0:KX, :], AX.X, ALU.add))
                step_done(nc.vector.tensor_scalar(wmean[0:KX, :], wsum[0:KX, :], 1.0 / D, None, ALU.mult))
                step_done(nc.vector.tensor_scalar(Wc[0:KX, :], We[0:KX, :], wmean[0:KX, :], None, ALU.subtract))
                step_done(nc.vector.tensor_scalar(Wo_T[:, :], nat[:, 0, :], nw_col, None, ALU.mult))
                step_done(nc.vector.tensor_copy(gfc1_T[:, :], nat[:, 1, :]))
                dve.wait_ge(pro_pe, 1)
                step_done(nc.vector.tensor_copy(WcT.rearrange("p (h c) -> p h c", h=2)[:, :, 0:KX],
                                                bank[3][:, 0:KX].unsqueeze(1).broadcast_to([D, 2, KX])))
                dve.wait_ge(pro_pe, 2)
                step_done(nc.vector.tensor_copy(fold[:, 0:512], bank[5][:, :]))
                step_done(nc.vector.tensor_copy(fold[:, 512:514], bank[6][:, 0:2]))
                for dst, taps in ((SA, bank[0]), (SB, bank[4])):
                    step_done(nc.vector.tensor_tensor(dst[:, 0:256], taps[:, 0:256], fold[:, 0:256], ALU.mult))
                    dst_q = dst[:, 386:514] if dst is SA else dst[:, 384:512]
                    step_done(nc.vector.tensor_tensor(dst_q, taps[:, 256:384], fold[:, 384:512], ALU.mult))
                step_done(nc.vector.tensor_tensor(SA[:, 0:256], bank[2][:, 0:256], SA[:, 0:256], ALU.add))
                step_done(nc.vector.tensor_tensor(SA[:, 386:514], bank[2][:, 256:384], SA[:, 386:514], ALU.add))
                nc.vector.memset(SA[64:128, 256:386], 0.0)
                nc.vector.tensor_copy(SA[0:64, 256:384], fold[0:64, 256:384])
                step_done(nc.vector.tensor_copy(SA[0:64, 384:386], fold[0:64, 512:514]))
                assert done[0] == DVE_PRO

            def body(j, par):
                p = 1 - par

                def new_blocks(k):
                    if not on(j, LI):
                        return
                    s = j + LI
                    dve.wait_ge(blk_ps_done, 6 * s + k)
                    need(dve, Xps_done, 6 * (s - 1) + k)
                    if k == 6:
                        nc.vector.tensor_copy(N6[64:128], by64(blk_ps)[64:128]).then_inc(blk_ready, 1)
                    elif k == 5:
                        for r in (32, 96):
                            ins = nc.vector.tensor_copy(N5[r:r + 32], by32(blk_ps)[r:r + 32])
                        ins.then_inc(blk_ready, 1)
                    else:
                        m = 1 << k
                        nc.vector.tensor_tensor(half(newblk[k], None, k, 0), by64(blk_ps).rearrange("p b (n m) -> p b n m", m=m),
                                                masks[:, MASKED.index(k), :].unsqueeze(1).broadcast_to([D, NB, 64]).rearrange("p b (n m) -> p b n m", m=m),
                                                ALU.mult).then_inc(blk_ready, 1)

                def grow(k):
                    if not on(j, LI):
                        return
                    s = j + LI
                    dve.wait_ge(Xps_done, 6 * s + k)
                    x = half(X[par], None, k, 1)
                    nc.vector.tensor_tensor(x, by64(X_ps).rearrange("p b (n m) -> p b n m", m=1 << k), x, ALU.add).then_inc(X_ready, 1)
                    dve.wait_ge(X_ready, 5 * s + k + 1)
                    nc.vector.transpose(Y[par].rearrange("p b c -> p (b c)"), X[par].rearrange("p b c -> p (b c)")).then_inc(Y_ready, 1)

                if on(j, LH):
                    s = j + LH
                    h = h1buf[:, :, bass.ds(s, 1), :].rearrange("p b s c -> p b (s c)")
                    dve.wait_ge(wo_ps, s + 1)
                    dve.wait_ge(h0_biased, s + 1)
                    nc.vector.tensor_tensor(h, by4(bank[6]), h, ALU.add).then_inc(h1_ready, 1)
                new_blocks(1)
                if on(j, LC):
                    s = j + LC
                    dve.wait_ge(km_ps, s + 1)
                    dve.wait_ge(gs_ready, s + 1)
                    dve.wait_ge(vt_ready, s + 1)
                    need(dve, z_ps, s)
                    for b in range(NB):
                        ins = nc.vector.scalar_tensor_tensor(Rn[:, b, :], by4(bank[5])[:, b, :], gs[p][:, b:b + 1], vt[p][:, b, :],
                                                             ALU.mult, ALU.subtract)
                    ins.then_inc(Rn_ready, 1)
                if on(j, LI):
                    s = j + LI
                    dve.wait_ge(g_ps, s + 1)
                    need(dve, state_ready, s - 1)
                    need(dve, QMs_ready, s - 1)
                    nc.vector.tensor_copy(gs[par][:, 4:12], small_ps[:, 20:28]).then_inc(alpha0_kept, 1)
                    dve.wait_ge(alpha0_kept, s + 1)
                    nc.vector.tensor_tensor(gs[par][:, 0:4], small_ps[:, 16:20], gs[par][:, 8:12], ALU.mult).then_inc(gs_ready, 1)
                grow(1)
                if on(j, LH):
                    s = j + LH
                    h = h1buf[:, :, bass.ds(s, 1), :].rearrange("p b s c -> p b (s c)")
                    dve.wait_ge(h1_ready, s + 1)
                    need(dve, mv2_ready, s)
                    apart(dve)
                    for b in range(NB):
                        ins = nc.vector.bn_stats(stats2[:, b, :], h[:, b, :])
                    ins.then_inc(stats2_done, 1)
                    dve.wait_ge(stats2_done, s + 1)
                    need(dve, hn_ready, s)
                    apart(dve)
                    for b in range(NB):
                        ins = nc.vector.bn_aggr(mv2[:, b, :], stats2[:, b, :])
                    ins.then_inc(mv2_ready, 1)
                new_blocks(2)
                if on(j, LI):
                    s = j + LI
                    dve.wait_ge(kvg_ready, NB * (s + 1))
                    need(dve, vmean_ready, s)
                    nc.vector.tensor_reduce(vsum[:, :], kvg[par][:, :, D:2 * D], AX.X, ALU.add).then_inc(vsum_ready, 1)
                grow(2)
                if on(j, LI):
                    s = j + LI
                    dve.wait_ge(cdecay_ready, s + 1)
                    need(dve, dm_ps, s - 1)
                    for b in range(NB):
                        ins = nc.vector.tensor_scalar(kd[par][:, b, :], kvg[par][:, b, 0:D], cdecay[:, b, C - 1:C], None, ALU.mult)
                    ins.then_inc(kd_ready, 1)
                    dve.wait_ge(vsum_ready, s + 1)
                    need(dve, vt_ready, s)
                    nc.vector.tensor_scalar(vmean[:, :], vsum[:, :], 1.0 / D, None, ALU.mult).then_inc(vmean_ready, 1)
                    dve.wait_ge(knorm_ready, s + 1)
                    dve.wait_ge(vmean_ready, s + 1)
                    need(dve, Rn_ready, s - 1)
                    for b in range(NB):
                        ins = nc.vector.tensor_scalar(vt[par][:, b, :], kvg[par][:, b, D:2 * D], vmean[:, b:b + 1], knorm[:, b:b + 1],
                                                      ALU.subtract, ALU.mult)
                    ins.then_inc(vt_ready, 1)
                new_blocks(3)
                if on(j, LH):
                    s = j + LH
                    h = h1buf[:, :, bass.ds(s, 1), :].rearrange("p b s c -> p b (s c)")
                    dve.wait_ge(mv2_ready, s + 1)
                    kept = ln2[:, bass.ds(s, 1), :, :].rearrange("p s b m -> p (s b) m")
                    nc.vector.tensor_copy(kept[:, :, 0], mv2[:, :, 0])
                    dve.wait_ge(rstd2_ready, s + 1)
                    nc.vector.tensor_copy(kept[:, :, 1], rstd2[:, :]).then_inc(ln2_kept, 1)
                    need(dve, hnT_ps, s)
                    for b in range(NB):
                        ins = nc.vector.tensor_scalar(hn[:, b, :], h[:, b, :], mv2[:, b, 0:1], rstd2[:, b:b + 1],
                                                      ALU.subtract, ALU.mult)
                    ins.then_inc(hn_ready, 1)

                grow(3)
                if on(j, LE):
                    s = j + LE
                    dve.wait_ge(h0_kept, s + 1)
                    need(dve, mv1_ready, s)
                    apart(dve)
                    for b in range(NB):
                        ins = nc.vector.bn_stats(stats1[:, b, :], by4(bank[1])[:, b, :])
                    ins.then_inc(stats1_done, 1)
                    dve.wait_ge(stats1_done, s + 1)
                    need(dve, var1e_ready, s)
                    apart(dve)
                    for b in range(NB):
                        ins = nc.vector.bn_aggr(mv1[:, b, :], stats1[:, b, :])
                    ins.then_inc(mv1_ready, 1)
                new_blocks(4)
                if on(j, LF):
                    s = j + LF
                    dve.wait_ge(expo_ready, s + 1)
                    need(dve, ab_ready, s)
                    nc.vector.tensor_scalar(expo1[:, :], expo[:, :], 1.0, None, ALU.add).then_inc(expo1_ready, 1)
                    dve.wait_ge(expo1_ready, s + 1)
                    need(dve, g_ps, s)
                    nc.vector.reciprocal(ab[:, :], expo1[:, :]).then_inc(ab_ready, 1)
                    dve.wait_ge(ab_ready, s + 1)
                    need(dve, alpha_ps, s)
                    nc.vector.tensor_tensor(ab0[:, :], ab[:, 0:NB], not_first[:, :], ALU.mult).then_inc(ab0_ready, 1)
                grow(4)
                if on(j, LC):
                    s = j + LC
                    dve.wait_ge(pz_ps, s + 1)
                    dve.wait_ge(QMs_ready, s + 1)
                    need(dve, og_ready, NB * s)
                    need(dve, so2_ready, s)
                    nc.vector.tensor_tensor(o, by4(bank[6]), QMs, ALU.add).then_inc(o_ready, 1)
                new_blocks(5)
                if on(j, LF):
                    s = j + LF
                    dve.wait_ge(alpha_ps, s + 1)
                    need(dve, g_ps, s)
                    need(dve, cdecay_ready, s)
                    need(dve, glast_ready, s)
                    nc.vector.tensor_tensor_scan(decay.rearrange("p b c -> p (b c)"), bank[4][:, :],
                                                 ident4[:, :, :].rearrange("p b c -> p (b c)"), 0.0, ALU.mult, ALU.add).then_inc(decay_ready, 1)
                    dve.wait_ge(decay_ready, s + 1)
                    nc.vector.tensor_copy(glast[:, NB:2 * NB], ab[0:1, 0:NB])
                    nc.vector.tensor_tensor(glast[:, 0:NB], decay[0:1, :, C - 1], ab[0:1, 0:NB], ALU.mult).then_inc(glast_ready, 1)
                if on(j, LC):
                    s = j + LC
                    dve.wait_ge(so2_ready, s + 1)
                    need(dve, oscale_ready, s)
                    nc.vector.scalar_tensor_tensor(ovar[:, :], so2[:, :], 1.0 / D, qn2e[p][:, :], ALU.mult, ALU.add).then_inc(ovar_ready, 1)
                if on(j, LF):
                    s = j + LF
                    dve.wait_ge(kvg_ready, NB * (s + 1))
                    dve.wait_ge(ssk_ready, s + 1)
                    need(dve, rk2_ready, s)
                    need(dve, knorm_ready, s)
                    nc.vector.tensor_scalar(kn2[:, :], ssk[:, :], 1e-24, None, ALU.max).then_inc(kn2_ready, 1)
                    dve.wait_ge(kn2_ready, s + 1)
                    nc.vector.reciprocal(rk2[:, :], kn2[:, :]).then_inc(rk2_ready, 1)
                    dve.wait_ge(rk2_ready, s + 1)
                    need(dve, cdecay_ready, s)
                    nc.vector.scalar_tensor_tensor(cneg[:, :], rk2[:, :], -1.0, ab[:, 4:8], ALU.mult, ALU.mult).then_inc(cneg_ready, 1)
                if on(j, LC):
                    s = j + LC
                    dve.wait_ge(dm_ps, s + 1)
                    for b in range(NB):
                        ins = nc.vector.scalar_tensor_tensor(state[:, b, :], state[:, b, :], gs[p][:, 4 + b:5 + b], by4(bank[5])[:, b, :],
                                                             ALU.mult, ALU.add)
                    ins.then_inc(state_ready, 1)
                if on(j, LF):
                    s = j + LF
                    dve.wait_ge(ssq_ready, s + 1)
                    need(dve, ovar_ready, s - 1)
                    nc.vector.tensor_scalar(qn2e[p][:, :], ssq[:, :], 1e-24, EPS, ALU.max, ALU.mult).then_inc(qn2_ready, 1)
                new_blocks(6)
                if on(j, LC):
                    s = j + LC
                    dve.wait_ge(oscale_ready, s + 1)
                    dve.wait_ge(gate_ready, s + 1)
                    need(dve, ogT_ps, s)
                    for b in range(NB):
                        nc.vector.scalar_tensor_tensor(og[:, b, :], o[:, b, :], oscale[:, b:b + 1], gate_kept[:, b, :],
                                                             ALU.mult, ALU.mult).then_inc(og_ready, 1)
                if on(j, LF):
                    s = j + LF
                    dve.wait_ge(kk_ps, s + 1)
                    dve.wait_ge(cdecay_ready, s + 1)
                    need(dve, blk_ps_done, 6 * (s - 1))
                    nc.vector.tensor_tensor(Bm[p], by4(bank[4]), cdecay, ALU.mult).then_inc(B_ready, 1)
                    dve.wait_ge(B_ready, s + 1)
                    nc.vector.tensor_tensor(pairs, Bm[p][:, :, 1:C:2], ident4[:, :, 0:C:2], ALU.mult).then_inc(pairs_ready, 1)
                    dve.wait_ge(pairs_ready, s + 1)
                    need(dve, X_reset, s - 1)
                    nc.vector.tensor_tensor(X[p][:, :, 1:C:2], X[p][:, :, 1:C:2], pairs, ALU.add).then_inc(X_ready, 1)
                    dve.wait_ge(X_ready, 5 * s + 1)
                    nc.vector.transpose(Y[p].rearrange("p b c -> p (b c)"), X[p].rearrange("p b c -> p (b c)")).then_inc(Y_ready, 1)
                if isinstance(j, int) and j == first:
                    fold_weights()
                if on(j, LE):
                    s = j + LE
                    dve.wait_ge(rb_ps, s + 1)
                    dve.wait_ge(xt_ready, s + 1)
                    need(dve, q_ps, s - 1)
                    need(dve, hist_ready, s)
                    nc.vector.tensor_tensor(xs[par][0:KX, :, HIST:XW], by4(bank[1])[0:KX], xt[par][0:KX, :, :],
                                            ALU.mult).then_inc(xs_ready, 1)
                if on(j, LF):
                    s = j + LF
                    dve.wait_ge(kq_ps, s + 1)
                    need(dve, pz_ps, s - 1)
                    nc.vector.tensor_tensor(Pm[p], by4(bank[3]), cdecay, ALU.mult).then_inc(P_ready, 1)

            iterations(dve, body)
            ffn["vector"](dve)

        @block.tensor
        def _(pe):
            mm = nc.tensor.matmul
            tr = nc.tensor.transpose
            pe.wait_ge(con, 2)
            pe.wait_ge(we_in, 16 * len(embedding))
            pe.wait_ge(zeroed, 1)

            def fold_weights():
                pe.wait_ge(w_in, W_IN)
                mm(bank[0][:, 0:384], selA, cwT, start=True, stop=True)
                mm(bank[4][:, 0:384], selB, cwT, start=True, stop=True)
                mm(bank[2][:, 0:384], onehot1, cb_row[:, 0:384], start=True, stop=True)
                pe.wait_ge(pro_dve, 3)
                tr(bank[3][:, 0:D], Wc, ident[:, :]).then_inc(pro_pe, 1)
                pe.wait_ge(pro_dve, 6)
                mm(bank[5][:, :], WcT, rhs_all[:, 0:512], start=True, stop=False)
                mm(bank[5][:, :], onehot2, bias_row[:, 0:512], start=False, stop=True)
                mm(bank[6][:, 0:2], WcT, rhs_all[:, 512:514], start=True, stop=False)
                mm(bank[6][:, 0:2], onehot2, bias_row[:, 512:514], start=False, stop=True).then_inc(pro_pe, 1)
                pe.wait_ge(pro_dve, DVE_PRO)
                pe.wait_ge(con, 2 + 2 * len(MASKED))

            def body(j, par):
                p = 1 - par
                F_, I_, C_, H_, E_ = on(j, LF), on(j, LI), on(j, LC), on(j, LH), on(j, LE)
                s1, s0, c, h, e = j + LF, j + LI, j + LC, j + LH, j + LE

                def level_blocks(k):
                    if not I_:
                        return
                    if k <= 5:
                        pe.wait_ge(Y_ready, 5 * s0 + k)
                    else:
                        pe.wait_ge(Y5_ready, s0 + 1)
                    need(pe, blk_ready, 6 * s0 + k - 1)
                    if k >= 5:
                        apart(pe)
                    for b in range(NB):
                        if k < 5:
                            ins = mm(by64(blk_ps)[:, b], Bm[par][:, b, :], half(Y[par], b, k, 0), start=True, stop=True)
                        elif k == 5:
                            for r in (0, 64):
                                ins = mm(by32(blk_ps)[r + 32:r + 64, b], Bm[par][r:r + 32, b, r + 32:r + 64],
                                         Y[par][r:r + 32, b, r:r + 32], start=True, stop=True)
                        else:
                            ins = mm(by64(blk_ps)[64:128, b], Bm[par][0:64, b, 64:128], Y[par][0:64, b, 0:64], start=True, stop=True)
                    ins.then_inc(blk_ps_done, 1)

                def level_update(k):
                    if not I_:
                        return
                    pe.wait_ge(blk_ready, 6 * s0 + k)
                    if k == 6:
                        pe.wait_ge(X5_ready, s0 + 1)
                    if k >= 5:
                        apart(pe)
                    if k == 5:
                        if F_:
                            pe.wait_ge(ssq_ready, s1 + 1)
                            apart(pe)
                        for b in range(NB):
                            for r in (0, 64):
                                ins = mm(by32(bank[1])[r + 32:r + 64, b], X[par][r + 32:r + 64, b, r + 32:r + 64],
                                         N5[r + 32:r + 64, b, :], start=True, stop=True)
                        ins.then_inc(Y5ps_done, 1)
                    if k == 1:
                        need(pe, X6_ready, s0)
                    for b in range(NB):
                        if k < 5:
                            ins = mm(by64(X_ps)[:, b], newblk[k][:, b, :], half(X[par], b, k, 1), start=True, stop=True)
                        elif k == 5:
                            for r in (0, 64):
                                ins = mm(by32(X_ps)[r:r + 32, b], N5[r + 32:r + 64, b, :],
                                         X[par][r + 32:r + 64, b, r + 32:r + 64], start=True, stop=True)
                        else:
                            ins = mm(by64(X_ps)[0:64, b], N6[64:128, b, :], X[par][64:128, b, 64:128], start=True, stop=True)
                    ins.then_inc(Xps_done, 1)

                def kvg_rows(b):
                    t = bank[4 - b % 2]
                    mm(t[:, 0:386], xs[p][:, b, HIST:XW], SA[:, 0:386], start=True, stop=False)
                    mm(t[:, 0:256], xs[p][:, b, 1:1 + C], SB[:, 0:256], start=False, stop=True).then_inc(kvg_ps, 1)

                if C_:
                    need(pe, state_ready, c)
                    need(pe, ogT_ready, c)
                    for b in range(NB):
                        ins = mm(by4(bank[5])[:, b, :], kT[p][:, b, :], state[:, b, :], start=True, stop=True)
                    ins.then_inc(km_ps, 1)
                level_blocks(1)
                if F_:
                    pe.wait_ge(xs_ready, s1 + 1)
                    pe.wait_ge(xs_shifted, s1 + 1)
                    need(pe, B_ready, s1)
                    kvg_rows(0)
                level_update(1)
                if F_:
                    need(pe, P_ready, s1)
                    kvg_rows(1)
                if C_:
                    pe.wait_ge(Rn_ready, c + 1)
                    pe.wait_ge(X6_ready, c + 1)
                    for b in range(NB):
                        ins = mm(by4(bank[5])[:, b, :], X[p][:, b, :], Rn[:, b, :], start=True, stop=True)
                    ins.then_inc(z_ps, 1)
                level_blocks(2)
                if E_:
                    pe.wait_ge(xt_ready, e + 1)
                    need(pe, xs_ready, e)
                    for b in range(NB):
                        ins = mm(by4(bank[1])[:, b, :], xt[par][0:KX, b, :], We[0:KX, :], start=True, stop=True)
                    ins.then_inc(h0_ps, 1)
                level_update(2)
                if F_:
                    pe.wait_ge(kvg_ready, NB * s1 + 1)
                    kvg_rows(2)
                if C_:
                    need(pe, h1_ready, c)
                    for b in range(NB):
                        ins = mm(by4(bank[6])[:, b, :], qT[p][:, b, :], state[:, b, :], start=True, stop=True)
                    ins.then_inc(qm_ps, 1)
                level_blocks(3)
                if F_:
                    pe.wait_ge(kvg_ready, NB * s1 + 2)
                    kvg_rows(3)
                level_update(3)
                if F_:
                    pe.wait_ge(kvg_ready, NB * s1 + 3)
                    mm(bank[4][:, :], SA[:, 386:514], xs[p][:, :, HIST:XW], start=True, stop=False)
                    mm(bank[4][:, :], SB[:, 384:512], xs[p][:, :, 1:1 + C], start=False, stop=True).then_inc(q_ps, 1)
                level_blocks(4)
                if C_:
                    pe.wait_ge(Zn_ready, c + 1)
                    pe.wait_ge(QMs_ready, c + 1)
                    for b in range(NB):
                        ins = mm(by4(bank[6])[:, b, :], Pm[p][:, b, :], Zn[:, b, :], start=True, stop=True)
                    ins.then_inc(pz_ps, 1)
                level_update(4)
                if F_:
                    pe.wait_ge(qT_ready, s1 + 1)
                    if E_:
                        pe.wait_ge(stats1_done, e + 1)
                    for b in range(NB):
                        ins = tr(by4(bank[1])[:, b, :], qT[p][:, b, :], ident[:, :])
                    ins.then_inc(qrows_ps, 1)
                if C_:
                    for b in range(NB):
                        ins = mm(by4(bank[5])[:, b, :], kd[p][:, b, :], Zn[:, b, :], start=True, stop=True)
                    ins.then_inc(dm_ps, 1)
                if F_:
                    pe.wait_ge(kvg_ready, NB * s1 + 4)
                    for b in range(NB):
                        ins = tr(by4(bank[3])[:, b, :], kvg[p][:, b, 0:D], ident[:, :])
                    ins.then_inc(kT_ps, 1)
                level_blocks(5)
                if F_:
                    pe.wait_ge(ab0_ready, s1 + 1)
                    pe.wait_ge(qT_ready, s1 + 1)
                    for b in range(NB):
                        ins = tr(by4(bank[4])[:, b, :], ab0[:, b:b + 1].broadcast_to([D, D]), ident[:, :])
                    ins.then_inc(alpha_ps, 1)
                if H_:
                    pe.wait_ge(hn_ready, h + 1)
                    if C_:
                        pe.wait_ge(o_ready, c + 1)
                    for b in range(NB):
                        ins = tr(by4(bank[6])[:, b, :], hn[:, b, :], ident[:, :])
                    ins.then_inc(hnT_ps, 1)
                level_update(5)
                if F_:
                    pe.wait_ge(kT_ready, s1 + 1)
                    pe.wait_ge(decay_ready, s1 + 1)
                    for b in range(NB):
                        ins = mm(by4(bank[4])[:, b, :], kT[p][:, b, :], kT[p][:, b, :], start=True, stop=True)
                    ins.then_inc(kk_ps, 1)
                if F_:
                    for b in range(NB):
                        ins = mm(by4(bank[3])[:, b, :], kT[p][:, b, :], qT[p][:, b, :], start=True, stop=True)
                    ins.then_inc(kq_ps, 1)
                level_blocks(6)
                if H_:
                    pe.wait_ge(hnT_ready, h + 1)
                    if I_:
                        pe.wait_ge(Y5_ready, s0 + 1)
                    mm(bank[1][:, :], gfc1_T[:, :], hnT.rearrange("p b c -> p (b c)"), start=True, stop=True).then_inc(gf_ps, 1)
                level_update(6)
                if C_:
                    pe.wait_ge(state_ready, c + 1)
                    for b in range(NB):
                        pe.wait_ge(og_ready, NB * c + b + 1)
                        ins = tr(by4(bank[5])[:, b, :], og[:, b, :], ident[:, :])
                    ins.then_inc(ogT_ps, 1)
                if isinstance(j, int) and j == first:
                    fold_weights()
                if E_:
                    pe.wait_ge(rmat_ready, e + 1)
                    need(pe, relu_ready, h + 1)
                    if F_:
                        pe.wait_ge(ssq_ready, s1 + 1)
                    need(pe, Y5_ready, s0 + 1)
                    apart(pe)
                    for b in range(NB):
                        ins = tr(by4(bank[1])[0:KX, b, :], rmat[:, b, :], ident[:, :])
                    ins.then_inc(rb_ps, 1)
                if F_:
                    pe.wait_ge(glast_ready, s1 + 1)
                    pe.wait_ge(ab_ready, s1 + 1)
                    need(pe, gs_ready, s1)
                    apart(pe)
                    for b in range(NB):
                        tr(small_ps[:, 16 + b:17 + b], decay[0:1, b, :], ident[0:1, 0:1])
                    mm(small_ps[:, 20:28], ones[0:1, :], glast[:, :], start=True, stop=True).then_inc(g_ps, 1)
                if C_:
                    pe.wait_ge(ogT_ready, c + 1)
                    need(pe, hnT_ready, h + 1)
                    pe.wait_ge(o_ready, c + 1)
                    for b in range(NB):
                        ins = mm(by4(bank[6])[:, b, :], ogT[:, b, :], Wo_T[:, :], start=True, stop=True)
                    ins.then_inc(wo_ps, 1)

            iterations(pe, body)
            ffn["tensor"](pe)


def make_ffn(nc, ctx, sb, sem, work, A):
    bank, h1buf, ln2, ident, ones = A["bank"], A["h1buf"], A["ln2"], A["ident"], A["ones"]
    gate_sum, by4 = A["gate_sum"], A["by4"]
    W1, b1, W2, b2, out = A["W1"], A["b1"], A["W2"], A["b2"], A["out"]
    tv_W1, tv_b1, tv_W2, tv_b2 = A["tv_W1"], A["tv_b1"], A["tv_W2"], A["tv_b2"]

    at = [0]

    def tile(*shape):
        n = 1
        for k in shape:
            n *= k
        t = work[:, at[0]:at[0] + n]
        at[0] += n
        if len(shape) == 2:
            t = t.rearrange("p (a c) -> p a c", a=shape[0])
        if len(shape) == 3:
            t = t.rearrange("p (a b c) -> p a b c", a=shape[0], b=shape[1])
        return t

    w1T = [tile(FB, D) for _ in range(2)]
    w2T = [tile(FB, D) for _ in range(2)]
    b2mix = tile(NB, D)
    ghT = [tile(GROUP, C) for _ in range(2)]
    hid = [tile(GROUP * C) for _ in range(FB)]
    fhn = [tile(GROUP, D) for _ in range(2)]
    fhnb = [tile(GROUP, D) for _ in range(2)]
    res = tile(GROUP, D)
    nrm = tile(GROUP, D)
    y = [tile(GROUP, D) for _ in range(2)]
    assert at[0] <= A["attention_end"] - 2 * NB * D
    tv1 = sb("tv1", [D, NE, FB, D])
    tv2 = sb("tv2", [D, NE, FB, D])
    w1nat = sb("w1nat", [D, FB, D])
    w2nat = sb("w2nat", [D, FB, D])
    tvb1 = sb("tvb1", [NE, F])
    tvb2 = sb("tvb2", [NE, D])
    tvln = sb("tvln", [NE, 2, D])
    ln_rows = sb("ln_rows", [1, 3, D])
    merge_w = sb("merge_w", [NE, 2, D])
    lng_lnb = sb("lng_lnb", [D, 2, D])
    lng, lnb = lng_lnb[:, 0, :], lng_lnb[:, 1, :]
    b1nat = sb("b1nat", [D, FB])
    b1mix = sb("b1mix", [D, NB, FB])
    gh = sb("gh", [D, NB])
    ghm = sb("ghm", [D, NB])
    gfc2T = sb("gfc2T", [D, NE])
    gfc2b = sb("gfc2b", [D, NE])
    gfc2b_col = sb("gfc2b_col", [NE, 1])
    g_all = sb("g_all", [D, NB, NE])
    g_T = sb("g_T", [NE, NB])
    fst = sb("fst", [D, GROUP, 6])
    fmv = sb("fmv", [D, GROUP, 2])
    fve = sb("fve", [D, GROUP])
    frs = sb("frs", [D, GROUP])
    half_neg = A["half_neg"]

    fw_in = sem("fw_in")
    merge_set = sem("merge_set")
    ln_ps = sem("ln_ps")
    ln_ready = sem("ln_ready")
    gh_sum = sem("gh_sum")
    gh_ready = sem("gh_ready")
    g_ps2 = sem("g_ps2")
    g_ready = sem("g_ready")
    bias_ps = sem("bias_ps")
    mix_step = sem("mix_step")
    b1_ready = sem("b1_ready")
    b2_ready = sem("b2_ready")
    fhn_ready = sem("fhn_ready")
    fhnb_ready = sem("fhnb_ready")
    fhT_ps = sem("fhT_ps")
    fhT_ready = sem("fhT_ready")
    hid_ps = sem("hid_ps")
    hid_ready = sem("hid_ready")
    out_ps = sem("out_ps")
    res_ready = sem("res_ready")
    fst_done = sem("fst_done")
    fmv_ready = sem("fmv_ready")
    fve_ready = sem("fve_ready")
    frs_ready = sem("frs_ready")
    nrm_ready = sem("nrm_ready")
    y1 = sem("y1")
    y2 = sem("y2")
    y_ready = sem("y_ready")
    y_out = [sem("y_out0"), sem("y_out1")]

    def row1(v):
        return v.rearrange("(a n) -> a n", a=1)

    def row(v):
        return v.partition_broadcast(D)

    loads = [
        (tvln[:, 0, :], A["tv_ln_g"][:, :]), (tvln[:, 1, :], A["tv_ln_b"][:, :]),
        (ln_rows[:, 0, :], row1(A["ln_g"])), (ln_rows[:, 1, :], row1(A["ln_b"])), (ln_rows[:, 2, :], row1(b2)),
        (gfc2T[:, :], A["gfc2_wT"][:, :]), (gfc2b[:, :], row(A["gfc2_b"])),
        (gfc2b_col[:, :], A["gfc2_b"].rearrange("(p a) -> p a", a=1)),
        (w1nat[:, :, :].rearrange("p a c -> p (a c)"), W1[:, :]), (w2nat[:, :, :], W2.rearrange("(a p) d -> p a d", p=D)),
        (b1nat[:, :], b1[:, :]), (tvb1[:, :], tv_b1[:, :]), (tvb2[:, :], tv_b2[:, :]),
    ]
    loads += [(tv1[:, e].rearrange("p a c -> p (a c)"), tv_W1[e]) for e in range(NE)]
    loads += [(tv2[:, e], tv_W2[e].rearrange("(a p) d -> p a d", p=D)) for e in range(NE)]
    LOADED = 16 * len(loads)

    def units(engine, body, image_start=None):
        for b in range(NB):
            if image_start is not None:
                image_start(b)
            u0, par = b * UNITS, b % 2
            start = 0
            if b == 0:
                body(0, 0, 0, 0, GROUP, (0, 1, GROUP), (0, 2, GROUP))
                body(0, 1, 1, 1, GROUP, (0, 2, GROUP), (0, 3, GROUP))
                start = 2
            with engine.Fori(start, GROUPS - 3, 2) as g:
                body(b, g, u0 + g, par, GROUP, (b, g + 1, GROUP), (b, g + 2, GROUP))
                body(b, g + 1, u0 + g + 1, 1 - par, GROUP, (b, g + 2, GROUP), (b, g + 3, GROUP))
            later = ((b + 1, 0, GROUP), (b + 1, 1, GROUP)) if b + 1 < NB else (None, None)
            body(b, GROUPS - 2, u0 + GROUPS - 2, par, GROUP, (b, GROUPS - 1, GROUP), (b, GROUPS, 1))
            body(b, GROUPS - 1, u0 + GROUPS - 1, 1 - par, GROUP, (b, GROUPS, 1), later[0])
            body(b, GROUPS, u0 + GROUPS, par, 1, later[0], later[1])

    def load(sp):
        for dst, src in loads:
            sp.dma_start(dst, src).then_inc(fw_in, 16)

    def sync(sp):
        def body(b, g, u, par, n, nxt, nxt2):
            sp.wait_ge(y_ready, u + 1)
            if n == GROUP:
                dst = out[b, bass.ds(g * (GROUP * C), GROUP * C), :].rearrange("(t p) d -> p t d", p=C)
                sp.dma_start(dst, y[par][:, :, :]).then_inc(y_out[par], 16)
            else:
                sp.dma_start(out[b, (STEPS - 1) * C:TOK, :], y[par][0:LAST, 0, :]).then_inc(y_out[par], 16)
        units(sp, body)
        sp.wait_ge(y_out[0], 16 * (NB * UNITS // 2))
        sp.wait_ge(y_out[1], 16 * (NB * UNITS // 2))

    def vector_early(dve):
        nc.vector.memset(merge_w[:, 0, :], LN_MERGE)
        nc.vector.memset(merge_w[0:1, 1, :], 1.0 - NE * LN_MERGE).then_inc(merge_set, 1)

    def tensor_early(pe):
        pe.wait_ge(merge_set, 1)
        pe.wait_ge(fw_in, LOADED)
        for i in range(2):
            t = bank[4][:, i * D:(i + 1) * D]
            nc.tensor.matmul(t, merge_w[:, 0, :], tvln[:, i, :], start=True, stop=False)
            ins = nc.tensor.matmul(t, merge_w[0:1, 1, :], ln_rows[:, i, :], start=False, stop=True)
        ins.then_inc(ln_ps, 1)

    def mix(dve, b, e, place, which=(0, 1)):
        if isinstance(place, int) and place == 0 and b >= 2:
            dve.wait_ge(out_ps, UNITS * (b - 1))
        ex = bass.ds(e, 1)
        for i in which:
            if not isinstance(place, int) or place > 0:
                step = 2 * NE * b + 2 * place if len(which) == 2 else NE * i + place
                dve.wait_ge(mix_step, step)
            t, tv, nat = ((w1T[b % 2], tv1, w1nat), (w2T[b % 2], tv2, w2nat))[i]
            nc.vector.scalar_tensor_tensor(t.rearrange("p a c -> p (a c)"), tv[:, ex, :, :].rearrange("p e a c -> p (e a c)"),
                                           g_all[:, b, ex], (nat[:, :, :] if isinstance(place, int) and place == 0 else t).rearrange("p a c -> p (a c)"),
                                           ALU.mult, ALU.add).then_inc(mix_step, 1)

    def vector(dve):
        def normed(b, g, u, par, n):
            need(dve, fhT_ps, u - 1)
            need(dve, fhnb_ready, u - 1)
            for t in range(n):
                s = g * GROUP + t
                st = ln2[:, bass.ds(s, 1), b, :].rearrange("p s m -> p (s m)")
                ins = nc.vector.tensor_scalar(fhn[par][:, t, :], h1buf[:, b, bass.ds(s, 1), :].rearrange("p s c -> p (s c)"),
                                              st[:, 0:1], st[:, 1:2], ALU.subtract, ALU.mult)
            ins.then_inc(fhn_ready, 1)

        dve.wait_ge(A["gate_summed"], STEPS)
        nc.vector.tensor_reduce(gh[:, :], gate_sum, AX.X, ALU.add).then_inc(gh_sum, 1)
        dve.wait_ge(gh_sum, 1)
        nc.vector.tensor_scalar(ghm[:, :], gh[:, :], 1.0 / TOK, None, ALU.mult).then_inc(gh_ready, 1)
        dve.wait_ge(A["og_ready"], NB * STEPS)
        dve.wait_ge(A["ln2_kept"], STEPS)
        normed(0, 0, 0, 0, GROUP)
        normed(0, 1, 1, 1, GROUP)
        dve.wait_ge(g_ps2, 1)
        dve.wait_ge(fw_in, LOADED)
        nc.vector.tensor_tensor(g_all[:, :, :], bank[0][:, 0:NB * NE].rearrange("p (b e) -> p b e", b=NB),
                                gfc2b[:, :].unsqueeze(1).broadcast_to([D, NB, NE]), ALU.add)
        nc.vector.tensor_scalar(g_T[:, :], bank[0][0:NE, 64:64 + NB], gfc2b_col[:, :], None, ALU.add).then_inc(g_ready, 1)
        dve.wait_ge(g_ready, 1)
        for e in range(NE):
            mix(dve, 0, e, e, which=(0,))
        dve.wait_ge(bias_ps, 1)
        nc.vector.tensor_tensor(b1mix[:, :, :], bank[6][:, 0:NB * FB].rearrange("p (f b) -> p b f", b=NB),
                                b1nat[:, :].unsqueeze(1).broadcast_to([D, NB, FB]), ALU.add).then_inc(b1_ready, 1)
        nc.vector.tensor_copy(b2mix, by4(bank[7])).then_inc(b2_ready, 1)
        for e in range(NE):
            mix(dve, 0, e, e, which=(1,))

        def image_start(b):
            if b + 1 < NB:
                mix(dve, b + 1, NE - 1, 0)
                mix(dve, b + 1, NE - 2, 1)

        def body(b, g, u, par, n, nxt, nxt2):
            if b + 1 < NB and not (isinstance(g, int) and g == GROUPS):
                mix(dve, b + 1, g, g + 2)
            ahead = nxt2 is not None and isinstance(g, int) and g == GROUPS - 1
            if ahead:
                normed(nxt2[0], nxt2[1], u + 2, par, nxt2[2])
            dve.wait_ge(out_ps, u + 1)
            dve.wait_ge(fhnb_ready, u + 1)
            need(dve, nrm_ready, u)
            nc.vector.tensor_tensor(res[:, 0:n, :], by4(bank[2])[:, 0:n, :], fhnb[par][:, 0:n, :], ALU.add).then_inc(res_ready, 1)
            dve.wait_ge(res_ready, u + 1)
            for t in range(n):
                ins = nc.vector.bn_stats(fst[:, t, :], res[:, t, :])
            ins.then_inc(fst_done, 1)
            dve.wait_ge(fst_done, u + 1)
            apart(dve)
            for t in range(n):
                ins = nc.vector.bn_aggr(fmv[:, t, :], fst[:, t, :])
            ins.then_inc(fmv_ready, 1)
            if nxt2 is not None and not ahead:
                normed(nxt2[0], nxt2[1], u + 2, par, nxt2[2])
            dve.wait_ge(frs_ready, u + 1)
            need(dve, y1, u)
            for t in range(n):
                ins = nc.vector.tensor_scalar(nrm[:, t, :], res[:, t, :], fmv[:, t, 0:1], frs[:, t:t + 1], ALU.subtract, ALU.mult)
            ins.then_inc(nrm_ready, 1)

        units(dve, body, image_start)

    def scalar(act):
        act.wait_ge(ln_ps, 1)
        nc.scalar.copy(lng_lnb[:, :, :], bank[4][:, 0:2 * D].rearrange("p (a c) -> p a c", a=2)).then_inc(ln_ready, 1)
        act.wait_ge(A["gate_summed"], STEPS)
        act.wait_ge(A["wo_ps"], STEPS)

        def cols_out(u, par, n):
            act.wait_ge(fhT_ps, u + 1)
            need(act, hid_ps, FB * (u - 1))
            nc.scalar.copy(ghT[par][:, 0:n, :], by4(bank[3])[:, 0:n, :]).then_inc(fhT_ready, 1)

        cols_out(0, 0, GROUP)
        act.wait_ge(b1_ready, 1)

        def body(b, g, u, par, n, nxt, nxt2):
            for f in range(FB):
                act.wait_ge(hid_ps, FB * u + f + 1)
                if f == 0:
                    need(act, out_ps, u)
                nc.scalar.activation(hid[f][:, 0:n * C], bank[(0, 1, 4, 5)[f]][:, 0:n * C], ACT.Relu, bias=b1mix[:, b, f:f + 1]).then_inc(hid_ready, 1)
            if nxt is not None:
                cols_out(u + 1, 1 - par, nxt[2])

        units(act, body)

    def gpsimd(pool):
        def biased(b, u, par, n):
            pool.wait_ge(fhn_ready, u + 1)
            need(pool, res_ready, u - 1)
            nc.gpsimd.tensor_tensor(fhnb[par][:, 0:n, :], fhn[par][:, 0:n, :], b2mix[:, b, :].unsqueeze(1).broadcast_to([D, n, D]), ALU.add).then_inc(fhnb_ready, 1)

        pool.wait_ge(b2_ready, 1)
        pool.wait_ge(ln_ready, 1)
        biased(0, 0, 0, GROUP)

        def body(b, g, u, par, n, nxt, nxt2):
            pool.wait_ge(fmv_ready, u + 1)
            apart(pool)
            nc.gpsimd.tensor_scalar(fve[:, 0:n], fmv[:, 0:n, 1], EPS, None, ALU.add).then_inc(fve_ready, 1)
            pool.wait_ge(fve_ready, u + 1)
            need(pool, nrm_ready, u)
            nc.gpsimd.tensor_tensor(frs[:, 0:n], fve[:, 0:n], half_neg[:, 0:n], ALU.pow).then_inc(frs_ready, 1)
            if nxt is not None:
                biased(nxt[0], u + 1, 1 - par, nxt[2])
            pool.wait_ge(nrm_ready, u + 1)
            need(pool, y_out[par], (u - par) * 8)
            nc.gpsimd.tensor_tensor(y[par][:, 0:n, :], nrm[:, 0:n, :], lng.unsqueeze(1).broadcast_to([D, n, D]), ALU.mult).then_inc(y1, 1)
            pool.wait_ge(y1, u + 1)
            nc.gpsimd.tensor_tensor(y[par][:, 0:n, :], y[par][:, 0:n, :], lnb.unsqueeze(1).broadcast_to([D, n, D]), ALU.add).then_inc(y2, 1)
            pool.wait_ge(y2, u + 1)
            apart(pool)
            nc.gpsimd.tensor_tensor(y[par][:, 0:n, :], y[par][:, 0:n, :], h1buf[:, b, bass.ds(g * GROUP, n), :], ALU.add).then_inc(y_ready, 1)

        units(pool, body)

    def tensor(pe):
        mm, tr = nc.tensor.matmul, nc.tensor.transpose

        def to_cols(u, par, n):
            pe.wait_ge(fhn_ready, u + 1)
            need(pe, fhT_ready, u)
            for t in range(n):
                ins = tr(by4(bank[3])[:, t, :], fhn[par][:, t, :], ident[:, :])
            ins.then_inc(fhT_ps, 1)

        tensor_early(pe)
        pe.wait_ge(gh_ready, 1)
        for b in range(NB):
            mm(bank[0][:, b * NE:(b + 1) * NE], ghm[:, b:b + 1].broadcast_to([D, D]), gfc2T[:, :], start=True, stop=True)
        mm(bank[0][0:NE, 64:64 + NB], gfc2T[:, :], ghm[:, :], start=True, stop=True).then_inc(g_ps2, 1)
        to_cols(0, 0, GROUP)
        pe.wait_ge(g_ready, 1)
        for f in range(FB):
            mm(bank[6][:, f * NB:(f + 1) * NB], tvb1[:, f * D:(f + 1) * D], g_T[:, :], start=True, stop=True)
        for b in range(NB):
            mm(by4(bank[7])[:, b, :], g_T[:, b:b + 1].broadcast_to([NE, D]), tvb2[:, :], start=True, stop=False)
            ins = mm(by4(bank[7])[:, b, :], ones[0:1, :], ln_rows[:, 2, :], start=False, stop=True)
        ins.then_inc(bias_ps, 1)

        pe.wait_ge(ln_ready, 1)

        def body(b, g, u, par, n, nxt, nxt2):
            pe.wait_ge(fhT_ready, u + 1)
            w1, w2 = w1T[b % 2], w2T[b % 2]

            def hidden(f):
                need(pe, hid_ready, FB * (u - 1) + f + 1)
                mm(bank[(0, 1, 4, 5)[f]][:, 0:n * C], w1[:, f, :], ghT[par][:, 0:n, :].rearrange("p t c -> p (t c)"), start=True, stop=True).then_inc(hid_ps, 1)

            def project(f):
                pe.wait_ge(hid_ready, FB * u + f + 1)
                if f == 0:
                    need(pe, res_ready, u)
                for t in range(n):
                    ins = mm(by4(bank[2])[:, t, :], hid[f][:, t * C:(t + 1) * C], w2[:, f, :], start=(f == 0 and t == 0),
                             stop=(f == FB - 1), skip_group_check=True)
                if f == FB - 1:
                    ins.then_inc(out_ps, 1)

            for f in range(FB):
                hidden(f)
            if isinstance(u, int) and u == 0:
                pe.wait_ge(mix_step, 2 * NE)
            project(0)
            project(1)
            if nxt is not None:
                to_cols(u + 1, 1 - par, nxt[2])
            project(2)
            project(3)

        units(pe, body, lambda b: pe.wait_ge(mix_step, 2 * NE * (b + 1) if b else NE))

    return {"sync": sync, "vector": vector, "scalar": scalar, "gpsimd": gpsimd, "tensor": tensor,
            "load": load, "vector_early": vector_early}


_INS = ['x'] + ['L0_tok_' + n for n in ('W', 'b', 'cls')] + ['projections', 'biases', 'taps'] + [
    'L0_attn_' + n for n in ('norm_w', 'Wo', 'bo')] + ['L0_ffn_' + n for n in (
        'gfc1_w', 'gfc1_b', 'gfc2_w', 'gfc2_b', 'W1', 'b1', 'W2', 'b2', 'ln_g', 'ln_b', 'tv_W1', 'tv_b1', 'tv_W2',
        'tv_b2', 'tv_ln_g', 'tv_ln_b')]
_TRANSPOSED = ['L0_tok_W', 'L0_attn_Wo'] + [
    'L0_ffn_gfc1_w', 'L0_ffn_gfc2_w', 'L0_ffn_W1', 'L0_ffn_W2']


def patch_vectors(_np, pixels):
    x = _np.zeros((KX, NB, STEPS * C), pixels.dtype)
    x[0:PIX, :, 1:TOK] = pixels
    x[PIX, :, 1:TOK] = 1
    x[PIX + 1, :, 0:TOK] = 1
    x[PIX + 2, :, 0] = 1
    return x


def kernel(**inputs):
    import numpy as _np
    import concourse.bacc as _bacc
    from concourse import mybir as _mybir
    from concourse.bass_utils import run_bass_kernel_spmd as _run

    nc = _bacc.Bacc("TRN2", target_bir_lowering=False, num_devices=1)
    arrays, args = {}, []

    def attention(*names):
        return [_np.asarray(inputs['L0_attn_' + n]) for n in names]

    inputs = dict(inputs)
    inputs['projections'] = _np.concatenate([w.T for w in attention('Wk', 'Wv', 'Wg', 'Wq', 'Wa', 'Wb')], axis=1)
    inputs['biases'] = _np.concatenate(attention('bk', 'bv', 'bg', 'bq', 'ba', 'bb', 'cbk', 'cbv', 'cbq'))
    inputs['taps'] = _np.concatenate([w.reshape(D, TAPS).T for w in attention('cwk', 'cwv', 'cwq')], axis=1)
    for name in _INS:
        a = _np.asarray(inputs[name])
        if name == 'x':
            a = a.reshape(NB, 3, GRID, PATCH, GRID, PATCH).transpose(1, 3, 5, 0, 2, 4).reshape(PIX, NB, GRID * GRID)
            a = patch_vectors(_np, a)
        elif name in _TRANSPOSED:
            a = a.T
        elif name in ('L0_ffn_tv_W1', 'L0_ffn_tv_W2'):
            a = a.transpose(0, 2, 1)
        elif name == 'L0_ffn_b1':
            a = a.reshape(FB, D).T
        a = _np.ascontiguousarray(a)
        arrays[f"in_{name}_dram"] = a
        args.append(nc.dram_tensor(f"in_{name}_dram", a.shape, _mybir.dt.from_np(a.dtype), kind="ExternalInput").ap())
    args.append(nc.dram_tensor("out_0_dram", (NB, TOK, D), _mybir.dt.float32, kind="ExternalOutput").ap())
    vit_tower(nc, *args)
    r = _run(nc, [arrays], core_ids=[0])
    return r.results[0]["out_0_dram"]
```
